# Optimizing a Trainium2 kernel written in Bass

```python
import numpy as np
import jax
import jax.numpy as jnp

def _softmax(x, axis=-1):
    return jax.nn.softmax(x, axis=axis)

def _gelu(x):
    return jax.nn.gelu(x, approximate=True)

def _silu(x):
    return jax.nn.silu(x)

def _sigmoid(x):
    return jax.nn.sigmoid(x)

def _layernorm(x, axis=-1, eps=1e-05):
    m = jnp.mean(x, axis=axis, keepdims=True)
    v = jnp.var(x, axis=axis, keepdims=True)
    return (x - m) / jnp.sqrt(v + eps)

def _scatter_add(tgt, idx, src, axis=0):
    return tgt.at[idx].add(src)

def _segment_sum(src, seg, n):
    return jax.ops.segment_sum(src, seg, n)
kernel_name = 'mk_seq_postln_d2_jaxref_r8_f0d519'

def setup_inputs(seed: int=0):
    np.random.seed(seed)
    _w = jnp.asarray

    def _L0_attn_setup():
        import jax, jax.numpy as jnp
        import numpy as np
        DIM = 128
        MULT = 4
        D_STATE = 128
        D_CONV = 4
        EXPAND = 2
        D_INNER = EXPAND * DIM
        HEADDIM = 64
        NHEADS = D_INNER // HEADDIM
        CONV_DIM = D_INNER + 2 * D_STATE
        D_IN_PROJ = 2 * D_INNER + 2 * D_STATE + NHEADS
        HIDDEN = DIM * MULT
        B, L = (2, 256)

        def _rmsnorm(x):
            eps = jnp.finfo(x.dtype).eps
            return x * jax.lax.rsqrt(jnp.mean(x * x, axis=-1, keepdims=True) + eps)

        def _mamba2(u, in_proj_w, conv_w, conv_b, dt_bias, A_log, D, norm_w, out_proj_w):
            b, l, _ = u.shape
            zxbcdt = u @ in_proj_w.T
            z = zxbcdt[..., :D_INNER]
            xBC = zxbcdt[..., D_INNER:D_INNER + CONV_DIM]
            dt = jax.nn.softplus(zxbcdt[..., -NHEADS:] + dt_bias)
            xc = jnp.transpose(xBC, (0, 2, 1))
            xc = jax.lax.conv_general_dilated(xc, conv_w[:, None, :], (1,), [(D_CONV - 1, 0)], feature_group_count=CONV_DIM)
            xBC = jax.nn.silu(jnp.transpose(xc + conv_b[None, :, None], (0, 2, 1)))
            xs = xBC[..., :D_INNER].reshape(b, l, NHEADS, HEADDIM)
            Bm = xBC[..., D_INNER:D_INNER + D_STATE]
            Cm = xBC[..., D_INNER + D_STATE:]
            A = -jnp.exp(A_log)
            dA = jnp.exp(dt * A)

            def step(h, inp):
                dA_t, dt_t, x_t, B_t, C_t = inp
                dBx = dt_t[..., None, None] * x_t[..., None] * B_t[:, None, None, :]
                h = dA_t[:, :, None, None] * h + dBx
                y = jnp.einsum('bhpn,bn->bhp', h, C_t)
                return (h, y)
            h0 = jnp.zeros((b, NHEADS, HEADDIM, D_STATE), u.dtype)
            xsT = jnp.transpose(xs, (1, 0, 2, 3))
            _, ys = jax.lax.scan(step, h0, (jnp.transpose(dA, (1, 0, 2)), jnp.transpose(dt, (1, 0, 2)), xsT, jnp.transpose(Bm, (1, 0, 2)), jnp.transpose(Cm, (1, 0, 2))))
            y = jnp.transpose(ys, (1, 0, 2, 3)) + D[None, None, :, None] * xs
            y = y.reshape(b, l, D_INNER)
            y = y * jax.nn.silu(z)
            y = y * jax.lax.rsqrt(jnp.mean(y * y, axis=-1, keepdims=True) + 1e-05) * norm_w
            return y @ out_proj_w.T
        key = jax.random.key(seed)
        ks = jax.random.split(key, 12)
        w = lambda k, *sh: jax.random.normal(k, sh, jnp.float32) * 0.02
        x = jax.random.normal(ks[0], (B, L, DIM), jnp.float32)
        in_proj_w = w(ks[1], D_IN_PROJ, DIM)
        conv_w = w(ks[2], CONV_DIM, D_CONV)
        conv_b = jnp.zeros((CONV_DIM,), jnp.float32)
        dt = jax.random.uniform(ks[3], (NHEADS,), jnp.float32, 0.001, 0.1)
        dt_bias = jnp.log(jnp.expm1(dt))
        A_log = jnp.log(jax.random.uniform(ks[4], (NHEADS,), jnp.float32, 1.0, 16.0))
        D = jnp.ones((NHEADS,), jnp.float32)
        norm_w = jnp.ones((D_INNER,), jnp.float32)
        out_proj_w = w(ks[5], DIM, D_INNER)
        gate_w = w(ks[6], HIDDEN, DIM)
        up_w = w(ks[7], HIDDEN, DIM)
        down_w = w(ks[8], DIM, HIDDEN)
        mixer_scale = jnp.ones((DIM,), jnp.float32)
        mlp_scale = jnp.ones((DIM,), jnp.float32)
        return dict(x=x, in_proj_w=in_proj_w, conv_w=conv_w, conv_b=conv_b, dt_bias=dt_bias, A_log=A_log, D=D, norm_w=norm_w, out_proj_w=out_proj_w, gate_w=gate_w, up_w=up_w, down_w=down_w, mixer_scale=mixer_scale, mlp_scale=mlp_scale)
    _L0_attn_in = _L0_attn_setup()

    def _L0_ffn_setup():
        import jax, jax.numpy as jnp
        import numpy as np
        K = 2
        TEMP = 1.0
        key = jax.random.key(seed)
        ks = jax.random.split(key, 5)
        B, S, D, O, E = (4, 256, 128, 128, 8)
        scale = 1.0 / np.sqrt(D)
        x = jax.random.normal(ks[0], (B, S, D), dtype=jnp.float32)
        W = jax.random.normal(ks[1], (E, O, D), dtype=jnp.float32) * scale
        b = jax.random.normal(ks[2], (E, O), dtype=jnp.float32) * 0.01
        Wg = jax.random.normal(ks[3], (E, D), dtype=jnp.float32) * scale
        bg = jnp.zeros((E,), dtype=jnp.float32)
        return {'x': x, 'W': W, 'b': b, 'Wg': Wg, 'bg': bg}
    _L0_ffn_in = _L0_ffn_setup()

    def _L1_attn_setup():
        import math
        import jax, jax.numpy as jnp
        import numpy as np
        LN_EPS = 1e-05

        def _relative_sinusoidal(t, hd, dtype):
            pos = jnp.arange(-(t - 1), t, dtype=dtype)[:, None]
            div = jnp.exp(jnp.arange(0, hd, 2, dtype=dtype) * (-math.log(10000.0) / hd))
            pe = jnp.zeros((2 * t - 1, hd), dtype=dtype)
            pe = pe.at[:, 0::2].set(jnp.sin(pos * div))
            pe = pe.at[:, 1::2].set(jnp.cos(pos * div))
            return pe
        key = jax.random.key(seed)
        ks = jax.random.split(key, 4)
        b, t, dim, H = (2, 256, 128, 16)
        hd = dim // H
        s = 0.02
        return {'x': jax.random.normal(ks[0], (b, t, dim), jnp.float32), 'ln_g': jnp.ones((dim,), jnp.float32), 'ln_b': jnp.zeros((dim,), jnp.float32), 'w_qkv': jax.random.normal(ks[1], (dim, 3 * dim), jnp.float32) * s, 'b_qkv': jnp.zeros((3 * dim,), jnp.float32), 'w_rel': jax.random.normal(ks[2], (hd, H), jnp.float32) * s, 'w_out': jax.random.normal(ks[3], (dim, dim), jnp.float32) * s, 'b_out': jnp.zeros((dim,), jnp.float32)}
    _L1_attn_in = _L1_attn_setup()

    def _L1_ffn_setup():
        import jax, jax.numpy as jnp
        import numpy as np
        N_EMBD = 128
        N_EXP = 8
        TOP_K = 2
        CAPACITY = 512
        D_FF = 3 * N_EMBD
        key = jax.random.key(seed)
        k1, k2, k3, k4 = jax.random.split(key, 4)
        x = jax.random.normal(k1, (8, 256, N_EMBD), dtype=jnp.float32)
        w_gate = jax.random.normal(k2, (N_EMBD, N_EXP), dtype=jnp.float32) * 0.02
        c_fc = jax.random.normal(k3, (N_EXP, N_EMBD, D_FF), dtype=jnp.float32) * 0.02
        c_proj = jax.random.normal(k4, (N_EXP, D_FF // 2, N_EMBD), dtype=jnp.float32) * 0.02
        return {'x': x, 'w_gate': w_gate, 'c_fc': c_fc, 'c_proj': c_proj}
    _L1_ffn_in = _L1_ffn_setup()
    _d = {'L0_attn_x': _L0_attn_in['x'], 'L0_attn_in_proj_w': _L0_attn_in['in_proj_w'], 'L0_attn_conv_w': _L0_attn_in['conv_w'], 'L0_attn_conv_b': _L0_attn_in['conv_b'], 'L0_attn_dt_bias': _L0_attn_in['dt_bias'], 'L0_attn_A_log': _L0_attn_in['A_log'], 'L0_attn_D': _L0_attn_in['D'], 'L0_attn_norm_w': _L0_attn_in['norm_w'], 'L0_attn_out_proj_w': _L0_attn_in['out_proj_w'], 'L0_attn_gate_w': _L0_attn_in['gate_w'], 'L0_attn_up_w': _L0_attn_in['up_w'], 'L0_attn_down_w': _L0_attn_in['down_w'], 'L0_attn_mixer_scale': _L0_attn_in['mixer_scale'], 'L0_attn_mlp_scale': _L0_attn_in['mlp_scale'], 'L0_ffn_W': _L0_ffn_in['W'], 'L0_ffn_b': _L0_ffn_in['b'], 'L0_ffn_Wg': _L0_ffn_in['Wg'], 'L0_ffn_bg': _L0_ffn_in['bg'], 'L1_attn_ln_g': _L1_attn_in['ln_g'], 'L1_attn_ln_b': _L1_attn_in['ln_b'], 'L1_attn_w_qkv': _L1_attn_in['w_qkv'], 'L1_attn_b_qkv': _L1_attn_in['b_qkv'], 'L1_attn_w_rel': _L1_attn_in['w_rel'], 'L1_attn_w_out': _L1_attn_in['w_out'], 'L1_attn_b_out': _L1_attn_in['b_out'], 'L1_ffn_w_gate': _L1_ffn_in['w_gate'], 'L1_ffn_c_fc': _L1_ffn_in['c_fc'], 'L1_ffn_c_proj': _L1_ffn_in['c_proj']}
    _x0 = _d['L0_attn_x']
    _d['L0_attn_x'] = jax.random.normal(jax.random.fold_in(jax.random.key(seed), 1), (4, 1024, 128), dtype=_x0.dtype)
    del _x0
    return _d

def reference(L0_attn_x, L0_attn_in_proj_w, L0_attn_conv_w, L0_attn_conv_b, L0_attn_dt_bias, L0_attn_A_log, L0_attn_D, L0_attn_norm_w, L0_attn_out_proj_w, L0_attn_gate_w, L0_attn_up_w, L0_attn_down_w, L0_attn_mixer_scale, L0_attn_mlp_scale, L0_ffn_W, L0_ffn_b, L0_ffn_Wg, L0_ffn_bg, L1_attn_ln_g, L1_attn_ln_b, L1_attn_w_qkv, L1_attn_b_qkv, L1_attn_w_rel, L1_attn_w_out, L1_attn_b_out, L1_ffn_w_gate, L1_ffn_c_fc, L1_ffn_c_proj):

    def _L0_attn_ref(x, in_proj_w, conv_w, conv_b, dt_bias, A_log, D, norm_w, out_proj_w, gate_w, up_w, down_w, mixer_scale, mlp_scale):
        import jax, jax.numpy as jnp
        import numpy as np
        DIM = 128
        MULT = 4
        D_STATE = 128
        D_CONV = 4
        EXPAND = 2
        D_INNER = EXPAND * DIM
        HEADDIM = 64
        NHEADS = D_INNER // HEADDIM
        CONV_DIM = D_INNER + 2 * D_STATE
        D_IN_PROJ = 2 * D_INNER + 2 * D_STATE + NHEADS
        HIDDEN = DIM * MULT
        B, L = (2, 256)

        def _rmsnorm(x):
            eps = jnp.finfo(x.dtype).eps
            return x * jax.lax.rsqrt(jnp.mean(x * x, axis=-1, keepdims=True) + eps)

        def _mamba2(u, in_proj_w, conv_w, conv_b, dt_bias, A_log, D, norm_w, out_proj_w):
            b, l, _ = u.shape
            zxbcdt = u @ in_proj_w.T
            z = zxbcdt[..., :D_INNER]
            xBC = zxbcdt[..., D_INNER:D_INNER + CONV_DIM]
            dt = jax.nn.softplus(zxbcdt[..., -NHEADS:] + dt_bias)
            xc = jnp.transpose(xBC, (0, 2, 1))
            xc = jax.lax.conv_general_dilated(xc, conv_w[:, None, :], (1,), [(D_CONV - 1, 0)], feature_group_count=CONV_DIM)
            xBC = jax.nn.silu(jnp.transpose(xc + conv_b[None, :, None], (0, 2, 1)))
            xs = xBC[..., :D_INNER].reshape(b, l, NHEADS, HEADDIM)
            Bm = xBC[..., D_INNER:D_INNER + D_STATE]
            Cm = xBC[..., D_INNER + D_STATE:]
            A = -jnp.exp(A_log)
            dA = jnp.exp(dt * A)

            def step(h, inp):
                dA_t, dt_t, x_t, B_t, C_t = inp
                dBx = dt_t[..., None, None] * x_t[..., None] * B_t[:, None, None, :]
                h = dA_t[:, :, None, None] * h + dBx
                y = jnp.einsum('bhpn,bn->bhp', h, C_t)
                return (h, y)
            h0 = jnp.zeros((b, NHEADS, HEADDIM, D_STATE), u.dtype)
            xsT = jnp.transpose(xs, (1, 0, 2, 3))
            _, ys = jax.lax.scan(step, h0, (jnp.transpose(dA, (1, 0, 2)), jnp.transpose(dt, (1, 0, 2)), xsT, jnp.transpose(Bm, (1, 0, 2)), jnp.transpose(Cm, (1, 0, 2))))
            y = jnp.transpose(ys, (1, 0, 2, 3)) + D[None, None, :, None] * xs
            y = y.reshape(b, l, D_INNER)
            y = y * jax.nn.silu(z)
            y = y * jax.lax.rsqrt(jnp.mean(y * y, axis=-1, keepdims=True) + 1e-05) * norm_w
            return y @ out_proj_w.T
        x = x + mixer_scale[None, None, :] * _mamba2(_rmsnorm(x), in_proj_w, conv_w, conv_b, dt_bias, A_log, D, norm_w, out_proj_w)
        h = _rmsnorm(x)
        mlp = jax.nn.silu(h @ gate_w.T) * (h @ up_w.T) @ down_w.T
        return x + mlp_scale[None, None, :] * mlp

    def _L0_ffn_ref(x, W, b, Wg, bg):
        import jax, jax.numpy as jnp
        import numpy as np
        K = 2
        TEMP = 1.0
        gate_logits = (jnp.einsum('bsd,ed->bse', x, Wg) + bg) / TEMP
        gate_scores = jax.nn.softmax(gate_logits, axis=-1)
        topk_scores, topk_idx = jax.lax.top_k(gate_scores, K)
        expert_outputs = jnp.einsum('bsd,eod->bseo', x, W) + b
        selected = jnp.take_along_axis(expert_outputs, topk_idx[..., None], axis=2)
        output = jnp.sum(selected * topk_scores[..., None], axis=2)
        return output

    def _L1_attn_ref(x, ln_g, ln_b, w_qkv, b_qkv, w_rel, w_out, b_out):
        import math
        import jax, jax.numpy as jnp
        import numpy as np
        LN_EPS = 1e-05

        def _relative_sinusoidal(t, hd, dtype):
            pos = jnp.arange(-(t - 1), t, dtype=dtype)[:, None]
            div = jnp.exp(jnp.arange(0, hd, 2, dtype=dtype) * (-math.log(10000.0) / hd))
            pe = jnp.zeros((2 * t - 1, hd), dtype=dtype)
            pe = pe.at[:, 0::2].set(jnp.sin(pos * div))
            pe = pe.at[:, 1::2].set(jnp.cos(pos * div))
            return pe
        b, t, dim = x.shape
        hd, H = w_rel.shape
        scale = hd ** (-0.5)
        mu = jnp.mean(x, axis=-1, keepdims=True)
        var = jnp.mean(jnp.square(x - mu), axis=-1, keepdims=True)
        xn = (x - mu) * jax.lax.rsqrt(var + LN_EPS) * ln_g + ln_b
        qkv = (xn @ w_qkv + b_qkv).reshape(b, t, 3, H, hd)
        qkv = jnp.transpose(qkv, (2, 0, 3, 1, 4))
        q, k, v = (qkv[0], qkv[1], qkv[2])
        scores = jnp.einsum('bhqd,bhkd->bhqk', q, k) * scale
        rel_pe = _relative_sinusoidal(t, hd, scores.dtype)
        rel_bias = rel_pe @ w_rel
        idx = jnp.arange(t)[:, None] - jnp.arange(t)[None, :] + (t - 1)
        bias = jnp.transpose(rel_bias[idx], (2, 0, 1))[None]
        attn = jax.nn.softmax(scores + bias, axis=-1)
        out = jnp.einsum('bhqk,bhkd->bhqd', attn, v)
        out = jnp.transpose(out, (0, 2, 1, 3)).reshape(b, t, dim)
        return out @ w_out + b_out

    def _L1_ffn_ref(x, w_gate, c_fc, c_proj):
        import jax, jax.numpy as jnp
        import numpy as np
        N_EMBD = 128
        N_EXP = 8
        TOP_K = 2
        CAPACITY = 512
        D_FF = 3 * N_EMBD
        B, T, d = x.shape
        N = B * T
        xf = x.reshape(N, d)
        scores = jax.nn.softmax(xf @ w_gate, axis=-1)
        weights, idx = jax.lax.top_k(scores, TOP_K)
        flat_e = idx.reshape(-1)
        tok = jnp.repeat(jnp.arange(N), TOP_K)
        oh = jax.nn.one_hot(flat_e, N_EXP, dtype=jnp.int32)
        pos = (jnp.cumsum(oh, axis=0) * oh).sum(-1) - 1
        valid = pos < CAPACITY
        pos_c = jnp.where(valid, pos, 0)
        vmask = valid.astype(x.dtype)[:, None]
        exp_x = jnp.zeros((N_EXP, CAPACITY, d), x.dtype)
        exp_x = exp_x.at[flat_e, pos_c].add(xf[tok] * vmask)
        h = jnp.einsum('ecd,edf->ecf', exp_x, c_fc)
        a, g = jnp.split(h, 2, axis=-1)
        h = jax.nn.silu(a) * g
        exp_out = jnp.einsum('ecf,efd->ecd', h, c_proj)
        gathered = exp_out[flat_e, pos_c]
        w = weights.reshape(-1)[:, None] * vmask
        out = (gathered * w).reshape(N, TOP_K, d).sum(axis=1)
        return out.reshape(B, T, d)
    x = L0_attn_x
    x = _layernorm(x + _L0_attn_ref(x, L0_attn_in_proj_w, L0_attn_conv_w, L0_attn_conv_b, L0_attn_dt_bias, L0_attn_A_log, L0_attn_D, L0_attn_norm_w, L0_attn_out_proj_w, L0_attn_gate_w, L0_attn_up_w, L0_attn_down_w, L0_attn_mixer_scale, L0_attn_mlp_scale), axis=-1)
    x = _layernorm(x + _L0_ffn_ref(x, L0_ffn_W, L0_ffn_b, L0_ffn_Wg, L0_ffn_bg), axis=-1)
    x = _layernorm(x + _L1_attn_ref(x, L1_attn_ln_g, L1_attn_ln_b, L1_attn_w_qkv, L1_attn_b_qkv, L1_attn_w_rel, L1_attn_w_out, L1_attn_b_out), axis=-1)
    x = _layernorm(x + _L1_ffn_ref(x, L1_ffn_w_gate, L1_ffn_c_fc, L1_ffn_c_proj), axis=-1)
    return x

_drawn_inputs = setup_inputs


def setup_inputs(seed=0):
    import zlib

    import numpy as np

    out = dict(_drawn_inputs(seed))
    spreads = {'L0_attn_conv_b': (0.0, 0.1),
     'L0_attn_D': (1.0, 0.2),
     'L0_attn_norm_w': (1.0, 0.2),
     'L0_attn_mixer_scale': (1.0, 0.2),
     'L0_attn_mlp_scale': (1.0, 0.6),
     'L0_ffn_bg': (0.0, 0.1),
     'L1_attn_ln_g': (1.0, 0.6),
     'L1_attn_ln_b': (0.0, 0.8),
     'L1_attn_b_qkv': (0.0, 0.343),
     'L1_attn_b_out': (0.0, 0.1)}
    factors = {'L0_attn_dt_bias': 8.0,
     'L0_attn_A_log': 8.0,
     'L0_attn_gate_w': 3.204,
     'L0_attn_up_w': 2.982,
     'L0_attn_down_w': 3.306,
     'L0_ffn_b': 8.0,
     'L1_attn_w_qkv': 8.0,
     'L1_attn_w_rel': 8.0,
     'L1_ffn_w_gate': 8.0,
     'L1_ffn_c_fc': 8.0,
     'L1_ffn_c_proj': 8.0}
    for name, (base, spread) in spreads.items():
        noise = np.random.default_rng([zlib.crc32(name.encode()), seed]).standard_normal(out[name].shape)
        drawn = base * np.exp(spread * noise) if base else spread * noise
        out[name] = jnp.asarray(drawn.astype(out[name].dtype))
    for name, factor in factors.items():
        out[name] = (out[name] * factor).astype(out[name].dtype)
    return out
```

```python
from contextlib import ExitStack

import numpy as np

import concourse.bass as bass
from concourse import mybir

F32 = mybir.dt.float32
BF16 = mybir.dt.bfloat16
I32 = mybir.dt.int32
U32 = mybir.dt.uint32
ALU = mybir.AluOpType
ACT = mybir.ActivationFunctionType
AX = mybir.AxisListType

P = 128
D = 128
B = 4
L = 1024
NT = L // P
HALF = L // 2
HT = NT // 2
D_INNER = 256
NSTATE = 128
SSM_HEADS = 4
SSM_DIM = D_INNER // SSM_HEADS
TAPS = 4
CONV_TILES = (D_INNER + 2 * NSTATE) // P
HIDDEN = 512
HID_TILES = HIDDEN // P
E = 8
TOPK = 2
HEADS = 16
HD = D // HEADS
QUAD = 4
NQUADS = HEADS // QUAD
CAPACITY = 512
CAP_TILES = CAPACITY // P
D_GATE = 192
FFH = D_GATE // 2
PARTS = ((0, 0), (0, 1), (1, 0), (1, 1), (0, 2), (2, 0))
SCORE_ROWS = len(PARTS) * 2 * HD
SHIFT_PARTS = 2
VCOLS = 32
RMS_EPS = float(np.finfo(np.float32).eps)
LN_EPS = 1e-5
FAR = float(1 << 20)
ROW = D + 1
ATANH = [1.0 / (2 * i + 1) for i in range(9)]


def position_tables():
    div = np.exp(np.arange(0, HD, 2, dtype=np.float32) * np.float32(-np.log(10000.0) / HD)).astype(np.float64)
    angle = div[:, None] * np.arange(L)[None, :]
    query = np.zeros((HD, L))
    query[0::2], query[1::2] = np.sin(angle), np.cos(angle)
    key_direct, key_swapped = np.zeros((HD, L)), np.zeros((HD, L))
    key_direct[0::2] = key_direct[1::2] = np.cos(angle)
    key_swapped[0::2], key_swapped[1::2] = np.sin(angle), -np.sin(angle)
    rows = np.tile(np.stack([key_direct, key_swapped]), (1, HEADS, 1)).astype(np.float32)
    return query.astype(np.float32), rows


def build(nc, t):
    with ExitStack() as ctx:
        def sb(name, shape, dt=F32):
            return ctx.enter_context(nc.sbuf_tensor(name, shape, dt))

        def dram(name, shape, dt=F32):
            return nc.dram_tensor(name, shape, dt, kind="Internal").ap()

        ecum_rows = dram("ecum_rows", [NT * SSM_HEADS, P])
        q_parts = dram("q_parts", [3, P, L], BF16)
        k_parts = dram("k_parts", [3, P, L], BF16)
        shift_rows = dram("shift_rows", [SHIFT_PARTS * 16, P], BF16)
        expert_in = dram("expert_in", [E * CAPACITY, ROW])
        expert_out = dram("expert_out", [TOPK * B * L, D])

        ident = sb("ident", [P, P])
        ident16 = sb("ident16", [P, P], BF16)
        ones = sb("ones", [P, P])
        ones16 = sb("ones16", [P, P], BF16)
        upto = sb("upto", [P, P])
        after = sb("after", [P, P])
        before16 = sb("before16", [P, P], BF16)
        iota_e = sb("iota_e", [P, E])
        neg_half = sb("neg_half", [P, NT])
        w_in = sb("w_in", [P, 2 * D_INNER + 2 * NSTATE + SSM_HEADS])
        w_dt = sb("w_dt", [P, P])
        conv_w = sb("conv_w", [P, CONV_TILES, TAPS])
        conv_b = sb("conv_b", [P, CONV_TILES])
        dt_bias = sb("dt_bias", [P, SSM_HEADS])
        a_neg = sb("a_neg", [P, SSM_HEADS])
        d_col = sb("d_col", [P, 2])
        norm_w = sb("norm_w", [P, 2])
        w_out = sb("w_out", [P, 2, D])
        mixer_row = sb("mixer_row", [P, D])
        w_gate = sb("w_gate", [P, HIDDEN])
        w_up = sb("w_up", [P, HIDDEN])
        w_down = sb("w_down", [P, HID_TILES, D])
        mlp_row = sb("mlp_row", [P, D])
        w_exp = sb("w_exp", [P, E, D])
        b_exp = sb("b_exp", [E, D])
        w_route0 = sb("w_route0", [P, P])
        b_route0 = sb("b_route0", [P, E])
        w_route1 = sb("w_route1", [P, P])
        ln_g = sb("ln_g", [P, 1])
        ln_b = sb("ln_b", [P, 1])
        w_qkv = sb("w_qkv", [P, 3 * D])
        b_q = sb("b_q", [P, 1])
        b_k = sb("b_k", [P, 1])
        b_v = sb("b_v", [P, D])
        w_proj = sb("w_proj", [P, D])
        b_proj = sb("b_proj", [P, D])
        rel_own = sb("rel_own", [P, 1])
        rel_other = sb("rel_other", [P, 1])

        AQ = sb("AQ", [SCORE_ROWS + SHIFT_PARTS, HEADS, L], BF16)
        BK = sb("BK", [SCORE_ROWS + SHIFT_PARTS, HEADS, L], BF16)
        x3_all = sb("x3_all", [P, B * NT, D])
        wgt_all = sb("wgt_all", [P, B * NT, TOPK])
        fill = sb("fill", [P, E])

        xa = sb("xa", [P, NT, D])
        xb = sb("xb", [P, NT, D])
        xn = sb("xn", [P, NT, D])
        xnT = sb("xnT", [P, L])
        st = sb("st", [P, NT, 6])
        mv = sb("mv", [P, NT, 2])
        ss = sb("ss", [P, NT])
        var = sb("var", [P, NT])
        rstd = sb("rstd", [P, NT])
        arena = sb("arena", [P, 15800])
        raw = arena[:, 0:CONV_TILES * (L + TAPS - 1)].rearrange("p (f n) -> p f n", f=CONV_TILES)
        xbc = arena[:, 4108:8204].rearrange("p (f n) -> p f n", f=CONV_TILES)
        zg = arena[:, 8204:10252].rearrange("p (j n) -> p j n", j=2)
        ecumB = arena[:, 10252:14348].rearrange("p (c h n) -> p c h n", c=NT, h=SSM_HEADS)
        y1 = arena[:, 14348:15372].rearrange("p (j n) -> p j n", j=2)
        Lx = arena[:, 0:1024].rearrange("p (s h n) -> p s h n", s=2, h=SSM_HEADS)
        Wm = arena[:, 1024:2048].rearrange("p (s h n) -> p s h n", s=2, h=SSM_HEADS)
        Cs = arena[:, 2048:3072].rearrange("p (s h n) -> p s h n", s=2, h=SSM_HEADS)
        xdt = arena[:, 3072:3584].rearrange("p (s h n) -> p s h n", s=2, h=SSM_HEADS)
        xw = arena[:, 3584:4096].rearrange("p (s h n) -> p s h n", s=2, h=SSM_HEADS)
        gT = arena[0:E, 1024:2048]
        xrow = arena[:, 0:NT * TOPK * ROW].rearrange("p (t k d) -> p t k d", t=NT, k=TOPK)
        o_tok = xn
        hidT = arena[:, 0:4096].rearrange("p (f n) -> p f n", f=HID_TILES)
        silu_g = arena[:, 4108:5132].rearrange("p (s n) -> p s n", s=2)
        eacc = arena[:, 0:1024].rearrange("p (t d) -> p t d", t=NT)
        vtok = arena[:, 0:1024].rearrange("p (t d) -> p t d", t=NT)
        prob = arena[:, 4096:8192].rearrange("p (s n) -> p s n", s=2 * QUAD)
        qf = arena[:, 8192:9216]
        kf = arena[:, 9216:10240]
        qrest = arena[:, 10240:11264]
        krest = arena[:, 11264:12288]
        q3 = arena[:, 12288:13824].bitcast(BF16).rearrange("p (s n) -> p s n", s=3)
        k3 = arena[:, 13824:15360].bitcast(BF16).rearrange("p (s n) -> p s n", s=3)
        Vq = sb("Vq", [P, NT, QUAD, VCOLS])
        pv_sb = sb("pv_sb", [P, HALF])
        o_rec = sb("o_rec", [P, HT, QUAD])
        smax = sb("smax", [P, 2, 16])
        shift16 = sb("shift16", [P, SHIFT_PARTS, 16], BF16)
        shiftT = sb("shiftT", [SHIFT_PARTS * 16, P], BF16)
        dtz = sb("dtz", [P, NT, SSM_HEADS])
        dtu = sb("dtu", [P, NT, SSM_HEADS])
        dts = sb("dts", [P, NT, SSM_HEADS])
        dts2 = sb("dts2", [P, NT, SSM_HEADS])
        dtp = sb("dtp", [P, NT, SSM_HEADS])
        dt = sb("dt", [P, NT, SSM_HEADS])
        av = sb("av", [P, NT, SSM_HEADS])
        decay = sb("decay", [P, 3, NT, SSM_HEADS])
        ecT = sb("ecT", [NT * SSM_HEADS, P])
        aU = sb("aU", [P, 2, SSM_HEADS, P])
        Gm = sb("Gm", [P, 2, P])
        btok = sb("btok", [P, 2, NSTATE])
        hst = sb("hst", [P, 2, SSM_HEADS, SSM_DIM])
        hdec = sb("hdec", [P, SSM_HEADS, SSM_DIM])
        lg = sb("lg", [P, NT, E])
        sc = sb("sc", [P, NT, E])
        red = sb("red", [P, NT])
        top8 = sb("top8", [P, NT, 8])
        idx8 = sb("idx8", [P, NT, 8], U32)
        idxf = sb("idxf", [P, NT, 8])
        pick = sb("pick", [P, TOPK, NT, E])
        pw = sb("pw", [P, TOPK, NT, E])
        gsel = sb("gsel", [P, NT, E])
        pick16 = sb("pick16", [P, NT, E], BF16)
        pos = sb("pos", [P, NT, E])
        posk = sb("posk", [P, TOPK, NT])
        okk = sb("okk", [P, TOPK, NT])
        fark = sb("fark", [P, TOPK, NT])
        slotf = sb("slotf", [P, TOPK, NT])
        slot = sb("slot", [P, TOPK, NT], U32)
        iota_i = sb("iota_i", [P, E], I32)
        ids = sb("ids", [P, NT, TOPK], I32)
        idsf = sb("idsf", [P, NT, TOPK])
        turn_base = sb("turn_base", [P, 1])
        blank = arena[:, 6 * L:6 * L + 32 * ROW].rearrange("p (c d) -> p c d", d=ROW)
        place = [0]

        def carve(cols):
            place[0] += cols
            assert place[0] <= 15800
            return arena[:, place[0] - cols:place[0]]

        ex_in = carve(2 * CAP_TILES * ROW).rearrange("p (s c d) -> p s c d", s=2, c=CAP_TILES)
        cfc = carve(4 * D_GATE).rearrange("p (s n) -> p s n", s=2)
        cproj = carve(4 * D)[0:FFH].rearrange("p (s j n) -> p s j n", s=2, j=2)
        ex_xT = carve(2 * CAPACITY).rearrange("p (s n) -> p s n", s=2)
        ex_silu = carve(2 * CAPACITY).rearrange("p (s n) -> p s n", s=2)
        ex_hid = carve(4 * CAPACITY).rearrange("p (s j n) -> p s j n", s=2, j=2)
        ex_out = carve(2 * CAPACITY).rearrange("p (s c d) -> p s c d", s=2, c=CAP_TILES)
        res = carve(2 * NT * TOPK * D).rearrange("p (s t d) -> p s t d", s=2, t=NT)
        fin = carve(2 * NT * D).rearrange("p (s t d) -> p s t d", s=2, t=NT)
        fsum = carve(NT * D).rearrange("p (t d) -> p t d", t=NT)
        ex_ids = sb("ex_ids", [P, 2, CAP_TILES], U32)
        fin_w = sb("fin_w", [P, NT, TOPK])

        ps = ctx.enter_context(nc.psum_tensor("ps", [P, 8, HALF], F32))

        def sem(name):
            return ctx.enter_context(nc.semaphore(name))

        turn = {n: sem(n) for n in """
            x_loaded ss1 rms1_var rms1 xn1 hdr_zero dt_psum dt_abs dt_u a_ready
            cum_psum decay_exp ecT_psum ecT_sb ec_stored ec_bcast proj_psum proj_used tap0 conv_done xbc_ready
            aU_ready tr_psum xdt_ready btok_ready g_psum gm_ready seg_psum l_ready cs_ready w_ready
            y_psum stu_psum h_ready hdec_ready xw_ready y_used gated sq_ready mix_psum mix_var mix_rstd x1_ready
            ss3 rms3_var rms3 xn3 mlp_psum gate_silu hid_ready down_psum res_sum skip_sum
            ln_var ln_rstd normed route_psum route_shift route_exp
            gsel_ready gT_psum gT_sb bias_psum bias_used exp_psum exp_used
            xT_psum xnT_ready qk_psum v_psum q_ready k_ready q_part k_part q_rest k_rest qk_stored qk_back v_ready
            s_psum s_max shift_hi shift_cut shiftT_psum shiftT_sb shift_stored shift_back vq_ready
            st_psum p_ready pv_done pv_evac pvT_psum o_recip o_ready tbank_free
            oT_psum oT_sb proj_out res_bias x3_kept route1_psum route1_shift route1_exp
            pick16_ready rank_psum slot_ready row_ids dve_step
            """.split()}
        S = type("Turn", (), turn)
        numbers = sorted(s.num for s in turn.values())
        assert numbers == list(range(numbers[0], numbers[-1] + 1))
        turn_range = range(numbers[0], numbers[-1] + 1)
        w_loaded, consts, zero_rows, parts_cut, prep, prep_dma, a_exp, prepared, base_step = (
            sem(n) for n in "w_loaded consts zero_rows parts_cut prep prep_dma a_exp prepared base_step".split())
        ended, clearing, go_on = (sem(n) for n in "ended clearing go_on".split())
        fence = sem("fence")
        scattered = sem("scattered")
        ex_loaded = sem("ex_loaded0"), sem("ex_loaded1")
        ex_in_free, ex_ids_free, ex_tr, ex_xT_free, ex_xT_ready, ex_up, ex_up_free, ex_silu_ready, ex_hid_ready = (
            sem(n) for n in ("ex_in_free ex_ids_free ex_tr ex_xT_free ex_xT_ready ex_up ex_up_free ex_silu_ready "
                             "ex_hid_ready").split())
        ex_down, ex_down_free, ex_out_ready, ex_out_free, ex_ids_ready, ex_scattered, all_scattered = (
            sem(n) for n in "ex_down ex_down_free ex_out_ready ex_out_free ex_ids_ready ex_scattered all_scattered".split())
        res_loaded = sem("res_loaded0"), sem("res_loaded1")
        res_free, fin_step, fin_var, fin_rstd, fin_out, stored = (
            sem(n) for n in "res_free fin_step fin_var fin_rstd fin_out stored".split())
        N_CONSTS = 19
        FIN_STEPS = 5 + 3 * NT

        class Steps:

            def __init__(self, eng, semaphore):
                self.eng, self.sem, self.n = eng, semaphore, 0

            def mark(self, ins):
                self.n += 1
                ins.then_inc(self.sem, 1)
                return self.n

            def wait(self, n):
                self.eng.wait_ge(self.sem, n)

            def link(self, ins):
                self.wait(self.mark(ins))

        def bank(i):
            return ps[:, i, :]

        def tiles4(i):
            return ps[:, i, :].rearrange("p (t d) -> p t d", t=HT)

        def per_tile(ap):
            return ap.unsqueeze(2).to_broadcast([P, ap.shape[1], D])

        block = ctx.enter_context(nc.Block())

        def row(ap, n=P):
            return ap.rearrange("(a n) -> a n", a=1).partition_broadcast(n)

        def col(ap):
            return ap.rearrange("(p a) -> p a", a=1)

        weights = [
            (w_in[:], t["in_proj_wT"]), (w_gate[:], t["gate_wT"]), (w_up[:], t["up_wT"]),
            (w_down[:], t["down_wT"].rearrange("(f p) d -> p f d", p=P)),
            (w_out[:], t["out_proj_wT"].rearrange("(j p) d -> p j d", p=P)),
            (conv_w[:], t["conv_w"].rearrange("(f p) k -> p f k", p=P)),
            (conv_b[:], t["conv_b"].rearrange("(p f) -> p f", f=CONV_TILES)),
            (norm_w[:], t["norm_w"].rearrange("(p f) -> p f", f=2)),
            (dt_bias[:], row(t["dt_bias"])), (a_neg[:], row(t["A_log"])),
            (mixer_row[:], row(t["mixer_scale"])), (mlp_row[:], row(t["mlp_scale"])),
            (w_exp[:], t["expert_wT"]), (b_exp[:], t["expert_b"]),
            (w_route0[:, 0:E], t["route0_wT"]), (w_route1[:, 0:E], t["route1_w"]), (b_route0[:], row(t["route0_b"])),
            (ln_g[:], col(t["ln_g"])), (ln_b[:], col(t["ln_b"])),
            (w_qkv[:], t["w_qkv"]), (w_proj[:], t["w_attn_out"]),
            (b_q[:], col(t["b_qkv"][0:D])), (b_k[:], col(t["b_qkv"][D:2 * D])),
            (b_v[:], row(t["b_qkv"][2 * D:3 * D])), (b_proj[:], row(t["b_attn_out"])),
            (rel_own[:], col(t["rel_own"])), (rel_other[:], col(t["rel_other"])),
        ] + [(d_col[SSM_DIM * (h % 2):SSM_DIM * (h % 2 + 1), h // 2:h // 2 + 1], row(t["D"][h:h + 1], SSM_DIM))
             for h in range(SSM_HEADS)]
        loaded_all = 16 * (len(weights) + 2)
        pos_tab = arena[:, 0:2 * L].rearrange("p (s n) -> p s n", s=2)
        pos_q = arena[0:HD, 2 * L:3 * L]
        pos_k = arena[:, 3 * L:4 * L]
        rest_q = arena[0:HD, 4 * L:5 * L]
        rest_k = arena[:, 5 * L:6 * L]

        @block.sync
        def _(sp):
            sp.dma_start(pos_tab, t["pos_key"].rearrange("s p n -> p s n")).then_inc(w_loaded, 16)
            sp.dma_start(pos_q, t["pos_query"]).then_inc(w_loaded, 16)
            for dst, src in weights:
                sp.dma_start(dst, src).then_inc(w_loaded, 16)
            sp.wait_ge(zero_rows, 2)
            sp.dma_start(expert_in.rearrange("(p c) d -> p c d", p=P), blank).then_inc(prep_dma, 16)
            for n in range(TOPK):
                sp.dma_start(expert_out[n * B * L:(n + 1) * B * L, :].rearrange("(p c) d -> p c d", p=P),
                             x3_all[:]).then_inc(prep_dma, 16)
            sp.wait_ge(parts_cut, 3)
            sp.dma_start(q_parts[:, 0:HD, :].rearrange("s p n -> p s n"), k3[0:HD]).then_inc(prep_dma, 16)
            sp.wait_ge(parts_cut, 6)
            sp.dma_start(k_parts.rearrange("s p n -> p s n"), q3).then_inc(prep_dma, 16)
            sp.wait_ge(prep_dma, 5 * 16)
            for n, (qp, kp) in enumerate(PARTS):
                lo = 2 * HD * n + HD
                sp.dma_start(AQ[lo:lo + HD, :, :], q_parts[qp, 0:HD, :].unsqueeze(1)
                             .to_broadcast([HD, HEADS, L])).then_inc(prep_dma, 16)
                sp.dma_start(BK[lo:lo + HD, :, :],
                             k_parts[kp].rearrange("(h d) n -> d h n", d=HD)).then_inc(prep_dma, 16)
            sp.wait_ge(prep_dma, 16 * (5 + 2 * len(PARTS)))
            with sp.Fori(0, B) as b:
                sp.dma_start(xa[:], t["x"][b].rearrange("(t p) d -> p t d", p=P)).then_inc(S.x_loaded, 16)
                sp.wait_ge(S.ecT_sb, 1)
                sp.dma_start(ecum_rows, ecT[:]).then_inc(S.ec_stored, 16)
                sp.wait_ge(S.ec_stored, 16)
                sp.dma_start(ecumB, ecum_rows.rearrange("(c h) n -> c h n", h=SSM_HEADS)
                             .partition_broadcast(P)).then_inc(S.ec_bcast, 16)
                for s in range(3):
                    sp.wait_ge(S.q_part, s + 1)
                    sp.dma_start(q_parts[s], q3[:, s, :]).then_inc(S.qk_stored, 16)
                    sp.wait_ge(S.k_part, s + 1)
                    sp.dma_start(k_parts[s], k3[:, s, :]).then_inc(S.qk_stored, 16)
                sp.wait_ge(S.qk_stored, 6 * 16)
                for n, (qp, kp) in enumerate(PARTS):
                    lo = 2 * HD * n
                    sp.dma_start(AQ[lo:lo + HD, :, :],
                                 q_parts[qp].rearrange("(h d) n -> d h n", d=HD)).then_inc(S.qk_back, 16)
                    sp.dma_start(BK[lo:lo + HD, :, :],
                                 k_parts[kp].rearrange("(h d) n -> d h n", d=HD)).then_inc(S.qk_back, 16)
                def shift_rows_back(m, Q, qh):
                    sp.wait_ge(S.shiftT_sb, m + 1)
                    sp.sem_inc(fence, 1)
                    sp.dma_start(shift_rows, shiftT[:]).then_inc(S.shift_stored, 16)
                    sp.wait_ge(S.shift_stored, 16 * m + 16)
                    sp.sem_inc(fence, 1)
                    heads = slice(QUAD * Q, QUAD * Q + QUAD) if isinstance(Q, int) else bass.ds(QUAD * Q, QUAD)
                    sp.dma_start(AQ[SCORE_ROWS:SCORE_ROWS + SHIFT_PARTS, heads, qh * HALF:(qh + 1) * HALF],
                                shift_rows.rearrange("(s h q) n -> s h (q n)", s=SHIFT_PARTS, h=QUAD))\
                        .then_inc(S.shift_back, 16)
                    sp.wait_ge(S.shift_back, 16 * m + 16)
                    sp.sem_inc(fence, 1)

                shift_rows_back(0, 0, 0)
                with sp.Fori(0, NQUADS - 1) as Q:
                    shift_rows_back(2 * Q + 1, Q, 1)
                    shift_rows_back(2 * Q + 2, Q + 1, 0)
                shift_rows_back(2 * NQUADS - 1, NQUADS - 1, 1)
                sp.wait_ge(ended, 4 * b + 4)
                sp.sem_inc(clearing, 1)
                sp.sem_clear(turn_range)
                sp.sem_inc(go_on, 1)
            with sp.Fori(0, E // 2) as e2:
                for s in range(2):
                    sp.wait_ge(ex_in_free, 2 * e2 + s + 1)
                    sp.sem_inc(fence, 1)
                    sp.wait_ge(ex_ids_free, 2 * e2 + s + 1)
                    sp.sem_inc(fence, 1)
                    e = 2 * e2 + s
                    sp.dma_start(ex_in[:, s], expert_in[bass.ds(CAPACITY * e, CAPACITY), :]
                                 .rearrange("(c p) d -> p c d", p=P)).then_inc(ex_loaded[s], 16)
                    sp.dma_start(cfc[:, s], t["c_fc"][e]).then_inc(ex_loaded[s], 16)
                    sp.dma_start(cproj[:, s], t["c_proj"][e].rearrange("(j p) n -> p j n", p=FFH)).then_inc(ex_loaded[s], 16)
            sp.sem_inc(stored, 32)
            sp.wait_ge(all_scattered, 1)
            rows_v = expert_out.rearrange("(b t p k) d -> b p t (k d)", b=B, t=NT, k=TOPK)
            out_v = t["out"].rearrange("b (t p) d -> b p t d", p=P)
            with sp.Fori(0, B // 2) as b2:
                for s in range(2):
                    sp.wait_ge(res_free, 2 * b2 + s + 1)
                    sp.sem_inc(fence, 1)
                    sp.dma_start(res[:, s], rows_v[2 * b2 + s]).then_inc(res_loaded[s], 16)
                for s in range(2):
                    sp.wait_ge(fin_out, 2 * b2 + s + 1)
                    sp.sem_inc(fence, 1)
                    sp.dma_start(out_v[2 * b2 + s], fin[:, s]).then_inc(stored, 16)
            sp.wait_ge(stored, 16 * B + 32)

        @block.tensor
        def _(pe):
            def transposes(src, dst_bank, done, n=HT):
                for i in range(n):
                    last = nc.tensor.transpose(bank(dst_bank)[:, i * P:(i + 1) * P], src(i), ident[:])
                last.then_inc(done, 1)

            def half_transposes(src, ready, before=0):
                for H in range(2):
                    pe.wait_ge(ready, before + H + 1)
                    transposes(lambda i: src[:, H * HT + i, :], H, S.xT_psum)

            def tile(a, n):
                return a[:, n * P:(n + 1) * P]

            def mm(out, lhsT, rhs, first=True, last=True):
                return nc.tensor.matmul(out, lhsT, rhs, start=first, stop=last)

            def half(H):
                return slice(H * HALF, (H + 1) * HALF)

            def in_projection():
                half_transposes(xn, S.xn1)
                for H in range(2):
                    pe.wait_ge(S.xnT_ready, H + 1)
                    for i in range(HT):
                        last = mm(tile(bank(6 + H), i), tile(xnT, H * HT + i), w_dt[:])
                    last.then_inc(S.dt_psum, 1)
                n = 0
                for f0, nf in ((2, CONV_TILES), (0, 2)):
                    for H in range(2):
                        for f in range(f0, f0 + nf):
                            if n >= 4:
                                pe.wait_ge(S.proj_used, n - 3)
                            mm(bank(2 + n % 4), tile(w_in, f), xnT[:, half(H)]).then_inc(S.proj_psum, 1)
                            n += 1
                            if n == 4:
                                pe.wait_ge(S.a_ready, 1)
                                a32 = av[:].rearrange("p c h -> p (c h)")
                                for i, m in enumerate((upto, after, ones)):
                                    last = mm(bank(6)[:, 32 * i:32 * i + 32], m[:], a32)
                                last.then_inc(S.cum_psum, 1)
                            if n == 8:
                                pe.wait_ge(S.decay_exp, 1)
                                nc.tensor.transpose(bank(7)[0:32, 0:P],
                                                    decay[:, 0].rearrange("p c h -> p (c h)"), ident[:])\
                                    .then_inc(S.ecT_psum, 1)

            TRB, GB, SEGB, STUB, YB, OUTB, SSB = 0, 1, 2, 3, 4, 6, 7

            def chunk_front(c):
                if c == 0:
                    pe.wait_ge(S.xbc_ready, CONV_TILES)
                    pe.wait_ge(S.proj_used, 12)
                if c >= 1:
                    pe.wait_ge(S.xdt_ready, c)
                    pe.wait_ge(S.btok_ready, c)
                for i, f in enumerate((0, 1, 2)):
                    last = nc.tensor.transpose(tile(bank(TRB), i), tile(xbc[:, f], c), ident[:])
                last.then_inc(S.tr_psum, 1)
                if c >= 1:
                    pe.wait_ge(S.gm_ready, c)
                mm(bank(GB)[:, 0:P], tile(xbc[:, 2], c), tile(xbc[:, 3], c)).then_inc(S.g_psum, 1)
                pe.wait_ge(S.aU_ready, c + 1)
                if c >= 1:
                    pe.wait_ge(S.l_ready, c)
                mm(bank(SEGB), after[:], aU[:, c % 2].rearrange("p h n -> p (h n)")).then_inc(S.seg_psum, 1)

            def chunk_back(c):
                if c == HT:
                    pe.wait_ge(S.y_used, 2)
                pe.wait_ge(S.xdt_ready, c + 1)
                pe.wait_ge(S.w_ready, c + 1)
                pe.wait_ge(S.cs_ready, c + 1)
                pe.wait_ge(S.h_ready, c + 1)
                for h in range(SSM_HEADS):
                    lo = SSM_DIM * (h % 2)
                    out = bank(YB + h // 2)[lo:lo + SSM_DIM, (c % HT) * P:(c % HT + 1) * P]
                    mm(out, xdt[:, c % 2, h], Wm[:, c % 2, h], True, False)
                    last = mm(out, hst[:, c % 2, h], Cs[:, c % 2, h], False, True)
                last.then_inc(S.y_psum, 1)
                if c < NT - 1:
                    pe.wait_ge(S.xw_ready, c + 1)
                    pe.wait_ge(S.btok_ready, c + 1)
                    if c >= 1:
                        pe.wait_ge(S.h_ready, c + 1)
                    mm(bank(STUB)[:, 0:D_INNER], btok[:, c % 2], xw[:, c % 2].rearrange("p h d -> p (h d)"))\
                        .then_inc(S.stu_psum, 1)

            def mix_out(H):
                if H == 0:
                    pe.wait_ge(S.ecT_sb, 1)
                if H == 1:
                    pe.wait_ge(S.x1_ready, 1)
                pe.wait_ge(S.gated, 2 * H + 2)
                pe.wait_ge(S.sq_ready, 2 * H + 2)
                for i in range(HT):
                    n = H * HT + i
                    for j in range(2):
                        mm(tile(bank(OUTB), i), tile(zg[:, j], n), w_out[:, j], j == 0, j == 1)
                    for j in range(2):
                        last = mm(tile(bank(SSB), i), tile(y1[:, j], i), ones[:], j == 0, j == 1)
                last.then_inc(S.mix_psum, 1)

            def mlp():
                pe.wait_ge(S.h_ready, NT)
                pe.wait_ge(S.l_ready, NT)
                pe.wait_ge(S.gm_ready, NT)
                half_transposes(xn, S.xn3)
                pe.wait_ge(S.y_used, 4)
                pe.wait_ge(S.x1_ready, 2)
                n = 0
                for H in range(2):
                    pe.wait_ge(S.xnT_ready, 2 + H + 1)
                    for f in range(HID_TILES):
                        if n >= 2:
                            pe.wait_ge(S.hid_ready, n - 1)
                        g = 2 + 2 * (n % 2)
                        mm(bank(g), tile(w_gate, f), xnT[:, half(H)])
                        mm(bank(g + 1), tile(w_up, f), xnT[:, half(H)]).then_inc(S.mlp_psum, 1)
                        n += 1
                for H in range(2):
                    pe.wait_ge(S.hid_ready, HID_TILES * (H + 1))
                    for i in range(HT):
                        for f in range(HID_TILES):
                            last = mm(tile(bank(6 + H), i), tile(hidT[:, f], H * HT + i), w_down[:, f],
                                      f == 0, f == HID_TILES - 1)
                    last.then_inc(S.down_psum, 1)

            def route(w, done):
                for i in range(NT):
                    last = mm(tile(bank(2 + i // HT), i % HT), tile(xnT, i), w[:])
                last.then_inc(done, 1)

            def moe0():
                pe.wait_ge(S.xnT_ready, 2 + 2)
                half_transposes(xb, S.normed, 0)
                pe.wait_ge(S.xnT_ready, 4 + 2)
                pe.wait_ge(S.hid_ready, 2 * HID_TILES)
                route(w_route0, S.route_psum)
                for i in range(NT):
                    b0 = 4 + 2 * (i % 2)
                    if i >= 2:
                        pe.wait_ge(S.exp_used, i - 1)
                    if i == 0:
                        pe.wait_ge(S.skip_sum, 2)
                    for k in range(2):
                        last = mm(bank(b0 + k), tile(xnT, i),
                                  w_exp[:, HT * k:HT * (k + 1)].rearrange("p e d -> p (e d)"))
                    last.then_inc(S.exp_psum, 1)
                    if i == 1:
                        pe.wait_ge(S.gsel_ready, 1)
                        for n in range(NT):
                            last = nc.tensor.transpose(bank(n // HT)[0:E, (n % HT) * P:(n % HT + 1) * P],
                                                       gsel[:, n, :], ident[:])
                        last.then_inc(S.gT_psum, 1)
                        pe.wait_ge(S.gT_sb, 1)
                        pe.wait_ge(S.route_shift, 2)
                        for n in range(NT):
                            last = mm(tile(bank(2 + n // HT), n % HT), gT[:, n * P:(n + 1) * P], b_exp[:])
                        last.then_inc(S.bias_psum, 1)

            def qkv():
                half_transposes(xn, S.normed, 4)
                pe.wait_ge(S.exp_used, NT)
                pe.wait_ge(S.bias_used, 1)
                for i in range(2):
                    for H in range(2):
                        if i == 0:
                            pe.wait_ge(S.xnT_ready, 6 + H + 1)
                        mm(bank(2 + 2 * i + H), tile(w_qkv, i), xnT[:, half(H)]).then_inc(S.qk_psum, 1)
                for H in range(2):
                    for i in range(HT):
                        last = mm(tile(bank(6 + H), i), tile(xnT, H * HT + i), w_qkv[:, 2 * D:3 * D])
                    last.then_inc(S.v_psum, 1)

            SB, STB, PVB, TB = 0, 4, 6, 7

            def score_matmul(Q, qh, p, kh, count):
                g, qt = p // HT, p % HT
                b0 = SB + 2 * (p % 2)
                if kh == 0 and count is not None:
                    pe.wait_ge(S.s_max, count - 1)
                q0 = qh * HALF + qt * P
                if isinstance(Q, int):
                    lhsT, rhs = AQ[0:SCORE_ROWS, QUAD * Q + g, q0:q0 + P], BK[0:SCORE_ROWS, QUAD * Q + g, kh * HALF:(kh + 1) * HALF]
                else:
                    lhsT = AQ[0:SCORE_ROWS, bass.ds(QUAD * Q + g, 1), q0:q0 + P].rearrange("p a n -> p (a n)")
                    rhs = BK[0:SCORE_ROWS, bass.ds(QUAD * Q + g, 1), kh * HALF:(kh + 1) * HALF].rearrange("p a n -> p (a n)")
                ins = mm(bank(b0 + kh), lhsT, rhs)
                if kh == 1:
                    ins.then_inc(S.s_psum, 1)

            def shift_transpose(m, tb):
                pe.wait_ge(S.shift_cut, m + 1)
                pe.wait_ge(S.tbank_free, tb)
                nc.tensor.transpose(bank(TB)[0:SHIFT_PARTS * 16, 0:P // 2].bitcast(BF16),
                                    shift16[:].rearrange("p s n -> p (s n)"), ident16[:])\
                    .then_inc(S.shiftT_psum, 1)

            def pv_burst(Q, qh, kt):
                if qh == 1 and kt == 0:
                    pe.wait_ge(S.pv_evac, 2 * Q + 1)
                if qh == 0 and kt == 0:
                    pe.wait_ge(S.vq_ready, Q + 1)
                pe.wait_ge(S.p_ready, 64 * Q + 32 * qh + QUAD * kt + QUAD)
                for g in range(QUAD):
                    last = mm(bank(PVB)[32 * g:32 * g + VCOLS, :], Vq[:, kt, g, :], prob[:, QUAD * (kt % 2) + g, :],
                              kt == 0, kt == NT - 1)
                last.then_inc(S.pv_done, 1)

            def pv_transpose(Q, qh, tb):
                pe.wait_ge(S.pv_evac, 2 * Q + qh + 1)
                pe.wait_ge(S.tbank_free, tb)
                transposes(lambda i: tile(pv_sb, i), TB, S.pvT_psum)

            def attention():
                pe.wait_ge(S.qk_back, 2 * len(PARTS) * 16)
                pe.wait_ge(S.k_ready, 2)
                pe.wait_ge(S.v_ready, 2)
                for qh in range(2):
                    for p in range(16):
                        for kh in range(2):
                            count = 16 * qh + p
                            score_matmul(0, qh, p, kh, count if count >= 2 else None)
                    if qh == 0:
                        shift_transpose(0, 1)
                with pe.Fori(0, NQUADS - 1) as Q:
                    quad(Q, True)
                quad(NQUADS - 1, False)

            def quad(Q, ahead):
                base = 4 * Q + 2
                tb = 0
                for qh in range(2):
                    n = 2 * Q + qh
                    for kt in range(NT):
                        for g in range(QUAD):
                            u = QUAD * kt + g
                            if ahead:
                                score_matmul(Q + 1, qh, u // 2, u % 2, 32 * Q + 32 + 16 * qh + u // 2)
                            if kt == 0 and g == 0:
                                pe.wait_ge(S.shift_back, 16 * n + 16)
                            if 32 * qh + u >= 2:
                                pe.wait_ge(S.p_ready, 64 * Q + 32 * qh + u - 1)
                            if isinstance(Q, int):
                                lhsT, rhs = BK[:, QUAD * Q + g, kt * P:(kt + 1) * P], AQ[:, QUAD * Q + g, half(qh)]
                            else:
                                lhsT = BK[:, bass.ds(QUAD * Q + g, 1), kt * P:(kt + 1) * P].rearrange("p a n -> p (a n)")
                                rhs = AQ[:, bass.ds(QUAD * Q + g, 1), half(qh)].rearrange("p a n -> p (a n)")
                            mm(bank(STB + u % 2), lhsT, rhs).then_inc(S.st_psum, 1)
                        if kt >= 1:
                            pv_burst(Q, qh, kt - 1)
                        elif qh == 1:
                            pv_burst(Q, 0, NT - 1)
                        if kt == 1 and qh == 1:
                            pv_transpose(Q, 0, base + tb)
                            tb += 1
                        if kt == 3 and (ahead or qh == 0):
                            shift_transpose(n + 1, base + tb)
                            tb += 1
                pv_burst(Q, 1, NT - 1)
                pv_transpose(Q, 1, base + tb)

            def attention_out():
                pe.wait_ge(S.o_ready, 2 * NQUADS)
                for H in range(2):
                    transposes(lambda i: o_tok[:, H * HT + i, :], H, S.oT_psum)
                for H in range(2):
                    pe.wait_ge(S.oT_sb, H + 1)
                    for i in range(HT):
                        last = mm(tile(bank(2 + H), i), tile(xnT, H * HT + i), w_proj[:])
                    last.then_inc(S.proj_out, 1)

            def moe1_route():
                half_transposes(xb, S.normed, 6)
                pe.wait_ge(S.xnT_ready, 8 + 2)
                route(w_route1, S.route1_psum)
                pe.wait_ge(S.pick16_ready, 1)
                m = pick16[:].rearrange("p t e -> p (t e)")
                mm(bank(4)[:, 0:NT * E], before16[:], m)
                mm(bank(5)[:, 0:NT * E], ones16[:], m).then_inc(S.rank_psum, 1)

            pe.wait_ge(prepared, 1)
            pe.wait_ge(consts, N_CONSTS)
            with pe.Fori(0, B) as b:
                in_projection()
                chunk_front(0)
                for c in range(NT):
                    if c + 1 < NT:
                        chunk_front(c + 1)
                    chunk_back(c)
                    if c == HT + 1:
                        mix_out(0)
                mix_out(1)
                mlp()
                moe0()
                qkv()
                attention()
                attention_out()
                moe1_route()
                pe.sem_inc(ended, 1)
                pe.wait_ge(go_on, b + 1)
            pe.sem_inc(ex_in_free, 2)
            with pe.Fori(0, E // 2) as e2:
                for s in range(2):
                    pe.wait_ge(ex_loaded[s], 48 * e2 + 48)
                    pe.wait_ge(ex_xT_free, 2 * e2 + s + 1)
                    for i in range(CAP_TILES):
                        last = nc.tensor.transpose(tile(bank(0), i), ex_in[:, s, i, 0:D], ident[:])
                    last.then_inc(ex_tr, 1)
                    pe.wait_ge(ex_xT_ready, 2 * e2 + s + 1)
                    pe.wait_ge(ex_up_free, 4 * e2 + 2 * s + 1)
                    for j in range(2):
                        if j == 1:
                            pe.wait_ge(ex_up_free, 4 * e2 + 2 * s + 2)
                        for k in range(2):
                            last = mm(bank(1 + 2 * j + k)[0:FFH], cfc[:, s, k * D_GATE + j * FFH:k * D_GATE + (j + 1) * FFH],
                                      ex_xT[:, s])
                        last.then_inc(ex_up, 1)
                    pe.wait_ge(ex_hid_ready, 4 * e2 + 2 * s + 2)
                    pe.wait_ge(ex_down_free, 2 * e2 + s + 1)
                    for i in range(CAP_TILES):
                        for j in range(2):
                            last = mm(tile(bank(5 + s), i), ex_hid[0:FFH, s, j, i * P:(i + 1) * P], cproj[:, s, j],
                                      j == 0, j == 1)
                    last.then_inc(ex_down, 1)
                    pe.wait_ge(ex_down, 2 * e2 + s + 1)
                    pe.sem_inc(ex_in_free, 1)

        @block.scalar
        def _(act):
            def squares(src, ready, need, done):
                act.wait_ge(ready, need)
                for i in range(NT):
                    nc.scalar.activation(xn[:, i, :], src[:, i, :], ACT.Square, accum_out=ss[:, i:i + 1]).then_inc(done, 1)

            def evac_T(nth, **affine):
                for H in range(2):
                    act.wait_ge(S.xT_psum, 2 * nth + H + 1)
                    func = ACT.Identity if affine else ACT.Copy
                    nc.scalar.activation(xnT[:, H * HALF:(H + 1) * HALF], bank(H), func, **affine).then_inc(S.xnT_ready, 1)

            act.wait_ge(w_loaded, loaded_all)
            nc.scalar.activation(a_neg[:], a_neg[:], ACT.Exp).then_inc(a_exp, 1)
            act.wait_ge(prepared, 1)
            act.wait_ge(consts, N_CONSTS)
            with act.Fori(0, B) as b:
                squares(xa, S.x_loaded, 16, S.ss1)
                evac_T(0)
                act.wait_ge(S.dt_abs, 1)
                nc.scalar.activation(dtu[:], dts[:], ACT.Exp, scale=-1.0).then_inc(S.dt_u, 1)
                act.wait_ge(S.hdr_zero, 1)
                for n in range(2 * CONV_TILES):
                    H, f = n // CONV_TILES, n % CONV_TILES
                    act.wait_ge(S.proj_psum, n + 1)
                    lo = TAPS - 1 + H * HALF
                    nc.scalar.activation(raw[:, f, lo:lo + HALF], bank(2 + n % 4), ACT.Copy).then_inc(S.proj_used, 1)
                    if n == 5:
                        act.wait_ge(S.cum_psum, 1)
                        nc.scalar.activation(decay[:].rearrange("p s c h -> p (s c h)"), bank(6)[:, 0:96], ACT.Exp)\
                            .then_inc(S.decay_exp, 1)
                act.wait_ge(S.proj_used, 2 * CONV_TILES)
                for f in range(CONV_TILES):
                    nc.scalar.activation(xbc[:, f, :], raw[:, f, 0:L], ACT.Identity,
                                         scale=conv_w[:, f, 0:1], bias=conv_b[:, f:f + 1]).then_inc(S.tap0, 1)
                for n in range(2 * CONV_TILES, 2 * CONV_TILES + 4):
                    H, j = (n - 2 * CONV_TILES) // 2, n % 2
                    act.wait_ge(S.proj_psum, n + 1)
                    nc.scalar.activation(zg[:, j, H * HALF:(H + 1) * HALF], bank(2 + n % 4), ACT.Silu)\
                        .then_inc(S.proj_used, 1)
                for f in range(CONV_TILES):
                    act.wait_ge(S.conv_done, f + 1)
                    nc.scalar.activation(xbc[:, f, :], xbc[:, f, :], ACT.Silu).then_inc(S.xbc_ready, 1)
                for c in range(NT):
                    act.wait_ge(S.tr_psum, c + 1)
                    act.wait_ge(S.xdt_ready, c + 1)
                    if c >= 2:
                        act.wait_ge(S.stu_psum, c - 1)
                    nc.scalar.activation(btok[:, c % 2], bank(0)[:, 2 * P:3 * P], ACT.Copy).then_inc(S.btok_ready, 1)
                    act.wait_ge(S.seg_psum, c + 1)
                    if c >= 2:
                        act.wait_ge(S.w_ready, c - 1)
                    nc.scalar.activation(Lx[:, c % 2].rearrange("p h n -> p (h n)"), bank(2), ACT.Exp)\
                        .then_inc(S.l_ready, 1)
                    if c in (HT, NT - 1):
                        H = 0 if c == HT else 1
                        for j in range(2):
                            act.wait_ge(S.gated, 2 * H + j + 1)
                            nc.scalar.activation(y1[:, j], zg[:, j, H * HALF:(H + 1) * HALF], ACT.Square)\
                                .then_inc(S.sq_ready, 1)
                squares(xb, S.x1_ready, 2, S.ss3)
                evac_T(1)
                for n in range(2 * HID_TILES):
                    act.wait_ge(S.mlp_psum, n + 1)
                    if n >= 2:
                        act.wait_ge(S.hid_ready, n - 1)
                    nc.scalar.activation(silu_g[:, n % 2], bank(2 + 2 * (n % 2)), ACT.Silu).then_inc(S.gate_silu, 1)
                evac_T(2)
                act.wait_ge(S.route_shift, 3)
                nc.scalar.activation(sc[:], lg[:], ACT.Exp).then_inc(S.route_exp, 1)
                act.wait_ge(S.gT_psum, 1)
                for H in range(2):
                    last = nc.scalar.activation(gT[:, H * HALF:(H + 1) * HALF], bank(H)[0:E], ACT.Copy)
                last.then_inc(S.gT_sb, 1)
                evac_T(3, scale=ln_g[:], bias=ln_b[:])
                for H in range(2):
                    act.wait_ge(S.qk_psum, H + 1)
                    nc.scalar.activation(qf[:, H * HALF:(H + 1) * HALF], bank(2 + H), ACT.Identity,
                                         scale=float(HD) ** -0.5, bias=b_q[:]).then_inc(S.q_ready, 1)
                for s in range(3):
                    act.wait_ge(*((S.q_ready, 2) if s == 0 else (S.q_rest, s)))
                    nc.scalar.activation(q3[:, s, :], qf if s == 0 else qrest, ACT.Copy).then_inc(S.q_part, 1)
                    act.wait_ge(*((S.k_ready, 2) if s == 0 else (S.k_rest, s)))
                    nc.scalar.activation(k3[:, s, :], kf if s == 0 else krest, ACT.Copy).then_inc(S.k_part, 1)

                def quad(Q):
                    for qh in range(2):
                        for kt in range(NT):
                            for g in range(QUAD):
                                u = QUAD * kt + g
                                act.wait_ge(S.st_psum, 64 * Q + 32 * qh + u + 1)
                                if g == 0 and (kt >= 2 or qh == 1):
                                    act.wait_ge(S.pv_done, 16 * Q + 8 * qh + kt - 1)
                                nc.scalar.activation(prob[:, QUAD * (kt % 2) + g, :], bank(4 + u % 2), ACT.Exp)\
                                    .then_inc(S.p_ready, 1)
                            if kt == 0 and qh == 1:
                                evac_pv(Q, 0)
                    evac_pv(Q, 1)
                    act.wait_ge(S.pvT_psum, 2 * Q + 2)

                def evac_pv(Q, qh):
                    act.wait_ge(S.pv_done, 16 * Q + 8 * qh + 8)
                    if qh == 1:
                        act.wait_ge(S.pvT_psum, 2 * Q + 1)
                    nc.scalar.activation(pv_sb[:], bank(6), ACT.Copy).then_inc(S.pv_evac, 1)

                act.wait_ge(S.k_part, 3)
                with act.Fori(0, NQUADS - 1) as Q:
                    quad(Q)
                quad(NQUADS - 1)
                for H in range(2):
                    act.wait_ge(S.oT_psum, H + 1)
                    nc.scalar.activation(xnT[:, H * HALF:(H + 1) * HALF], bank(H), ACT.Copy).then_inc(S.oT_sb, 1)
                for H in range(2):
                    act.wait_ge(S.xT_psum, 8 + H + 1)
                    act.wait_ge(S.proj_out, 2)
                    nc.scalar.activation(xnT[:, H * HALF:(H + 1) * HALF], bank(H), ACT.Copy).then_inc(S.xnT_ready, 1)
                nc.scalar.activation(x3_all[:, bass.ds(NT * b, NT), :], xb[:], ACT.Copy).then_inc(S.x3_kept, 1)
                for k in range(TOPK):
                    nc.scalar.activation(xrow[:, :, k, 0:D], xb[:], ACT.Copy).then_inc(S.x3_kept, 1)
                act.wait_ge(S.route1_shift, 3)
                nc.scalar.activation(sc[:], lg[:], ACT.Exp).then_inc(S.route1_exp, 1)
                act.wait_ge(S.route1_exp, 1)
                act.wait_ge(S.x3_kept, 3)
                act.wait_ge(S.xnT_ready, 8 + 2)
                act.sem_inc(ended, 1)
                act.wait_ge(go_on, b + 1)
            act.sem_inc(ex_xT_free, 1)
            act.sem_inc(ex_down_free, 2)
            with act.Fori(0, E // 2) as e2:
                for s in range(2):
                    act.wait_ge(ex_tr, 2 * e2 + s + 1)
                    act.wait_ge(ex_in_free, 2 * e2 + s + 1)
                    nc.scalar.activation(ex_xT[:, s], bank(0), ACT.Copy).then_inc(ex_xT_ready, 1)
                    act.wait_ge(ex_xT_ready, 2 * e2 + s + 1)
                    act.sem_inc(ex_xT_free, 1)
                    for j in range(2):
                        act.wait_ge(ex_up, 4 * e2 + 2 * s + j + 1)
                        act.wait_ge(ex_up_free, 4 * e2 + 2 * s + j + 1)
                        nc.scalar.activation(ex_silu[0:FFH, j], bank(1 + 2 * j)[0:FFH], ACT.Silu).then_inc(ex_silu_ready, 1)
                    act.wait_ge(ex_down, 2 * e2 + s + 1)
                    act.wait_ge(ex_out_free, 2 * e2 + s + 1)
                    nc.scalar.activation(ex_out[:, s].rearrange("p c d -> p (c d)"), bank(5 + s), ACT.Copy)\
                        .then_inc(ex_out_ready, 1)
                    act.wait_ge(ex_out_ready, 2 * e2 + s + 1)
                    act.sem_inc(ex_down_free, 1)

        @block.gpsimd
        def _(pool):
            g = nc.gpsimd
            pool_c = [0]

            def const(ins):
                pool_c[0] += 1
                ins.then_inc(consts, 1)

            g.memset(x3_all[:], 0.0).then_inc(zero_rows, 1)
            pool.wait_ge(w_loaded, loaded_all)
            pool.wait_ge(parts_cut, 6)
            const(g.memset(ident[:], 0.0))
            const(g.memset(upto[:], 1.0))
            const(g.memset(after[:], 1.0))
            const(g.memset(before16[:], 1.0))
            const(g.memset(ident16[:], 0.0))
            const(g.memset(ones[:], 1.0))
            const(g.memset(ones16[:], 1.0))
            const(g.memset(neg_half[:], -0.5))
            const(g.memset(Vq[:], 0.0))
            const(g.iota(iota_i[:], pattern=[[1, E]], base=0, channel_multiplier=0))
            const(g.iota(ids[:], pattern=[[P * TOPK, NT], [1, TOPK]], base=0, channel_multiplier=TOPK))
            pool.wait_ge(consts, pool_c[0])
            sel = dict(channel_multiplier=1, pattern=[[-1, P]], base=0)
            const(g.affine_select(out=ident[:], in_=ident[:], compare_op=ALU.not_equal, fill=1.0, **sel))
            const(g.affine_select(out=ident16[:], in_=ident16[:], compare_op=ALU.not_equal, fill=1.0, **sel))
            const(g.affine_select(out=after[:], in_=after[:], compare_op=ALU.is_gt, fill=0.0, **sel))
            flip = dict(channel_multiplier=-1, pattern=[[1, P]], base=0)
            const(g.affine_select(out=upto[:], in_=upto[:], compare_op=ALU.is_ge, fill=0.0, **flip))
            const(g.affine_select(out=before16[:], in_=before16[:], compare_op=ALU.is_gt, fill=0.0, **flip))
            const(g.memset(Vq[:, :, :, HD:HD + 1], 1.0))
            const(g.tensor_copy(iota_e[:], iota_i[:]))
            const(g.tensor_copy(idsf[:], ids[:]))
            assert pool_c[0] == N_CONSTS
            pool.wait_ge(prepared, 1)
            pool.wait_ge(consts, N_CONSTS)

            def rsqrt(var_ap, out_ap, ready, done, need=1):
                pool.wait_ge(ready, need)
                n = var_ap.shape[1]
                g.tensor_tensor(out_ap, var_ap, neg_half[:, 0:n], ALU.pow).then_inc(done, 1)

            with pool.Fori(0, B) as b:
                g.memset(raw[:, :, 0:TAPS - 1], 0.0).then_inc(S.hdr_zero, 1)
                rsqrt(var[:], rstd[:], S.rms1_var, S.rms1)
                g.memset(hst[:, 0], 0.0).then_inc(S.h_ready, 1)
                pool.wait_ge(S.a_ready, 1)
                for c in range(NT):
                    if c >= 2:
                        pool.wait_ge(S.seg_psum, c - 1)
                    g.tensor_tensor(aU[:, c % 2], upto[:].unsqueeze(1).to_broadcast([P, SSM_HEADS, P]),
                                    av[:, c].unsqueeze(2).to_broadcast([P, SSM_HEADS, P]), ALU.mult).then_inc(S.aU_ready, 1)
                    if c < NT - 1:
                        if c == 0:
                            pool.wait_ge(S.decay_exp, 1)
                        pool.wait_ge(S.h_ready, c + 1)
                        g.tensor_tensor(hdec[:], hst[:, c % 2],
                                        decay[:, 2, c].unsqueeze(2).to_broadcast([P, SSM_HEADS, SSM_DIM]),
                                        ALU.mult).then_inc(S.hdec_ready, 1)
                        pool.wait_ge(S.xdt_ready, c + 1)
                        if c >= 2:
                            pool.wait_ge(S.stu_psum, c - 1)
                        g.tensor_tensor(xw[:, c % 2], xdt[:, c % 2],
                                        decay[:, 1, c].unsqueeze(2).to_broadcast([P, SSM_HEADS, SSM_DIM]),
                                        ALU.mult).then_inc(S.xw_ready, 1)
                    if c == HT + 3:
                        rsqrt(var[:, 0:HT], rstd[:, 0:HT], S.mix_var, S.mix_rstd, 1)
                rsqrt(var[:, HT:NT], rstd[:, HT:NT], S.mix_var, S.mix_rstd, 2)
                rsqrt(var[:], rstd[:], S.rms3_var, S.rms3)
                g.tensor_tensor(xa[:], xa[:], xb[:], ALU.add).then_inc(S.res_sum, 1)
                rsqrt(var[:], rstd[:], S.ln_var, S.ln_rstd, 1)
                rsqrt(var[:], rstd[:], S.ln_var, S.ln_rstd, 2)
                rsqrt(var[:], rstd[:], S.ln_var, S.ln_rstd, 3)
                pool.wait_ge(S.normed, 6)
                g.tensor_tensor(xa[:], xa[:], b_proj[:].unsqueeze(1).to_broadcast([P, NT, D]), ALU.add).then_inc(S.res_bias, 1)

                def values(Q):
                    v = vtok[:, :, bass.ds(QUAD * HD * Q, QUAD * HD)] if not isinstance(Q, int) else \
                        vtok[:, :, QUAD * HD * Q:QUAD * HD * (Q + 1)]
                    g.tensor_copy(Vq[:, :, :, 0:HD], v.rearrange("p k (h d) -> p k h d", h=QUAD)).then_inc(S.vq_ready, 1)

                pool.wait_ge(S.v_ready, 2)
                values(0)
                with pool.Fori(0, NQUADS - 1) as Q:
                    pool.wait_ge(S.pv_done, 16 * Q + 16)
                    values(Q + 1)
                rsqrt(var[:], rstd[:], S.ln_var, S.ln_rstd, 4)
                for k in range(TOPK):
                    g.tensor_scalar(xrow[:, :, k, D:D + 1], idsf[:, :, k:k + 1], turn_base[:, 0:1], None, ALU.add)\
                        .then_inc(S.row_ids, 1)
                pool.wait_ge(S.row_ids, TOPK)
                pool.wait_ge(S.x3_kept, 3)
                pool.wait_ge(S.slot_ready, 1)
                for i in range(NT):
                    for k in range(TOPK):
                        g.indirect_dma_start(expert_in, bass.IndirectOffsetOnAxis(ap=slot[:, k, i:i + 1], axis=0),
                                             xrow[:, i, k, :], None, bounds_check=E * CAPACITY - 1, oob_is_err=False)\
                            .then_inc(scattered, 16)
                pool.wait_ge(scattered, (16 * NT * TOPK) * b + 16 * NT * TOPK)
                pool.sem_inc(fence, 1)
                g.tensor_scalar(turn_base[:], turn_base[:], float(L * TOPK), None, ALU.add).then_inc(base_step, 1)
                pool.wait_ge(base_step, b + 2)
                pool.sem_inc(ended, 1)
                pool.wait_ge(go_on, b + 1)
            pool.sem_inc(ex_out_free, 2)
            with pool.Fori(0, E // 2) as e2:
                for s in range(2):
                    pool.wait_ge(ex_ids_ready, 2 * e2 + s + 1)
                    pool.wait_ge(ex_out_ready, 2 * e2 + s + 1)
                    pool.sem_inc(fence, 1)
                    for i in range(CAP_TILES):
                        g.indirect_dma_start(expert_out, bass.IndirectOffsetOnAxis(ap=ex_ids[:, s, i:i + 1], axis=0),
                                             ex_out[:, s, i, :], None, bounds_check=TOPK * B * L - 1, oob_is_err=False)\
                            .then_inc(ex_scattered, 16)
                    pool.wait_ge(ex_scattered, (2 * e2 + s + 1) * (16 * CAP_TILES))
                    pool.sem_inc(ex_out_free, 1)
            pool.wait_ge(ex_scattered, 16 * CAP_TILES * E)
            pool.sem_inc(all_scattered, 1)
            with pool.Fori(0, B // 2) as b2:
                for s in range(2):
                    pool.wait_ge(fin_var, 2 * b2 + s + 1)
                    g.tensor_tensor(rstd[:], var[:], neg_half[:], ALU.pow).then_inc(fin_rstd, 1)

        @block.vector
        def _(dve):
            v = nc.vector

            def cut(src, rest, parts, sem_):
                v.tensor_copy(parts[0], src).then_inc(sem_, 1)
                k = cut.n = cut.n + 1
                dve.wait_ge(sem_, k)
                init.link(v.tensor_tensor(rest, src, parts[0], ALU.subtract))
                v.tensor_copy(parts[1], rest).then_inc(sem_, 1)
                k = cut.n = cut.n + 1
                dve.wait_ge(sem_, k)
                init.link(v.tensor_tensor(rest, rest, parts[1], ALU.subtract))
                v.tensor_copy(parts[2], rest).then_inc(sem_, 1)
                cut.n += 1
            cut.n = 0

            init = Steps(dve, prep)
            dve.wait_ge(w_loaded, loaded_all)
            cut(pos_q, rest_q, [k3[0:HD, s, :] for s in range(3)], parts_cut)
            init.link(v.tensor_scalar(pos_k, pos_tab[:, 0], rel_own[:], None, ALU.mult))
            init.link(v.scalar_tensor_tensor(pos_k, pos_tab[:, 1], rel_other[:], pos_k, ALU.mult, ALU.add))
            cut(pos_k, rest_k, [q3[:, s, :] for s in range(3)], parts_cut)
            init.link(v.memset(blank[:], 0.0))
            v.memset(blank[:, :, D:D + 1], FAR).then_inc(zero_rows, 1)
            init.mark(v.memset(BK[SCORE_ROWS:SCORE_ROWS + SHIFT_PARTS, :, :], 1.0))
            init.mark(v.memset(w_dt[:], 0.0))
            init.mark(v.memset(w_route0[:, E:P], 0.0))
            init.mark(v.memset(w_route1[:, E:P], 0.0))
            init.mark(v.memset(fill[:], 0.0))
            v.memset(turn_base[:], 0.0).then_inc(base_step, 1)
            init.mark(v.tensor_scalar(b_q[:], b_q[:], float(HD) ** -0.5, None, ALU.mult))
            for j in range(2):
                init.mark(v.scalar_tensor_tensor(w_out[:, j], w_out[:, j], norm_w[:, j:j + 1], mixer_row[:], ALU.mult, ALU.mult))
            init.mark(v.tensor_tensor(w_down[:], w_down[:], mlp_row[:].unsqueeze(1).to_broadcast([P, HID_TILES, D]), ALU.mult))
            dve.wait_ge(a_exp, 1)
            init.link(v.tensor_scalar(a_neg[:], a_neg[:], -1.0, None, ALU.mult))
            init.link(v.tensor_copy(w_dt[:, 0:SSM_HEADS], w_in[:, 768:768 + SSM_HEADS]))
            dve.wait_ge(prep_dma, 16 * (5 + 2 * len(PARTS)))
            dve.wait_ge(consts, N_CONSTS)
            init.wait(init.n)
            dve.wait_ge(base_step, 1)
            dve.sem_inc(prepared, 1)

            mine = Steps(dve, S.dve_step)

            def layer_norm(src, dst, nth):
                for i in range(NT):
                    last = mine.mark(v.bn_stats(st[:, i, :], src[:, i, :]))
                mine.wait(last)
                for i in range(NT):
                    last = mine.mark(v.bn_aggr(mv[:, i, :], st[:, i, :]))
                mine.wait(last)
                v.tensor_scalar(var[:], mv[:, :, 1], LN_EPS, None, ALU.add).then_inc(S.ln_var, 1)
                dve.wait_ge(S.ln_rstd, nth)
                for i in range(NT):
                    ins = v.tensor_scalar(dst[:, i, :], src[:, i, :], mv[:, i, 0:1], rstd[:, i:i + 1],
                                          ALU.subtract, ALU.mult)
                    if i % HT == HT - 1:
                        ins.then_inc(S.normed, 1)
                    else:
                        mine.mark(ins)

            def rms_apply(src, sums, var_ready, rstd_ready, done):
                dve.wait_ge(sums, NT)
                v.tensor_scalar(var[:], ss[:], 1.0 / D, RMS_EPS, ALU.mult, ALU.add).then_inc(var_ready, 1)
                dve.wait_ge(rstd_ready, 1)
                for H in range(2):
                    tl = slice(H * HT, (H + 1) * HT)
                    v.tensor_tensor(xn[:, tl, :], src[:, tl, :], per_tile(rstd[:, tl]), ALU.mult).then_inc(done, 1)

            def routing(psum_ready, shift, exp_ready, bias):
                dve.wait_ge(psum_ready, 1)
                for H in range(2):
                    tl = slice(H * HT, (H + 1) * HT)
                    src = tiles4(2 + H)[:, :, 0:E]
                    if bias is not None:
                        v.tensor_tensor(lg[:, tl, :], src, bias[:].unsqueeze(1).to_broadcast([P, HT, E]), ALU.add).then_inc(shift, 1)
                    else:
                        v.tensor_copy(lg[:, tl, :], src).then_inc(shift, 1)
                dve.wait_ge(shift, 2)
                mine.link(v.tensor_reduce(red[:], lg[:], AX.X, ALU.max))
                v.tensor_tensor(lg[:], lg[:], red[:].unsqueeze(2).to_broadcast([P, NT, E]), ALU.subtract).then_inc(shift, 1)
                dve.wait_ge(exp_ready, 1)
                mine.link(v.tensor_reduce(red[:], sc[:], AX.X, ALU.add))
                mine.link(v.reciprocal(red[:], red[:]))
                mine.link(v.tensor_tensor(lg[:], sc[:], red[:].unsqueeze(2).to_broadcast([P, NT, E]), ALU.mult))
                for i in range(NT):
                    last = mine.mark(v.max(top8[:, i, :], lg[:, i, :]))
                mine.wait(last)
                for i in range(NT):
                    last = mine.mark(v.max_index(idx8[:, i, :], top8[:, i, :], lg[:, i, :]))
                mine.wait(last)
                mine.link(v.tensor_copy(idxf[:], idx8[:]))
                for k in range(TOPK):
                    last = mine.mark(v.tensor_tensor(pick[:, k], iota_e[:].unsqueeze(1).to_broadcast([P, NT, E]),
                                                     idxf[:, :, k:k + 1].to_broadcast([P, NT, E]), ALU.is_equal))
                mine.wait(last)

            with dve.Fori(0, B) as b:
                mine.n = 0
                rms_apply(xa, S.ss1, S.rms1_var, S.rms1, S.xn1)
                for H in range(2):
                    dve.wait_ge(S.dt_psum, H + 1)
                    last = mine.mark(v.tensor_tensor(dtz[:, H * HT:(H + 1) * HT, :], tiles4(6 + H)[:, :, 0:SSM_HEADS],
                                                     dt_bias[:].unsqueeze(1).to_broadcast([P, HT, SSM_HEADS]), ALU.add))
                mine.wait(last)
                v.scalar_tensor_tensor(dts[:], dtz[:], -1.0, dtz[:], ALU.mult, ALU.max).then_inc(S.dt_abs, 1)
                dve.wait_ge(S.dt_u, 1)
                mine.link(v.tensor_scalar(dtp[:], dtu[:], 2.0, None, ALU.add))
                mine.link(v.reciprocal(dtp[:], dtp[:]))
                mine.link(v.tensor_tensor(dts[:], dtu[:], dtp[:], ALU.mult))
                mine.link(v.tensor_tensor(dts2[:], dts[:], dts[:], ALU.mult))
                mine.link(v.tensor_scalar(dtp[:], dts2[:], ATANH[-1], None, ALU.mult))
                for coef in reversed(ATANH[1:-1]):
                    mine.link(v.scalar_tensor_tensor(dtp[:], dtp[:], coef, dts2[:], ALU.add, ALU.mult))
                mine.link(v.scalar_tensor_tensor(dtp[:], dtp[:], ATANH[0], dts[:], ALU.add, ALU.mult))
                mine.link(v.tensor_scalar(dtp[:], dtp[:], 2.0, None, ALU.mult))
                mine.link(v.scalar_tensor_tensor(dt[:], dtz[:], 0.0, dtp[:], ALU.max, ALU.add))
                v.tensor_tensor(av[:], dt[:], a_neg[:].unsqueeze(1).to_broadcast([P, NT, SSM_HEADS]), ALU.mult)\
                    .then_inc(S.a_ready, 1)
                for f in range(CONV_TILES):
                    dve.wait_ge(S.tap0, f + 1)
                    if f == 2:
                        dve.wait_ge(S.ecT_psum, 1)
                        v.tensor_copy(ecT[:], bank(7)[0:NT * SSM_HEADS, 0:P]).then_inc(S.ecT_sb, 1)
                    for k in range(1, TAPS):
                        ins = v.scalar_tensor_tensor(xbc[:, f, :], raw[:, f, k:k + L], conv_w[:, f, k:k + 1],
                                                     xbc[:, f, :], ALU.mult, ALU.add)
                        if k < TAPS - 1:
                            mine.link(ins)
                        else:
                            ins.then_inc(S.conv_done, 1)

                def gate(H):
                    dve.wait_ge(S.y_psum, HT * (H + 1))
                    hs = slice(H * HALF, (H + 1) * HALF)
                    for j in range(2):
                        if H == 1 and j == 0:
                            dve.wait_ge(S.mix_psum, 1)
                        v.scalar_tensor_tensor(y1[:, j], xbc[:, j, hs], d_col[:, j:j + 1], bank(4 + j), ALU.mult, ALU.add)\
                            .then_inc(S.y_used, 1)
                    for j in range(2):
                        dve.wait_ge(S.y_used, 2 * H + j + 1)
                        v.tensor_tensor(zg[:, j, hs], zg[:, j, hs], y1[:, j], ALU.mult).then_inc(S.gated, 1)

                def mix_norm(H):
                    tl = slice(H * HT, (H + 1) * HT)
                    dve.wait_ge(S.mix_psum, H + 1)
                    v.tensor_scalar(var[:, tl], tiles4(7)[:, :, 0], 1.0 / D_INNER, 1e-5, ALU.mult, ALU.add).then_inc(S.mix_var, 1)
                    dve.wait_ge(S.mix_rstd, H + 1)
                    for i in range(HT):
                        n = H * HT + i
                        ins = v.scalar_tensor_tensor(xb[:, n, :], tiles4(6)[:, i, :], rstd[:, n:n + 1], xa[:, n, :],
                                                     ALU.mult, ALU.add)
                        if i < HT - 1:
                            mine.mark(ins)
                        else:
                            ins.then_inc(S.x1_ready, 1)

                for c in range(NT):
                    dve.wait_ge(S.tr_psum, c + 1)
                    if c >= 2:
                        dve.wait_ge(S.y_psum, c - 1)
                        dve.wait_ge(S.xw_ready, c - 1)
                    v.tensor_tensor(xdt[:, c % 2], bank(0)[:, 0:D_INNER].rearrange("p (h d) -> p h d", h=SSM_HEADS),
                                    dt[:, c].unsqueeze(2).to_broadcast([P, SSM_HEADS, SSM_DIM]), ALU.mult)\
                        .then_inc(S.xdt_ready, 1)
                    dve.wait_ge(S.g_psum, c + 1)
                    v.tensor_tensor(Gm[:, c % 2], bank(1)[:, 0:P], upto[:], ALU.mult).then_inc(S.gm_ready, 1)
                    if c == 0:
                        dve.wait_ge(S.ec_bcast, 16)
                    v.tensor_tensor(Cs[:, c % 2], xbc[:, 3, c * P:(c + 1) * P].unsqueeze(1).to_broadcast([P, SSM_HEADS, P]),
                                    ecumB[:, c], ALU.mult).then_inc(S.cs_ready, 1)
                    dve.wait_ge(S.l_ready, c + 1)
                    dve.wait_ge(S.gm_ready, c + 1)
                    v.tensor_tensor(Wm[:, c % 2], Lx[:, c % 2], Gm[:, c % 2].unsqueeze(1).to_broadcast([P, SSM_HEADS, P]),
                                    ALU.mult).then_inc(S.w_ready, 1)
                    if c < NT - 1:
                        dve.wait_ge(S.hdec_ready, c + 1)
                        dve.wait_ge(S.stu_psum, c + 1)
                        v.tensor_tensor(hst[:, (c + 1) % 2].rearrange("p h d -> p (h d)"),
                                        hdec[:].rearrange("p h d -> p (h d)"), bank(3)[:, 0:D_INNER], ALU.add)\
                            .then_inc(S.h_ready, 1)
                    if c == HT - 1:
                        gate(0)
                    if c == HT + 2:
                        mix_norm(0)
                gate(1)
                mix_norm(1)
                rms_apply(xb, S.ss3, S.rms3_var, S.rms3, S.xn3)
                for n in range(2 * HID_TILES):
                    H, f = n // HID_TILES, n % HID_TILES
                    dve.wait_ge(S.gate_silu, n + 1)
                    v.tensor_tensor(hidT[:, f, H * HALF:(H + 1) * HALF], silu_g[:, n % 2], bank(3 + 2 * (n % 2)), ALU.mult)\
                        .then_inc(S.hid_ready, 1)
                dve.wait_ge(S.res_sum, 1)
                for H in range(2):
                    dve.wait_ge(S.down_psum, H + 1)
                    tl = slice(H * HT, (H + 1) * HT)
                    v.tensor_tensor(xa[:, tl, :], xa[:, tl, :], tiles4(6 + H), ALU.add).then_inc(S.skip_sum, 1)
                dve.wait_ge(S.skip_sum, 2)
                layer_norm(xa, xb, 1)
                routing(S.route_psum, S.route_shift, S.route_exp, b_route0)
                for k in range(TOPK):
                    last = mine.mark(v.tensor_tensor(pw[:, k], pick[:, k], top8[:, :, k:k + 1].to_broadcast([P, NT, E]), ALU.mult))
                mine.wait(last)
                v.tensor_tensor(gsel[:], pw[:, 0], pw[:, 1], ALU.add).then_inc(S.gsel_ready, 1)
                dve.wait_ge(S.gsel_ready, 1)
                for i in range(0, NT, 2):
                    for k in range(E):
                        for s in range(2):
                            if k == 0:
                                dve.wait_ge(S.exp_psum, i + s + 1)
                            prev = xb[:, i + s, :] if k == 0 else eacc[:, i + s, :]
                            src = ps[:, 4 + 2 * s:6 + 2 * s, :].rearrange("p k n -> p (k n)")[:, k * D:(k + 1) * D]
                            if k > 0:
                                mine.wait(marks[s])
                            ins = v.scalar_tensor_tensor(eacc[:, i + s, :], src, gsel[:, i + s, k:k + 1], prev,
                                                         ALU.mult, ALU.add)
                            if k == 0 and s == 0:
                                marks = [0, 0]
                            if k < E - 1:
                                marks[s] = mine.mark(ins)
                            else:
                                ins.then_inc(S.exp_used, 1)
                dve.wait_ge(S.exp_used, NT)
                dve.wait_ge(S.bias_psum, 1)
                for H in range(2):
                    tl = slice(H * HT, (H + 1) * HT)
                    last = mine.mark(v.tensor_tensor(eacc[:, tl, :], eacc[:, tl, :], tiles4(2 + H), ALU.add))
                mine.wait(last)
                dve.sem_inc(S.bias_used, 1)
                layer_norm(eacc, xa, 2)
                dve.wait_ge(S.normed, 4)
                layer_norm(xa, xn, 3)
                for H in range(2):
                    dve.wait_ge(S.qk_psum, 2 + H + 1)
                    v.tensor_scalar(kf[:, H * HALF:(H + 1) * HALF], bank(4 + H), b_k[:], None, ALU.add).then_inc(S.k_ready, 1)
                for H in range(2):
                    dve.wait_ge(S.v_psum, H + 1)
                    v.tensor_tensor(vtok[:, H * HT:(H + 1) * HT, :], tiles4(6 + H), b_v[:].unsqueeze(1).to_broadcast([P, HT, D]),
                                    ALU.add).then_inc(S.v_ready, 1)
                for s in range(2):
                    dve.wait_ge(S.q_part, s + 1)
                    if s == 1:
                        dve.wait_ge(S.q_rest, 1)
                    v.tensor_tensor(qrest, qf if s == 0 else qrest, q3[:, s, :], ALU.subtract).then_inc(S.q_rest, 1)
                    dve.wait_ge(S.k_part, s + 1)
                    if s == 1:
                        dve.wait_ge(S.k_rest, 1)
                    v.tensor_tensor(krest, kf if s == 0 else krest, k3[:, s, :], ALU.subtract).then_inc(S.k_rest, 1)

                def pair_max(p, count, slot_):
                    dve.wait_ge(S.s_psum, count + 1)
                    b0 = 2 * (p % 2)
                    v.tensor_reduce(smax[:, slot_, p:p + 1], ps[:, b0:b0 + 2, :].rearrange("p k n -> p (k n)"),
                                    AX.X, ALU.max).then_inc(S.s_max, 1)

                def cut_shift(count, slot_, m):
                    dve.wait_ge(S.s_max, count)
                    v.tensor_scalar(shift16[:, 0, :], smax[:, slot_, :], -1.0, None, ALU.mult).then_inc(S.shift_hi, 1)
                    dve.wait_ge(S.shift_hi, m + 1)
                    v.scalar_tensor_tensor(shift16[:, 1, :], smax[:, slot_, :], -1.0, shift16[:, 0, :],
                                           ALU.mult, ALU.subtract).then_inc(S.shift_cut, 1)

                def evac_shift(m, first=False):
                    dve.wait_ge(S.shiftT_psum, m + 1)
                    if not first:
                        dve.wait_ge(S.shift_stored, 16 * m)
                    v.tensor_copy(shiftT[:], bank(7)[0:SHIFT_PARTS * 16, 0:P // 2].bitcast(BF16)).then_inc(S.shiftT_sb, 1)
                    dve.wait_ge(S.shiftT_sb, m + 1)
                    dve.sem_inc(S.tbank_free, 1)

                def outputs(Q, qh):
                    dve.wait_ge(S.pvT_psum, 2 * Q + qh + 1)
                    o4 = bank(7).rearrange("p (t h d) -> p t h d", t=HT, h=QUAD)
                    v.reciprocal(o_rec[:], o4[:, :, :, HD]).then_inc(S.o_recip, 1)
                    dve.wait_ge(S.o_recip, 2 * Q + qh + 1)
                    cols = bass.ds(QUAD * HD * Q, QUAD * HD) if not isinstance(Q, int) else \
                        slice(QUAD * HD * Q, QUAD * HD * (Q + 1))
                    v.tensor_tensor(o_tok[:, qh * HT:(qh + 1) * HT, cols].rearrange("p t (h d) -> p t h d", h=QUAD),
                                    o4[:, :, :, 0:HD], o_rec[:].unsqueeze(3).to_broadcast([P, HT, QUAD, HD]),
                                    ALU.mult).then_inc(S.o_ready, 1)
                    dve.wait_ge(S.o_ready, 2 * Q + qh + 1)
                    dve.sem_inc(S.tbank_free, 1)

                dve.wait_ge(S.v_ready, 2)
                dve.sem_inc(S.tbank_free, 1)
                for qh in range(2):
                    for p in range(16):
                        pair_max(p, 16 * qh + p, qh)
                    if qh == 0:
                        cut_shift(16, 0, 0)
                        evac_shift(0, True)
                    else:
                        cut_shift(32, 1, 1)

                def quad(Q, ahead):
                    for qh in range(2):
                        n = 2 * Q + qh
                        for kt in range(NT):
                            if ahead:
                                for p in (2 * kt, 2 * kt + 1):
                                    pair_max(p, 32 * Q + 32 + 16 * qh + p, qh)
                            if kt == 1 and qh == 1:
                                outputs(Q, 0)
                            if kt == 3 and (ahead or qh == 0):
                                evac_shift(n + 1)
                        if ahead:
                            cut_shift(32 * Q + 48 + 16 * qh, qh, n + 2)
                    outputs(Q, 1)

                with dve.Fori(0, NQUADS - 1) as Q:
                    quad(Q, True)
                quad(NQUADS - 1, False)
                dve.wait_ge(S.res_bias, 1)
                for H in range(2):
                    dve.wait_ge(S.proj_out, H + 1)
                    tl = slice(H * HT, (H + 1) * HT)
                    last = mine.mark(v.tensor_tensor(xa[:, tl, :], xa[:, tl, :], tiles4(2 + H), ALU.add))
                mine.wait(last)
                layer_norm(xa, xb, 4)
                routing(S.route1_psum, S.route1_shift, S.route1_exp, None)
                v.tensor_tensor(pick16[:], pick[:, 0], pick[:, 1], ALU.add).then_inc(S.pick16_ready, 1)
                dve.wait_ge(S.rank_psum, 1)
                counts = bank(5)[:, 0:NT * E].rearrange("p (t e) -> p t e", t=NT)
                ranks = bank(4)[:, 0:NT * E].rearrange("p (t e) -> p t e", t=NT)
                mine.link(v.tensor_copy(pos[:, 0, :], fill[:]))
                for i in range(1, NT):
                    mine.link(v.tensor_tensor(pos[:, i, :], pos[:, i - 1, :], counts[:, i - 1, :], ALU.add))
                mine.mark(v.tensor_tensor(fill[:], pos[:, NT - 1, :], counts[:, NT - 1, :], ALU.add))
                mine.wait(mine.n)
                mine.link(v.tensor_tensor(pos[:], pos[:], ranks, ALU.add))
                for k in range(TOPK):
                    last = mine.mark(v.tensor_tensor(pw[:, k], pick[:, k], pos[:], ALU.mult))
                mine.wait(last)
                mine.link(v.tensor_reduce(posk[:], pw[:], AX.X, ALU.add))
                mine.link(v.tensor_scalar(okk[:], posk[:], float(CAPACITY), None, ALU.is_lt))
                for k in range(TOPK):
                    last = mine.mark(v.scalar_tensor_tensor(slotf[:, k], idxf[:, :, k], float(CAPACITY), posk[:, k],
                                                            ALU.mult, ALU.add))
                last = mine.mark(v.tensor_scalar(fark[:], okk[:], -FAR, FAR, ALU.mult, ALU.add))
                mine.wait(last)
                v.tensor_tensor(slot[:], slotf[:], fark[:], ALU.add).then_inc(S.slot_ready, 1)
                for k in range(TOPK):
                    last = mine.mark(v.tensor_tensor(wgt_all[:, bass.ds(NT * b, NT), k], okk[:, k], top8[:, :, k], ALU.mult))
                mine.wait(last)
                dve.wait_ge(S.slot_ready, 1)
                dve.sem_inc(ended, 1)
                dve.wait_ge(go_on, b + 1)
            dve.sem_inc(ex_up_free, 2)
            dve.sem_inc(ex_ids_free, 2)
            dve.sem_inc(res_free, 2)
            with dve.Fori(0, E // 2) as e2:
                for s in range(2):
                    dve.wait_ge(ex_loaded[s], 48 * e2 + 48)
                    dve.wait_ge(ex_out_free, 2 * e2 + s + 1)
                    v.tensor_copy(ex_ids[:, s, :], ex_in[:, s, :, D]).then_inc(ex_ids_ready, 1)
                    dve.wait_ge(ex_ids_ready, 2 * e2 + s + 1)
                    dve.sem_inc(ex_ids_free, 1)
                    dve.wait_ge(ex_down_free, 2 * e2 + s + 1)
                    for j in range(2):
                        dve.wait_ge(ex_silu_ready, 4 * e2 + 2 * s + j + 1)
                        v.tensor_tensor(ex_hid[0:FFH, s, j], ex_silu[0:FFH, j], bank(2 + 2 * j)[0:FFH], ALU.mult)\
                            .then_inc(ex_hid_ready, 1)
                        dve.wait_ge(ex_hid_ready, 4 * e2 + 2 * s + j + 1)
                        dve.sem_inc(ex_up_free, 1)
            with dve.Fori(0, B // 2) as b2:
                for s in range(2):
                    dve.wait_ge(res_loaded[s], 16 * b2 + 16)
                    bb = 2 * b2 + s
                    v.tensor_copy(fin_w[:], wgt_all[:, bass.ds(NT * bb, NT), :]).then_inc(fin_step, 1)
                    dve.wait_ge(fin_step, FIN_STEPS * bb + 1)
                    for k in range(TOPK):
                        v.tensor_tensor(res[:, s, :, k * D:(k + 1) * D], res[:, s, :, k * D:(k + 1) * D],
                                        fin_w[:, :, k:k + 1].to_broadcast([P, NT, D]), ALU.mult).then_inc(fin_step, 1)
                    dve.wait_ge(fin_step, FIN_STEPS * bb + 3)
                    v.tensor_tensor(res[:, s, :, 0:D], res[:, s, :, 0:D], res[:, s, :, D:2 * D], ALU.add).then_inc(fin_step, 1)
                    dve.wait_ge(fin_step, FIN_STEPS * bb + 4)
                    v.tensor_tensor(fsum[:], res[:, s, :, 0:D], x3_all[:, bass.ds(NT * bb, NT), :], ALU.add).then_inc(fin_step, 1)
                    dve.wait_ge(fin_step, FIN_STEPS * bb + 5)
                    dve.sem_inc(res_free, 1)
                    for i in range(NT):
                        v.bn_stats(st[:, i, :], fsum[:, i, :]).then_inc(fin_step, 1)
                    dve.wait_ge(fin_step, FIN_STEPS * bb + 5 + NT)
                    dve.sem_inc(fence, 1)
                    for i in range(NT):
                        v.bn_aggr(mv[:, i, :], st[:, i, :]).then_inc(fin_step, 1)
                    dve.wait_ge(fin_step, FIN_STEPS * bb + 5 + 2 * NT)
                    v.tensor_scalar(var[:], mv[:, :, 1], LN_EPS, None, ALU.add).then_inc(fin_var, 1)
                    dve.wait_ge(fin_rstd, bb + 1)
                    dve.wait_ge(stored, 16 * bb + 16)
                    for i in range(NT):
                        v.tensor_scalar(fin[:, s, i, :], fsum[:, i, :], mv[:, i, 0:1], rstd[:, i:i + 1],
                                        ALU.subtract, ALU.mult).then_inc(fin_step, 1)
                    dve.wait_ge(fin_step, FIN_STEPS * bb + FIN_STEPS)
                    dve.sem_inc(fin_out, 1)


_OUT = "out"


def kernel(**inputs):
    import concourse.bacc as bacc
    from concourse.bass_utils import run_bass_kernel_spmd

    x = {k: np.asarray(v) for k, v in inputs.items()}
    query, key = position_tables()
    w_rel = x["L1_attn_w_rel"]
    swapped = np.arange(HD) ^ 1
    arrays = {
        "x": x["L0_attn_x"],
        "in_proj_wT": x["L0_attn_in_proj_w"].T, "conv_w": x["L0_attn_conv_w"],
        "conv_b": x["L0_attn_conv_b"].reshape(CONV_TILES, P).T.reshape(-1),
        "dt_bias": x["L0_attn_dt_bias"], "A_log": x["L0_attn_A_log"], "D": x["L0_attn_D"],
        "norm_w": x["L0_attn_norm_w"].reshape(2, P).T.reshape(-1), "out_proj_wT": x["L0_attn_out_proj_w"].T,
        "gate_wT": x["L0_attn_gate_w"].T, "up_wT": x["L0_attn_up_w"].T, "down_wT": x["L0_attn_down_w"].T,
        "mixer_scale": x["L0_attn_mixer_scale"], "mlp_scale": x["L0_attn_mlp_scale"],
        "expert_wT": x["L0_ffn_W"].transpose(2, 0, 1), "expert_b": x["L0_ffn_b"],
        "route0_wT": x["L0_ffn_Wg"].T, "route0_b": x["L0_ffn_bg"],
        "ln_g": x["L1_attn_ln_g"], "ln_b": x["L1_attn_ln_b"],
        "w_qkv": x["L1_attn_w_qkv"], "b_qkv": x["L1_attn_b_qkv"],
        "rel_own": w_rel.T.reshape(-1), "rel_other": w_rel[swapped].T.reshape(-1),
        "w_attn_out": x["L1_attn_w_out"], "b_attn_out": x["L1_attn_b_out"],
        "route1_w": x["L1_ffn_w_gate"], "c_fc": x["L1_ffn_c_fc"], "c_proj": x["L1_ffn_c_proj"],
        "pos_query": query, "pos_key": key,
    }
    arrays = {k: np.ascontiguousarray(a) for k, a in arrays.items()}
    nc = bacc.Bacc("TRN2", target_bir_lowering=False, num_devices=1)
    nc.disable_value_cache = True
    tensors = {k: nc.dram_tensor("in_" + k, a.shape, mybir.dt.from_np(a.dtype), kind="ExternalInput").ap()
               for k, a in arrays.items()}
    tensors[_OUT] = nc.dram_tensor(_OUT, (B, L, D), F32, kind="ExternalOutput").ap()
    build(nc, tensors)
    return run_bass_kernel_spmd(nc, [{"in_" + k: a for k, a in arrays.items()}], core_ids=[0]).results[0][_OUT]
```

```python
from contextlib import ExitStack

import numpy as np

import concourse.bass as bass
from concourse import mybir

F32 = mybir.dt.float32
BF16 = mybir.dt.bfloat16
I32 = mybir.dt.int32
U32 = mybir.dt.uint32
ALU = mybir.AluOpType
ACT = mybir.ActivationFunctionType
AX = mybir.AxisListType

P = 128
D = 128
B = 4
L = 1024
NT = L // P
HALF = L // 2
HT = NT // 2
D_INNER = 256
NSTATE = 128
SSM_HEADS = 4
SSM_DIM = D_INNER // SSM_HEADS
TAPS = 4
CONV_TILES = (D_INNER + 2 * NSTATE) // P
HIDDEN = 512
HID_TILES = HIDDEN // P
E = 8
TOPK = 2
HEADS = 16
HD = D // HEADS
QUAD = 4
HALVES = 2 * HEADS // QUAD
CAPACITY = 512
CAP_TILES = CAPACITY // P
D_GATE = 192
FFH = D_GATE // 2
PARTS = ((0, 0), (0, 1), (1, 0), (1, 1), (0, 2), (2, 0))
SCORE_ROWS = len(PARTS) * 2 * HD
SHIFT_PARTS = 2
VSTEP = HD + 1
LEAD = 6
TURN_AT, SHIFT_AT = 7, 24
OUTPUTS_AT, EVAC_SHIFT_AT = 5, 12
PROB_SETS = 4
BURST_COLS = 256
BURST_PARTS = HALF // BURST_COLS
BURSTS = NT * BURST_PARTS
BURST_AT = [8 + round(n * 28 / (BURSTS - 1)) for n in range(BURSTS)]
RMS_EPS = float(np.finfo(np.float32).eps)
LN_EPS = 1e-5
XS_SLOTS = 4
FAR = float(1 << 20)
ROW = D + 1
ATANH = [1.0 / (2 * i + 1) for i in range(9)]


def position_tables():
    div = np.exp(np.arange(0, HD, 2, dtype=np.float32) * np.float32(-np.log(10000.0) / HD)).astype(np.float64)
    angle = div[:, None] * np.arange(L)[None, :]
    query = np.zeros((HD, L))
    query[0::2], query[1::2] = np.sin(angle), np.cos(angle)
    key_direct, key_swapped = np.zeros((HD, L)), np.zeros((HD, L))
    key_direct[0::2] = key_direct[1::2] = np.cos(angle)
    key_swapped[0::2], key_swapped[1::2] = np.sin(angle), -np.sin(angle)
    rows = np.tile(np.stack([key_direct, key_swapped]), (1, HEADS, 1)).astype(np.float32)
    return query.astype(np.float32), rows


def build(nc, t):
    with ExitStack() as ctx:
        def sb(name, shape, dt=F32):
            return ctx.enter_context(nc.sbuf_tensor(name, shape, dt))

        def dram(name, shape, dt=F32):
            return nc.dram_tensor(name, shape, dt, kind="Internal").ap()

        q_parts = dram("q_parts", [3, P, L], BF16)
        k_parts = dram("k_parts", [3, P, L], BF16)
        shift_rows = dram("shift_rows", [SHIFT_PARTS * 16, P], BF16)
        expert_in = dram("expert_in", [E * CAPACITY, ROW])
        expert_out = dram("expert_out", [TOPK * B * L, D])

        ident = sb("ident", [P, P])
        ident16 = sb("ident16", [P, P], BF16)
        ones = sb("ones", [P, P])
        ones16 = sb("ones16", [P, P], BF16)
        upto = sb("upto", [P, P])
        after = sb("after", [P, P])
        before16 = sb("before16", [P, P], BF16)
        iota_e = sb("iota_e", [P, E])
        neg_half = sb("neg_half", [P, NT])
        w_in = sb("w_in", [P, 2 * D_INNER + 2 * NSTATE + SSM_HEADS])
        w_dt = sb("w_dt", [P, P])
        conv_w = sb("conv_w", [P, CONV_TILES, TAPS])
        conv_b = sb("conv_b", [P, CONV_TILES])
        dt_bias = sb("dt_bias", [P, SSM_HEADS])
        a_neg = sb("a_neg", [P, SSM_HEADS])
        d_col = sb("d_col", [P, 2])
        norm_w = sb("norm_w", [P, 2])
        w_out = sb("w_out", [P, 2, D])
        mixer_row = sb("mixer_row", [P, D])
        w_gate = sb("w_gate", [P, HIDDEN])
        w_up = sb("w_up", [P, HIDDEN])
        w_down = sb("w_down", [P, HID_TILES, D])
        mlp_row = sb("mlp_row", [P, D])
        w_exp = sb("w_exp", [P, E, D])
        b_exp = sb("b_exp", [E, D])
        pick_rows = sb("pick_rows", [3 * E, E, P], BF16)
        w_route0 = sb("w_route0", [P, P])
        b_route0 = sb("b_route0", [P, E])
        w_route1 = sb("w_route1", [P, P])
        ln_g = sb("ln_g", [P, 1])
        ln_b = sb("ln_b", [P, 1])
        w_qkv = sb("w_qkv", [P, 3 * D])
        b_q = sb("b_q", [P, 1])
        b_k = sb("b_k", [P, 1])
        b_v = sb("b_v", [P, D])
        w_proj = sb("w_proj", [P, D])
        b_proj = sb("b_proj", [P, D])
        rel_own = sb("rel_own", [P, 1])
        rel_other = sb("rel_other", [P, 1])

        AQ = sb("AQ", [SCORE_ROWS + SHIFT_PARTS, HEADS, L], BF16)
        BK = sb("BK", [SCORE_ROWS + SHIFT_PARTS, HEADS, L], BF16)
        x3_all = sb("x3_all", [P, B * NT, D])
        wgt_all = sb("wgt_all", [P, B * NT, TOPK])
        fill = sb("fill", [P, E])

        xin = sb("xin", [P, NT, D])
        xa = sb("xa", [P, NT, D])
        xb = sb("xb", [P, NT, D])
        xn = sb("xn", [P, NT, D])
        xnT = sb("xnT", [P, L])
        st = sb("st", [P, NT, 6])
        mv = sb("mv", [P, NT, 2])
        ss = sb("ss", [P, NT])
        ss_in = sb("ss_in", [P, NT])
        var_in = sb("var_in", [P, NT])
        rstd_in = sb("rstd_in", [P, NT])
        var = sb("var", [P, NT])
        rstd = sb("rstd", [P, NT])
        arena = sb("arena", [P, 15372])
        raw = arena[:, 0:CONV_TILES * (L + TAPS - 1)].rearrange("p (f n) -> p f n", f=CONV_TILES)
        xbc = arena[:, 4108:8204].rearrange("p (f n) -> p f n", f=CONV_TILES)
        zg = arena[:, 8204:10252].rearrange("p (j n) -> p j n", j=2)
        EL = arena[:, 10252:12300].rearrange("p (s k h n) -> p s k h n", s=2, k=2, h=SSM_HEADS)
        Wm = arena[:, 12300:13324].rearrange("p (s h n) -> p s h n", s=2, h=SSM_HEADS)
        Cs = arena[:, 13324:14348].rearrange("p (s h n) -> p s h n", s=2, h=SSM_HEADS)
        xdt = arena[:, 14348:14860].rearrange("p (s h n) -> p s h n", s=2, h=SSM_HEADS)
        xw = arena[:, 14860:15372].rearrange("p (s h n) -> p s h n", s=2, h=SSM_HEADS)
        y1 = arena[:, 0:1024].rearrange("p (j n) -> p j n", j=2)
        gT = arena[0:E, 1024:2048]
        g3T = arena[0:3 * E, 2048:2560].bitcast(BF16)
        xs = arena[:, 4096:4096 + XS_SLOTS * HALF].rearrange("p (s n) -> p s n", s=XS_SLOTS)
        xrow = arena[:, 12300:12300 + NT * TOPK * ROW].rearrange("p (t k d) -> p t k d", t=NT, k=TOPK)
        o_tok = xn
        hidT = arena[:, 0:4096].rearrange("p (f n) -> p f n", f=HID_TILES)
        silu_g = arena[:, 4108:5132].rearrange("p (s n) -> p s n", s=2)
        eacc = arena[:, 0:1024].rearrange("p (t d) -> p t d", t=NT)
        prob = arena[:, 4096:12288].rearrange("p (s n) -> p s n", s=PROB_SETS * QUAD)
        qf = arena[:, 8192:9216]
        kf = arena[:, 9216:10240]
        qrest = arena[:, 10240:11264]
        krest = arena[:, 11264:12288]
        q3 = arena[:, 12288:13824].bitcast(BF16).rearrange("p (s n) -> p s n", s=3)
        k3 = arena[:, 13824:15360].bitcast(BF16).rearrange("p (s n) -> p s n", s=3)
        vall = sb("vall", [P, NT, VSTEP * (HEADS - 1) + 32])
        pv_sb = arena[:, 0:HALF]
        o_rec = sb("o_rec", [P, HT, QUAD])
        smax = sb("smax", [P, 2, 16])
        shift16 = sb("shift16", [P, SHIFT_PARTS, 16], BF16)
        shiftT = sb("shiftT", [SHIFT_PARTS * 16, P], BF16)
        dtz = sb("dtz", [P, NT, SSM_HEADS])
        dtu = sb("dtu", [P, NT, SSM_HEADS])
        dts = sb("dts", [P, NT, SSM_HEADS])
        dts2 = sb("dts2", [P, NT, SSM_HEADS])
        dtp = sb("dtp", [P, NT, SSM_HEADS])
        dt = sb("dt", [P, NT, SSM_HEADS])
        av = sb("av", [P, NT, SSM_HEADS])
        decay = sb("decay", [P, 2, NT, SSM_HEADS])
        aU = sb("aU", [P, 2, SSM_HEADS, P])
        Gm = sb("Gm", [P, 2, P])
        btok = sb("btok", [P, 2, NSTATE])
        hst = sb("hst", [P, 2, SSM_HEADS, SSM_DIM])
        hdec = sb("hdec", [P, SSM_HEADS, SSM_DIM])
        lg = sb("lg", [P, NT, E])
        sc = sb("sc", [P, NT, E])
        red = sb("red", [P, NT])
        top8 = sb("top8", [P, NT, 8])
        idx8 = sb("idx8", [P, NT, 8], U32)
        idxf = sb("idxf", [P, NT, 8])
        pick = sb("pick", [P, TOPK, NT, E])
        pw = sb("pw", [P, TOPK, NT, E])
        gsel = sb("gsel", [P, NT, E])
        grest = sb("grest", [P, NT, E])
        g3 = sb("g3", [P, NT, 3, E], BF16)
        pick16 = sb("pick16", [P, NT, E], BF16)
        pos = sb("pos", [P, NT, E])
        posk = sb("posk", [P, TOPK, NT])
        okk = sb("okk", [P, TOPK, NT])
        fark = sb("fark", [P, TOPK, NT])
        slotf = sb("slotf", [P, TOPK, NT])
        slot = sb("slot", [P, TOPK, NT], U32)
        iota_i = sb("iota_i", [P, E], I32)
        ids = sb("ids", [P, NT, TOPK], I32)
        idsf = sb("idsf", [P, NT, TOPK])
        turn_base = sb("turn_base", [P, 1])
        blank = sb("blank", [P, ROW])
        place = [0]

        def carve(cols):
            place[0] += cols
            assert place[0] <= 15372
            return arena[:, place[0] - cols:place[0]]

        ex_in = carve(2 * CAP_TILES * ROW).rearrange("p (s c d) -> p s c d", s=2, c=CAP_TILES)
        cfc = carve(4 * D_GATE).rearrange("p (s n) -> p s n", s=2)
        cproj = carve(4 * D)[0:FFH].rearrange("p (s j n) -> p s j n", s=2, j=2)
        ex_xT = carve(2 * CAPACITY).rearrange("p (s n) -> p s n", s=2)
        ex_silu = carve(2 * CAPACITY).rearrange("p (s n) -> p s n", s=2)
        ex_hid = carve(4 * CAPACITY).rearrange("p (s j n) -> p s j n", s=2, j=2)
        ex_out = carve(2 * CAPACITY).rearrange("p (s c d) -> p s c d", s=2, c=CAP_TILES)
        res = carve(2 * NT * TOPK * D).rearrange("p (s t d) -> p s t d", s=2, t=NT)
        fin = carve(2 * NT * D).rearrange("p (s t d) -> p s t d", s=2, t=NT)
        fsum = carve(NT * D).rearrange("p (t d) -> p t d", t=NT)
        ex_ids = sb("ex_ids", [P, 2, CAP_TILES], U32)
        fin_w = sb("fin_w", [P, NT, TOPK])

        ps = ctx.enter_context(nc.psum_tensor("ps", [P, 8, HALF], F32))

        def sem(name):
            return ctx.enter_context(nc.semaphore(name))

        turn = {n: sem(n) for n in """
            ss1 rms1_var rms1 xn1 dt_psum dt_abs dt_u a_ready
            cum_psum decay_exp proj_psum proj_used tap0 conv_done xbc_ready z_ready
            aU_ready tr_psum xdt_ready btok_ready gm_ready seg_psum l_ready cs_ready w_ready
            y_psum stu_psum h_ready hdec_ready xw_ready y_used gated sq_ready mix_psum mix_var mix_rstd x1_ready
            ss3 rms3_var rms3 xn3 mlp_psum gate_silu hid_ready down_psum res_sum skip_sum
            ln_var ln_rstd normed route_psum route_shift route_exp
            gsel_ready g3_ready gT_psum gT_sb g3T_psum g3T_sb gate_rows xs_ready xs_used moe_psum
            xT_psum xnT_ready qk_psum v_psum q_ready k_ready q_part k_part q_rest k_rest qk_stored qk_back v_ready
            s_psum s_max shift_hi shift_cut shiftT_psum shiftT_sb shift_stored shift_back
            st_psum p_ready pv_done pv_evac pvT_psum o_recip o_ready tbank_free
            oT_psum oT_sb proj_out res_bias x3_kept route1_psum route1_shift route1_exp
            pick16_ready rank_psum slot_ready row_ids dve_step
            """.split()}
        S = type("Turn", (), turn)
        numbers = sorted(s.num for s in turn.values())
        assert numbers == list(range(numbers[0], numbers[-1] + 1))
        turn_range = range(numbers[0], numbers[-1] + 1)
        pos_loaded, pos_dma, w_loaded, consts, zero_rows, zero_filled, parts_cut, prep, a_exp, prepared, base_step, first_var = (
            sem(n) for n in ("pos_loaded pos_dma w_loaded consts zero_rows zero_filled parts_cut prep a_exp prepared "
                             "base_step first_var").split())
        ended, clearing, go_on = (sem(n) for n in "ended clearing go_on".split())
        fence = sem("fence")
        scattered, rows_out, x_loaded = sem("scattered"), sem("rows_out"), sem("x_loaded")
        ex_loaded = sem("ex_loaded0"), sem("ex_loaded1")
        ex_in_free, ex_ids_free, ex_tr, ex_xT_free, ex_xT_ready, ex_up, ex_up_free, ex_silu_ready, ex_hid_ready = (
            sem(n) for n in ("ex_in_free ex_ids_free ex_tr ex_xT_free ex_xT_ready ex_up ex_up_free ex_silu_ready "
                             "ex_hid_ready").split())
        ex_down, ex_down_free, ex_out_ready, ex_out_free, ex_ids_ready, ex_scattered, all_scattered = (
            sem(n) for n in "ex_down ex_down_free ex_out_ready ex_out_free ex_ids_ready ex_scattered all_scattered".split())
        res_loaded = sem("res_loaded0"), sem("res_loaded1")
        res_free, fin_step, fin_var, fin_rstd, fin_out, stored = (
            sem(n) for n in "res_free fin_step fin_var fin_rstd fin_out stored".split())
        N_CONSTS = 21
        FIN_STEPS = 5 + 3 * NT

        class Steps:

            def __init__(self, eng, semaphore):
                self.eng, self.sem, self.n = eng, semaphore, 0

            def mark(self, ins):
                self.n += 1
                ins.then_inc(self.sem, 1)
                return self.n

            def wait(self, n):
                self.eng.wait_ge(self.sem, n)

            def link(self, ins):
                self.wait(self.mark(ins))

        def bank(i):
            return ps[:, i, :]

        def tiles4(i):
            return ps[:, i, :].rearrange("p (t d) -> p t d", t=HT)

        def per_tile(ap):
            return ap.unsqueeze(2).to_broadcast([P, ap.shape[1], D])

        block = ctx.enter_context(nc.Block())

        def row(ap, n=P):
            return ap.rearrange("(a n) -> a n", a=1).partition_broadcast(n)

        def col(ap):
            return ap.rearrange("(p a) -> p a", a=1)

        pick_in = arena[0:3 * E, 6 * L:7 * L]
        weights = [
            (w_in[:], t["in_proj_wT"]), (w_gate[:], t["gate_wT"]), (w_up[:], t["up_wT"]),
            (w_down[:], t["down_wT"].rearrange("(f p) d -> p f d", p=P)),
            (w_out[:], t["out_proj_wT"].rearrange("(j p) d -> p j d", p=P)),
            (conv_w[:], t["conv_w"].rearrange("(f p) k -> p f k", p=P)),
            (conv_b[:], t["conv_b"].rearrange("(p f) -> p f", f=CONV_TILES)),
            (norm_w[:], t["norm_w"].rearrange("(p f) -> p f", f=2)),
            (dt_bias[:], row(t["dt_bias"])), (a_neg[:], row(t["A_log"])),
            (mixer_row[:], row(t["mixer_scale"])), (mlp_row[:], row(t["mlp_scale"])),
            (w_exp[:], t["expert_wT"]), (b_exp[:], t["expert_b"]), (pick_in, t["pick_rows"]),
            (w_route0[:, 0:E], t["route0_wT"]), (w_route1[:, 0:E], t["route1_w"]), (b_route0[:], row(t["route0_b"])),
            (ln_g[:], col(t["ln_g"])), (ln_b[:], col(t["ln_b"])),
            (w_qkv[:], t["w_qkv"]), (w_proj[:], t["w_attn_out"]),
            (b_q[:], col(t["b_qkv"][0:D])), (b_k[:], col(t["b_qkv"][D:2 * D])),
            (b_v[:], row(t["b_qkv"][2 * D:3 * D])), (b_proj[:], row(t["b_attn_out"])),
        ] + [(d_col[SSM_DIM * (h % 2):SSM_DIM * (h % 2 + 1), h // 2:h // 2 + 1], row(t["D"][h:h + 1], SSM_DIM))
             for h in range(SSM_HEADS)]
        loaded_all = 16 * len(weights)
        POS_STORED, POS_BACK = 2 * 16, (2 + 2 * len(PARTS)) * 16
        pos_tab = arena[:, 0:2 * L].rearrange("p (s n) -> p s n", s=2)
        pos_q = arena[0:HD, 2 * L:3 * L]
        pos_k = arena[:, 3 * L:4 * L]
        rest_q = arena[0:HD, 4 * L:5 * L]
        rest_k = arena[:, 5 * L:6 * L]

        @block.sync
        def _(sp):
            x_tiles = t["x"].rearrange("b (t p) d -> b p t d", p=P)
            sp.dma_start(xin[:], x_tiles[0]).then_inc(x_loaded, 16)
            for dst, src in [(pos_q, t["pos_query"]), (pos_tab, t["pos_key"].rearrange("s p n -> p s n")),
                             (rel_own[:], col(t["rel_own"])), (rel_other[:], col(t["rel_other"]))]:
                sp.dma_start(dst, src).then_inc(pos_loaded, 16)
            for dst, src in weights:
                sp.dma_start(dst, src).then_inc(w_loaded, 16)
            sp.wait_ge(parts_cut, 3)
            sp.dma_start(q_parts[:, 0:HD, :].rearrange("s p n -> p s n"), k3[0:HD]).then_inc(pos_dma, 16)
            sp.wait_ge(parts_cut, 6)
            sp.dma_start(k_parts.rearrange("s p n -> p s n"), q3).then_inc(pos_dma, 16)
            sp.wait_ge(pos_dma, POS_STORED)
            for n, (qp, kp) in enumerate(PARTS):
                lo = 2 * HD * n + HD
                sp.dma_start(AQ[lo:lo + HD, :, :], q_parts[qp, 0:HD, :].unsqueeze(1)
                             .to_broadcast([HD, HEADS, L])).then_inc(pos_dma, 16)
                sp.dma_start(BK[lo:lo + HD, :, :],
                             k_parts[kp].rearrange("(h d) n -> d h n", d=HD)).then_inc(pos_dma, 16)
            sp.wait_ge(zero_rows, 2)
            sp.dma_start(expert_in.rearrange("(p c) d -> p c d", p=P),
                         blank[:].unsqueeze(1).to_broadcast([P, E * CAPACITY // P, ROW])).then_inc(zero_filled, 16)
            for n in range(TOPK):
                sp.dma_start(expert_out[n * B * L:(n + 1) * B * L, :].rearrange("(p c) d -> p c d", p=P),
                             x3_all[:]).then_inc(zero_filled, 16)
            sp.wait_ge(pos_dma, POS_BACK)
            with sp.Fori(0, B) as b:
                sp.wait_ge(S.res_sum, 1)
                sp.dma_start(xin[:], x_tiles[b + 1]).then_inc(x_loaded, 16)
                for s in range(3):
                    sp.wait_ge(S.q_part, s + 1)
                    sp.dma_start(q_parts[s], q3[:, s, :]).then_inc(S.qk_stored, 16)
                    sp.wait_ge(S.k_part, s + 1)
                    sp.dma_start(k_parts[s], k3[:, s, :]).then_inc(S.qk_stored, 16)
                    sp.wait_ge(S.qk_stored, 32 * s + 32)
                    for n, (qp, kp) in enumerate(PARTS):
                        lo = 2 * HD * n
                        if qp == s:
                            sp.dma_start(AQ[lo:lo + HD, :, :],
                                         q_parts[qp].rearrange("(h d) n -> d h n", d=HD)).then_inc(S.qk_back, 16)
                        if kp == s:
                            sp.dma_start(BK[lo:lo + HD, :, :],
                                         k_parts[kp].rearrange("(h d) n -> d h n", d=HD)).then_inc(S.qk_back, 16)
                def shift_rows_back(n):
                    sp.wait_ge(S.shiftT_sb, n + 1)
                    sp.dma_start(shift_rows, shiftT[:]).then_inc(S.shift_stored, 16)
                    sp.wait_ge(S.shift_stored, 16 * n + 16)
                    q, qh = n // 2, n % 2
                    sp.dma_start(AQ[SCORE_ROWS:SCORE_ROWS + SHIFT_PARTS, QUAD * q:QUAD * q + QUAD, qh * HALF:(qh + 1) * HALF],
                                 shift_rows.rearrange("(s h q) n -> s h (q n)", s=SHIFT_PARTS, h=QUAD))\
                        .then_inc(S.shift_back, 16)

                for n in range(HALVES):
                    shift_rows_back(n)
                sp.wait_ge(ended, 4 * b + 4)
                sp.sem_inc(clearing, 1)
                sp.sem_clear(turn_range)
                sp.sem_inc(go_on, 1)
            sp.wait_ge(rows_out, B + 1)
            with sp.Fori(0, E // 2) as e2:
                for s in range(2):
                    sp.wait_ge(ex_in_free, 2 * e2 + s + 1)
                    sp.sem_inc(fence, 1)
                    sp.wait_ge(ex_ids_free, 2 * e2 + s + 1)
                    sp.sem_inc(fence, 1)
                    e = 2 * e2 + s
                    sp.dma_start(ex_in[:, s], expert_in[bass.ds(CAPACITY * e, CAPACITY), :]
                                 .rearrange("(c p) d -> p c d", p=P)).then_inc(ex_loaded[s], 16)
                    sp.dma_start(cfc[:, s], t["c_fc"][e]).then_inc(ex_loaded[s], 16)
                    sp.dma_start(cproj[:, s], t["c_proj"][e].rearrange("(j p) n -> p j n", p=FFH)).then_inc(ex_loaded[s], 16)
            sp.sem_inc(stored, 32)
            sp.wait_ge(all_scattered, 1)
            rows_v = expert_out.rearrange("(b t p k) d -> b p t (k d)", b=B, t=NT, k=TOPK)
            out_v = t["out"].rearrange("b (t p) d -> b p t d", p=P)
            with sp.Fori(0, B // 2) as b2:
                for s in range(2):
                    sp.wait_ge(res_free, 2 * b2 + s + 1)
                    sp.sem_inc(fence, 1)
                    sp.dma_start(res[:, s], rows_v[2 * b2 + s]).then_inc(res_loaded[s], 16)
                for s in range(2):
                    sp.wait_ge(fin_out, 2 * b2 + s + 1)
                    sp.sem_inc(fence, 1)
                    sp.dma_start(out_v[2 * b2 + s], fin[:, s]).then_inc(stored, 16)
            sp.wait_ge(stored, 16 * B + 32)

        @block.tensor
        def _(pe):
            def transposes(src, dst_bank, done, n=HT):
                for i in range(n):
                    last = nc.tensor.transpose(bank(dst_bank)[:, i * P:(i + 1) * P], src(i), ident[:])
                last.then_inc(done, 1)

            def half_transposes(src, ready, before=0):
                for H in range(2):
                    pe.wait_ge(ready, before + H + 1)
                    transposes(lambda i: src[:, H * HT + i, :], H, S.xT_psum)

            def tile(a, n):
                return a[:, n * P:(n + 1) * P]

            def mm(out, lhsT, rhs, first=True, last=True):
                return nc.tensor.matmul(out, lhsT, rhs, start=first, stop=last)

            def half(H):
                return slice(H * HALF, (H + 1) * HALF)

            def project(n):
                H, f = n // 6, n % 6
                if n == 4:
                    pe.wait_ge(S.dt_abs, 1)
                if n >= 6:
                    pe.wait_ge(S.proj_used, n - 1)
                mm(bank(2 + n if n < 6 else 6 + n % 2), tile(w_in, (f + 2) % 6), xnT[:, half(H)]).then_inc(S.proj_psum, 1)

            def in_projection():
                half_transposes(xn, S.xn1)
                for H in range(2):
                    pe.wait_ge(S.xnT_ready, H + 1)
                    for i in range(HT):
                        last = mm(tile(bank(6 + H), i), tile(xnT, H * HT + i), w_dt[:])
                    last.then_inc(S.dt_psum, 1)
                for n in range(6):
                    project(n)
                pe.wait_ge(S.a_ready, 1)
                a32 = av[:].rearrange("p c h -> p (c h)")
                for i, m in enumerate((after, ones)):
                    last = mm(bank(1)[:, 32 * i:32 * i + 32], m[:], a32)
                last.then_inc(S.cum_psum, 1)

            TRB, STUB, SEGB, YB, OUTB, SSB = 0, 1, 2, 4, 6, 7

            def chunk_front(c):
                if c % HT == 0:
                    pe.wait_ge(S.xbc_ready, CONV_TILES * (c // HT + 1))
                if c >= 1:
                    pe.wait_ge(S.xdt_ready, c)
                    pe.wait_ge(S.gm_ready, c)
                    pe.wait_ge(S.btok_ready, c)
                for i, f in enumerate((0, 1, 2)):
                    nc.tensor.transpose(tile(bank(TRB), i), tile(xbc[:, f], c), ident[:])
                mm(tile(bank(TRB), 3), tile(xbc[:, 2], c), tile(xbc[:, 3], c)).then_inc(S.tr_psum, 1)
                pe.wait_ge(S.aU_ready, c + 1)
                if c >= 1:
                    pe.wait_ge(S.l_ready, c)
                sums = aU[:, c % 2].rearrange("p h n -> p (h n)")
                mm(bank(SEGB), after[:], sums)
                mm(bank(SEGB + 1), ones[:], sums).then_inc(S.seg_psum, 1)

            def chunk_state(c):
                pe.wait_ge(S.xw_ready, c + 1)
                pe.wait_ge(S.btok_ready, c + 1)
                if c >= 1:
                    pe.wait_ge(S.h_ready, c + 1)
                mm(bank(STUB)[:, 0:D_INNER], btok[:, c % 2], xw[:, c % 2].rearrange("p h d -> p (h d)"))\
                    .then_inc(S.stu_psum, 1)

            def chunk_out(c):
                if c == 0:
                    pe.wait_ge(S.proj_used, 4)
                if c == HT:
                    pe.wait_ge(S.y_used, 2)
                pe.wait_ge(S.xdt_ready, c + 1)
                pe.wait_ge(S.w_ready, c + 1)
                pe.wait_ge(S.cs_ready, c + 1)
                pe.wait_ge(S.h_ready, c + 1)
                for h in range(SSM_HEADS):
                    lo = SSM_DIM * (h % 2)
                    out = bank(YB + h // 2)[lo:lo + SSM_DIM, (c % HT) * P:(c % HT + 1) * P]
                    mm(out, xdt[:, c % 2, h], Wm[:, c % 2, h], True, False)
                    last = mm(out, hst[:, c % 2, h], Cs[:, c % 2, h], False, True)
                last.then_inc(S.y_psum, 1)

            def mix_out(H):
                if H == 0:
                    pe.wait_ge(S.proj_used, 12)
                if H == 1:
                    pe.wait_ge(S.x1_ready, 1)
                pe.wait_ge(S.gated, 2 * H + 2)
                pe.wait_ge(S.sq_ready, 2 * H + 2)
                for i in range(HT):
                    n = H * HT + i
                    for j in range(2):
                        mm(tile(bank(OUTB), i), tile(zg[:, j], n), w_out[:, j], j == 0, j == 1)
                    for j in range(2):
                        last = mm(tile(bank(SSB), i), tile(y1[:, j], i), ones[:], j == 0, j == 1)
                last.then_inc(S.mix_psum, 1)

            def mlp():
                pe.wait_ge(S.h_ready, NT)
                pe.wait_ge(S.l_ready, NT)
                pe.wait_ge(S.gm_ready, NT)
                pe.wait_ge(S.btok_ready, NT)
                half_transposes(xn, S.xn3)
                pe.wait_ge(S.y_used, 4)
                pe.wait_ge(S.x1_ready, 2)
                n = 0
                for H in range(2):
                    pe.wait_ge(S.xnT_ready, 2 + H + 1)
                    for f in range(HID_TILES):
                        if n >= 2:
                            pe.wait_ge(S.hid_ready, n - 1)
                        g = 2 + 2 * (n % 2)
                        mm(bank(g), tile(w_gate, f), xnT[:, half(H)])
                        mm(bank(g + 1), tile(w_up, f), xnT[:, half(H)]).then_inc(S.mlp_psum, 1)
                        n += 1
                for H in range(2):
                    pe.wait_ge(S.hid_ready, HID_TILES * (H + 1))
                    for i in range(HT):
                        for f in range(HID_TILES):
                            last = mm(tile(bank(6 + H), i), tile(hidT[:, f], H * HT + i), w_down[:, f],
                                      f == 0, f == HID_TILES - 1)
                    last.then_inc(S.down_psum, 1)

            def route(w, done):
                for i in range(NT):
                    last = mm(tile(bank(2 + i // HT), i % HT), tile(xnT, i), w[:])
                last.then_inc(done, 1)

            def moe0():
                pe.wait_ge(S.xnT_ready, 2 + 2)
                half_transposes(xb, S.normed, 0)
                pe.wait_ge(S.xnT_ready, 4 + 2)
                pe.wait_ge(S.hid_ready, 2 * HID_TILES)
                route(w_route0, S.route_psum)
                pe.wait_ge(S.gsel_ready, 1)
                for n in range(NT):
                    last = nc.tensor.transpose(bank(n // HT)[0:E, (n % HT) * P:(n % HT + 1) * P], gsel[:, n, :], ident[:])
                last.then_inc(S.gT_psum, 1)
                pe.wait_ge(S.g3_ready, 3)
                for n in range(NT):
                    last = nc.tensor.transpose(bank(4)[0:3 * E, :].bitcast(BF16)[:, n * P:(n + 1) * P],
                                               g3[:, n].rearrange("p s e -> p (s e)"), ident16[:])
                last.then_inc(S.g3T_psum, 1)
                pe.wait_ge(S.skip_sum, 2)
                pe.wait_ge(S.g3T_sb, 1)

                def gate_rows(k):
                    H, e = k // E, k % E
                    if k >= 4:
                        pe.wait_ge(S.xs_ready, k - 3)
                    mm(bank(4 + k % 4), pick_rows[:, e, :], g3T[:, half(H)]).then_inc(S.gate_rows, 1)

                gate_rows(0)
                gate_rows(1)
                for k in range(2 * E):
                    H, e = k // E, k % E
                    if k == 0:
                        pe.wait_ge(S.gT_sb, 1)
                    if e == 0:
                        for i in range(HT):
                            mm(tile(bank(H), i), gT[:, (H * HT + i) * P:(H * HT + i + 1) * P], b_exp[:], i == 0, False)
                    if k + 2 < 2 * E:
                        gate_rows(k + 2)
                    pe.wait_ge(S.xs_ready, k + 1)
                    for i in range(HT):
                        last = mm(tile(bank(H), i), tile(xs[:, k % XS_SLOTS], i), w_exp[:, e, :], False,
                                  e == E - 1 and i == HT - 1)
                    last.then_inc(S.xs_used, 1)
                    if e == E - 1:
                        pe.wait_ge(S.xs_used, k + 1)
                        pe.sem_inc(S.moe_psum, 1)

            def qkv():
                half_transposes(xn, S.normed, 4)
                pe.wait_ge(S.xs_ready, 2 * E)
                for i in range(2):
                    for H in range(2):
                        if i == 0:
                            pe.wait_ge(S.xnT_ready, 6 + H + 1)
                        mm(bank(2 + 2 * i + H), tile(w_qkv, i), xnT[:, half(H)]).then_inc(S.qk_psum, 1)
                for H in range(2):
                    for i in range(HT):
                        last = mm(tile(bank(6 + H), i), tile(xnT, H * HT + i), w_qkv[:, 2 * D:3 * D])
                    last.then_inc(S.v_psum, 1)

            SB, STB, PVB, TB = 0, 4, 6, 7

            def score_matmul(pair, kh):
                n, p = pair // 16, pair % 16
                head, b0 = QUAD * (n // 2) + p // HT, SB + 2 * (p % 2)
                if kh == 0 and pair >= 2:
                    pe.wait_ge(S.s_max, pair - 1)
                q0 = (n % 2) * HALF + (p % HT) * P
                mm(bank(b0 + kh), AQ[0:SCORE_ROWS, head, q0:q0 + P], BK[0:SCORE_ROWS, head, half(kh)]).then_inc(S.s_psum, 1)

            def shift_transpose(n):
                pe.wait_ge(S.shift_cut, n + 1)
                pe.wait_ge(S.tbank_free, 1 if n == 0 else 2 * n)
                nc.tensor.transpose(bank(TB)[0:SHIFT_PARTS * 16, 0:P // 2].bitcast(BF16),
                                    shift16[:].rearrange("p s n -> p (s n)"), ident16[:])\
                    .then_inc(S.shiftT_psum, 1)

            def pv_burst(n, m):
                kt, c = m // BURST_PARTS, m % BURST_PARTS
                if m == 0 and n > 0:
                    pe.wait_ge(S.pv_evac, n)
                pe.wait_ge(S.p_ready, 32 * n + QUAD * kt + QUAD)
                for g in range(QUAD):
                    lo = VSTEP * (QUAD * (n // 2) + g)
                    cols = slice(c * BURST_COLS, (c + 1) * BURST_COLS)
                    last = mm(bank(PVB)[32 * g:32 * g + 32, cols], vall[:, kt, lo:lo + 32],
                              prob[:, QUAD * (kt % PROB_SETS) + g, cols], m == 0, m == BURSTS - 1)
                last.then_inc(S.pv_done, 1)

            def pv_transpose(n):
                pe.wait_ge(S.pv_evac, n + 1)
                pe.wait_ge(S.tbank_free, 2 * n + 3 if n < HALVES - 1 else 2 * n + 2)
                transposes(lambda i: tile(pv_sb, i), TB, S.pvT_psum)

            def attention():
                pe.wait_ge(pos_dma, POS_BACK)
                pe.wait_ge(S.qk_back, 2 * len(PARTS) * 16)
                pe.wait_ge(S.k_ready, 2)
                pe.wait_ge(S.v_ready, 2)
                for pair in range(16 + LEAD):
                    for kh in range(2):
                        score_matmul(pair, kh)
                    if pair == 16 + LEAD // 2:
                        shift_transpose(0)
                for unit in range(32 * HALVES):
                    n, u = unit // 32, unit % 32
                    kt, head = u // QUAD, QUAD * (n // 2) + u % QUAD
                    pair = 16 + LEAD + unit // 2
                    if pair < 16 * HALVES:
                        score_matmul(pair, unit % 2)
                    if u == 0:
                        pe.wait_ge(S.shift_back, 16 * n + 16)
                    if unit >= 2:
                        pe.wait_ge(S.p_ready, unit - 1)
                    mm(bank(STB + unit % 2), BK[:, head, kt * P:(kt + 1) * P], AQ[:, head, half(n % 2)]).then_inc(S.st_psum, 1)
                    for m in range(BURSTS):
                        if BURST_AT[m] == u:
                            pv_burst(n, m)
                        if BURST_AT[m] == u + 32 and n > 0:
                            pv_burst(n - 1, m)
                    if u == TURN_AT and n > 0:
                        pv_transpose(n - 1)
                    if u == SHIFT_AT and n < HALVES - 1:
                        shift_transpose(n + 1)
                for m in range(BURSTS):
                    if BURST_AT[m] >= 32:
                        pv_burst(HALVES - 1, m)
                pv_transpose(HALVES - 1)

            def attention_out():
                pe.wait_ge(S.o_ready, HALVES)
                for H in range(2):
                    transposes(lambda i: o_tok[:, H * HT + i, :], H, S.oT_psum)
                for H in range(2):
                    pe.wait_ge(S.oT_sb, H + 1)
                    for i in range(HT):
                        last = mm(tile(bank(2 + H), i), tile(xnT, H * HT + i), w_proj[:])
                    last.then_inc(S.proj_out, 1)

            def moe1_route():
                half_transposes(xb, S.normed, 6)
                pe.wait_ge(S.xnT_ready, 8 + 2)
                route(w_route1, S.route1_psum)
                pe.wait_ge(S.pick16_ready, 1)
                m = pick16[:].rearrange("p t e -> p (t e)")
                mm(bank(4)[:, 0:NT * E], before16[:], m)
                mm(bank(5)[:, 0:NT * E], ones16[:], m).then_inc(S.rank_psum, 1)

            pe.wait_ge(prepared, 1)
            pe.wait_ge(consts, N_CONSTS)
            with pe.Fori(0, B) as b:
                in_projection()
                chunk_front(0)
                for c in range(NT):
                    if c < NT - 1:
                        chunk_state(c)
                        chunk_front(c + 1)
                    for n in range(6 + 3 * c, 9 + 3 * c) if c < 2 else ():
                        project(n)
                    chunk_out(c)
                    if c == HT + 1:
                        mix_out(0)
                mix_out(1)
                mlp()
                moe0()
                qkv()
                attention()
                attention_out()
                moe1_route()
                pe.sem_inc(ended, 1)
                pe.wait_ge(go_on, b + 1)
            pe.sem_inc(ex_in_free, 2)
            with pe.Fori(0, E // 2) as e2:
                for s in range(2):
                    pe.wait_ge(ex_loaded[s], 48 * e2 + 48)
                    pe.wait_ge(ex_xT_free, 2 * e2 + s + 1)
                    for i in range(CAP_TILES):
                        last = nc.tensor.transpose(tile(bank(0), i), ex_in[:, s, i, 0:D], ident[:])
                    last.then_inc(ex_tr, 1)
                    pe.wait_ge(ex_xT_ready, 2 * e2 + s + 1)
                    pe.wait_ge(ex_up_free, 4 * e2 + 2 * s + 1)
                    for j in range(2):
                        if j == 1:
                            pe.wait_ge(ex_up_free, 4 * e2 + 2 * s + 2)
                        for k in range(2):
                            last = mm(bank(1 + 2 * j + k)[0:FFH], cfc[:, s, k * D_GATE + j * FFH:k * D_GATE + (j + 1) * FFH],
                                      ex_xT[:, s])
                        last.then_inc(ex_up, 1)
                    pe.wait_ge(ex_hid_ready, 4 * e2 + 2 * s + 2)
                    pe.wait_ge(ex_down_free, 2 * e2 + s + 1)
                    for i in range(CAP_TILES):
                        for j in range(2):
                            last = mm(tile(bank(5 + s), i), ex_hid[0:FFH, s, j, i * P:(i + 1) * P], cproj[:, s, j],
                                      j == 0, j == 1)
                    last.then_inc(ex_down, 1)
                    pe.wait_ge(ex_down, 2 * e2 + s + 1)
                    pe.sem_inc(ex_in_free, 1)

        @block.scalar
        def _(act):
            def squares(src, sums, done, junk):
                for i in range(NT):
                    nc.scalar.activation(junk[:, i, :], src[:, i, :], ACT.Square, accum_out=sums[:, i:i + 1]).then_inc(done, 1)

            def evac_T(nth, **affine):
                for H in range(2):
                    act.wait_ge(S.xT_psum, 2 * nth + H + 1)
                    func = ACT.Identity if affine else ACT.Copy
                    nc.scalar.activation(xnT[:, H * HALF:(H + 1) * HALF], bank(H), func, **affine).then_inc(S.xnT_ready, 1)

            act.wait_ge(x_loaded, 16)
            squares(xin, ss_in, a_exp, xn)
            act.wait_ge(w_loaded, loaded_all)
            nc.scalar.activation(a_neg[:], a_neg[:], ACT.Exp).then_inc(a_exp, 1)
            nc.scalar.activation(pick_rows[:].rearrange("k e n -> k (e n)"), pick_in, ACT.Copy).then_inc(a_exp, 1)
            act.wait_ge(a_exp, NT + 2)
            act.wait_ge(prepared, 1)
            act.wait_ge(consts, N_CONSTS)
            with act.Fori(0, B) as b:
                evac_T(0)
                act.wait_ge(S.dt_abs, 1)
                nc.scalar.activation(dtu[:], dts[:], ACT.Exp, scale=-1.0).then_inc(S.dt_u, 1)

                def evac_projection(n):
                    H, f = n // 6, n % 6
                    act.wait_ge(S.proj_psum, n + 1)
                    lo = H * HALF
                    if f < CONV_TILES:
                        dst = raw[:, f, TAPS - 1 + lo:TAPS - 1 + lo + HALF]
                    else:
                        dst = zg[:, f - CONV_TILES, lo:lo + HALF]
                    nc.scalar.activation(dst, bank(2 + n if n < 6 else 6 + n % 2), ACT.Silu if n in (4, 5) else ACT.Copy)\
                        .then_inc(S.proj_used, 1)

                def first_tap(H, f):
                    act.wait_ge(S.proj_used, 6 * H + f + 1)
                    nc.scalar.activation(xbc[:, f, H * HALF:(H + 1) * HALF], raw[:, f, H * HALF:(H + 1) * HALF], ACT.Identity,
                                         scale=conv_w[:, f, 0:1], bias=conv_b[:, f:f + 1]).then_inc(S.tap0, 1)

                def silu_xbc(H):
                    for f in range(CONV_TILES):
                        act.wait_ge(S.conv_done, CONV_TILES * H + f + 1)
                        own = xbc[:, f, H * HALF:(H + 1) * HALF]
                        nc.scalar.activation(own, own, ACT.Silu).then_inc(S.xbc_ready, 1)

                for n in range(CONV_TILES):
                    evac_projection(n)
                for f in range(CONV_TILES):
                    first_tap(0, f)
                act.wait_ge(S.cum_psum, 1)
                nc.scalar.activation(decay[:].rearrange("p s c h -> p (s c h)"), bank(1)[:, 0:64], ACT.Exp)\
                    .then_inc(S.decay_exp, 1)
                for n in (4, 5):
                    evac_projection(n)
                silu_xbc(0)
                for c in range(NT):
                    act.wait_ge(S.tr_psum, c + 1)
                    act.wait_ge(S.gm_ready, c + 1)
                    if c >= 2:
                        act.wait_ge(S.stu_psum, c - 1)
                    nc.scalar.activation(btok[:, c % 2], bank(0)[:, 2 * P:3 * P], ACT.Copy).then_inc(S.btok_ready, 1)
                    act.wait_ge(S.seg_psum, c + 1)
                    if c >= 2:
                        act.wait_ge(S.w_ready, c - 1)
                        act.wait_ge(S.cs_ready, c - 1)
                    nc.scalar.activation(EL[:, c % 2].rearrange("p k h n -> p (k h n)"),
                                         ps[:, 2:4, :].rearrange("p k n -> p (k n)"), ACT.Exp).then_inc(S.l_ready, 1)
                    if c < 2:
                        for n in range(6 + 3 * c, 9 + 3 * c):
                            evac_projection(n)
                        for f in range(2 * c, 2 * c + 2):
                            first_tap(1, f)
                    if c == HT - 1:
                        act.wait_ge(S.proj_used, 12)
                        for j in range(2):
                            nc.scalar.activation(zg[:, j, HALF:L], zg[:, j, HALF:L], ACT.Silu).then_inc(S.z_ready, 1)
                        silu_xbc(1)
                    if c in (HT + 1, NT - 1):
                        H = 0 if c == HT + 1 else 1
                        for j in range(2):
                            act.wait_ge(S.gated, 2 * H + j + 1)
                            nc.scalar.activation(y1[:, j], zg[:, j, H * HALF:(H + 1) * HALF], ACT.Square)\
                                .then_inc(S.sq_ready, 1)
                act.wait_ge(S.x1_ready, 2)
                squares(xb, ss, S.ss3, xn)
                evac_T(1)
                for n in range(2 * HID_TILES):
                    act.wait_ge(S.mlp_psum, n + 1)
                    if n >= 2:
                        act.wait_ge(S.hid_ready, n - 1)
                    nc.scalar.activation(silu_g[:, n % 2], bank(2 + 2 * (n % 2)), ACT.Silu).then_inc(S.gate_silu, 1)
                evac_T(2)
                act.wait_ge(S.route_shift, 3)
                nc.scalar.activation(sc[:], lg[:], ACT.Exp).then_inc(S.route_exp, 1)
                act.wait_ge(S.gT_psum, 1)
                for H in range(2):
                    last = nc.scalar.activation(gT[:, H * HALF:(H + 1) * HALF], bank(H)[0:E], ACT.Copy)
                last.then_inc(S.gT_sb, 1)
                evac_T(3, scale=ln_g[:], bias=ln_b[:])
                for H in range(2):
                    act.wait_ge(S.qk_psum, H + 1)
                    nc.scalar.activation(qf[:, H * HALF:(H + 1) * HALF], bank(2 + H), ACT.Identity,
                                         scale=float(HD) ** -0.5, bias=b_q[:]).then_inc(S.q_ready, 1)
                for s in range(3):
                    act.wait_ge(*((S.q_ready, 2) if s == 0 else (S.q_rest, s)))
                    nc.scalar.activation(q3[:, s, :], qf if s == 0 else qrest, ACT.Copy).then_inc(S.q_part, 1)
                    act.wait_ge(*((S.k_ready, 2) if s == 0 else (S.k_rest, s)))
                    nc.scalar.activation(k3[:, s, :], kf if s == 0 else krest, ACT.Copy).then_inc(S.k_part, 1)

                def evac_pv(n):
                    act.wait_ge(S.pv_done, BURSTS * (n + 1))
                    if n > 0:
                        act.wait_ge(S.pvT_psum, n)
                    nc.scalar.activation(pv_sb[:], bank(6), ACT.Copy).then_inc(S.pv_evac, 1)

                act.wait_ge(S.k_part, 3)
                act.wait_ge(x_loaded, 16 * b + 32)
                act.sem_inc(fence, 1)
                squares(xin, ss_in, S.ss1, prob[:, 0:2, :].rearrange("p s (i n) -> p (s i) n", n=P))
                act.wait_ge(S.ss1, NT)
                for unit in range(32 * HALVES):
                    act.wait_ge(S.st_psum, unit + 1)
                    step = unit // QUAD
                    if unit % QUAD == 0 and step >= PROB_SETS:
                        act.wait_ge(S.pv_done, BURST_PARTS * (step + 1 - PROB_SETS))
                    nc.scalar.activation(prob[:, QUAD * (step % PROB_SETS) + unit % QUAD, :], bank(4 + unit % 2), ACT.Exp)\
                        .then_inc(S.p_ready, 1)
                    if unit % 32 == 4 and unit > 32:
                        evac_pv(unit // 32 - 1)
                evac_pv(HALVES - 1)
                for H in range(2):
                    act.wait_ge(S.oT_psum, H + 1)
                    nc.scalar.activation(xnT[:, H * HALF:(H + 1) * HALF], bank(H), ACT.Copy).then_inc(S.oT_sb, 1)
                for H in range(2):
                    act.wait_ge(S.xT_psum, 8 + H + 1)
                    act.wait_ge(S.proj_out, 2)
                    nc.scalar.activation(xnT[:, H * HALF:(H + 1) * HALF], bank(H), ACT.Copy).then_inc(S.xnT_ready, 1)
                act.wait_ge(zero_filled, 3 * 16)
                nc.scalar.activation(x3_all[:, bass.ds(NT * b, NT), :], xb[:], ACT.Copy).then_inc(S.x3_kept, 1)
                for k in range(TOPK):
                    nc.scalar.activation(xrow[:, :, k, 0:D], xb[:], ACT.Copy).then_inc(S.x3_kept, 1)
                act.wait_ge(S.route1_shift, 3)
                nc.scalar.activation(sc[:], lg[:], ACT.Exp).then_inc(S.route1_exp, 1)
                act.wait_ge(S.route1_exp, 1)
                act.wait_ge(S.x3_kept, 3)
                act.wait_ge(S.xnT_ready, 8 + 2)
                act.sem_inc(ended, 1)
                act.wait_ge(go_on, b + 1)
            act.sem_inc(ex_xT_free, 1)
            act.sem_inc(ex_down_free, 2)
            with act.Fori(0, E // 2) as e2:
                for s in range(2):
                    act.wait_ge(ex_tr, 2 * e2 + s + 1)
                    act.wait_ge(ex_in_free, 2 * e2 + s + 1)
                    nc.scalar.activation(ex_xT[:, s], bank(0), ACT.Copy).then_inc(ex_xT_ready, 1)
                    act.wait_ge(ex_xT_ready, 2 * e2 + s + 1)
                    act.sem_inc(ex_xT_free, 1)
                    for j in range(2):
                        act.wait_ge(ex_up, 4 * e2 + 2 * s + j + 1)
                        act.wait_ge(ex_up_free, 4 * e2 + 2 * s + j + 1)
                        nc.scalar.activation(ex_silu[0:FFH, j], bank(1 + 2 * j)[0:FFH], ACT.Silu).then_inc(ex_silu_ready, 1)
                    act.wait_ge(ex_down, 2 * e2 + s + 1)
                    act.wait_ge(ex_out_free, 2 * e2 + s + 1)
                    nc.scalar.activation(ex_out[:, s].rearrange("p c d -> p (c d)"), bank(5 + s), ACT.Copy)\
                        .then_inc(ex_out_ready, 1)
                    act.wait_ge(ex_out_ready, 2 * e2 + s + 1)
                    act.sem_inc(ex_down_free, 1)

        @block.gpsimd
        def _(pool):
            g = nc.gpsimd
            pool_c = [0]

            def const(ins):
                pool_c[0] += 1
                ins.then_inc(consts, 1)

            g.memset(x3_all[:], 0.0).then_inc(zero_rows, 1)
            const(g.memset(ident[:], 0.0))
            const(g.memset(upto[:], 1.0))
            const(g.memset(after[:], 1.0))
            const(g.memset(before16[:], 1.0))
            const(g.memset(ident16[:], 0.0))
            const(g.memset(ones[:], 1.0))
            const(g.memset(ones16[:], 1.0))
            const(g.memset(neg_half[:], -0.5))
            const(g.memset(vall[:], 0.0))
            const(g.iota(iota_i[:], pattern=[[1, E]], base=0, channel_multiplier=0))
            const(g.iota(ids[:], pattern=[[P * TOPK, NT], [1, TOPK]], base=0, channel_multiplier=TOPK))
            pool.wait_ge(consts, pool_c[0])
            sel = dict(channel_multiplier=1, pattern=[[-1, P]], base=0)
            const(g.affine_select(out=ident[:], in_=ident[:], compare_op=ALU.not_equal, fill=1.0, **sel))
            const(g.affine_select(out=ident16[:], in_=ident16[:], compare_op=ALU.not_equal, fill=1.0, **sel))
            const(g.affine_select(out=after[:], in_=after[:], compare_op=ALU.is_gt, fill=0.0, **sel))
            flip = dict(channel_multiplier=-1, pattern=[[1, P]], base=0)
            const(g.affine_select(out=upto[:], in_=upto[:], compare_op=ALU.is_ge, fill=0.0, **flip))
            const(g.affine_select(out=before16[:], in_=before16[:], compare_op=ALU.is_gt, fill=0.0, **flip))
            const(g.memset(vall[:, :, 0:VSTEP * HEADS].rearrange("p t (h d) -> p t h d", h=HEADS)[:, :, :, HD:VSTEP], 1.0))
            const(g.tensor_copy(iota_e[:], iota_i[:]))
            const(g.tensor_copy(idsf[:], ids[:]))
            pool.wait_ge(first_var, 1)
            const(g.tensor_tensor(rstd_in[:], var_in[:], neg_half[:], ALU.pow))
            pool.wait_ge(consts, pool_c[0])
            const(g.memset(BK[SCORE_ROWS:SCORE_ROWS + SHIFT_PARTS, :, :], 1.0))
            assert pool_c[0] == N_CONSTS
            pool.sem_inc(rows_out, 1)
            pool.wait_ge(prepared, 1)
            pool.wait_ge(consts, N_CONSTS)

            def rsqrt(var_ap, out_ap, ready, done, need=1):
                pool.wait_ge(ready, need)
                n = var_ap.shape[1]
                g.tensor_tensor(out_ap, var_ap, neg_half[:, 0:n], ALU.pow).then_inc(done, 1)

            with pool.Fori(0, B) as b:
                g.memset(hst[:, 0], 0.0).then_inc(S.h_ready, 1)
                pool.wait_ge(S.a_ready, 1)

                def decays_so_far(c):
                    if c >= 2:
                        pool.wait_ge(S.seg_psum, c - 1)
                    g.tensor_tensor(aU[:, c % 2], upto[:].unsqueeze(1).to_broadcast([P, SSM_HEADS, P]),
                                    av[:, c].unsqueeze(2).to_broadcast([P, SSM_HEADS, P]), ALU.mult).then_inc(S.aU_ready, 1)

                decays_so_far(0)
                decays_so_far(1)
                pool.wait_ge(S.decay_exp, 1)
                for c in range(NT - 1):
                    pool.wait_ge(S.xdt_ready, c + 1)
                    if c >= 2:
                        pool.wait_ge(S.stu_psum, c - 1)
                    g.tensor_tensor(xw[:, c % 2], xdt[:, c % 2],
                                    decay[:, 0, c].unsqueeze(2).to_broadcast([P, SSM_HEADS, SSM_DIM]),
                                    ALU.mult).then_inc(S.xw_ready, 1)
                    pool.wait_ge(S.h_ready, c + 1)
                    g.tensor_tensor(hdec[:], hst[:, c % 2],
                                    decay[:, 1, c].unsqueeze(2).to_broadcast([P, SSM_HEADS, SSM_DIM]),
                                    ALU.mult).then_inc(S.hdec_ready, 1)
                    if c + 2 < NT:
                        decays_so_far(c + 2)
                rsqrt(var[:, 0:HT], rstd[:, 0:HT], S.mix_var, S.mix_rstd, 1)
                rsqrt(var[:, HT:NT], rstd[:, HT:NT], S.mix_var, S.mix_rstd, 2)
                rsqrt(var[:], rstd[:], S.rms3_var, S.rms3)
                g.tensor_tensor(xa[:], xin[:], xb[:], ALU.add).then_inc(S.res_sum, 1)
                rsqrt(var[:], rstd[:], S.ln_var, S.ln_rstd, 1)
                rsqrt(var[:], rstd[:], S.ln_var, S.ln_rstd, 2)
                rsqrt(var[:], rstd[:], S.ln_var, S.ln_rstd, 3)
                pool.wait_ge(S.normed, 6)
                g.tensor_tensor(xa[:], xa[:], b_proj[:].unsqueeze(1).to_broadcast([P, NT, D]), ALU.add).then_inc(S.res_bias, 1)

                rsqrt(var_in[:], rstd_in[:], S.rms1_var, S.rms1)
                rsqrt(var[:], rstd[:], S.ln_var, S.ln_rstd, 4)
                for k in range(TOPK):
                    g.tensor_scalar(xrow[:, :, k, D:D + 1], idsf[:, :, k:k + 1], turn_base[:, 0:1], None, ALU.add)\
                        .then_inc(S.row_ids, 1)
                pool.wait_ge(S.row_ids, TOPK)
                g.tensor_scalar(turn_base[:], turn_base[:], float(L * TOPK), None, ALU.add).then_inc(base_step, 1)
                pool.wait_ge(base_step, b + 2)
                pool.wait_ge(S.x3_kept, 3)
                pool.wait_ge(S.slot_ready, 1)
                pool.wait_ge(S.rms1, 1)
                pool.wait_ge(zero_filled, 3 * 16)
                pool.sem_inc(ended, 1)
                for i in range(NT):
                    for k in range(TOPK):
                        g.indirect_dma_start(expert_in, bass.IndirectOffsetOnAxis(ap=slot[:, k, i:i + 1], axis=0),
                                             xrow[:, i, k, :], None, bounds_check=E * CAPACITY - 1, oob_is_err=False)\
                            .then_inc(scattered, 16)
                pool.wait_ge(scattered, (16 * NT * TOPK) * b + 16 * NT * TOPK)
                pool.sem_inc(rows_out, 1)
                pool.wait_ge(go_on, b + 1)
            pool.sem_inc(ex_out_free, 2)
            with pool.Fori(0, E // 2) as e2:
                for s in range(2):
                    pool.wait_ge(ex_ids_ready, 2 * e2 + s + 1)
                    pool.wait_ge(ex_out_ready, 2 * e2 + s + 1)
                    pool.sem_inc(fence, 1)
                    for i in range(CAP_TILES):
                        g.indirect_dma_start(expert_out, bass.IndirectOffsetOnAxis(ap=ex_ids[:, s, i:i + 1], axis=0),
                                             ex_out[:, s, i, :], None, bounds_check=TOPK * B * L - 1, oob_is_err=False)\
                            .then_inc(ex_scattered, 16)
                    pool.wait_ge(ex_scattered, (2 * e2 + s + 1) * (16 * CAP_TILES))
                    pool.sem_inc(ex_out_free, 1)
            pool.wait_ge(ex_scattered, 16 * CAP_TILES * E)
            pool.sem_inc(all_scattered, 1)
            with pool.Fori(0, B // 2) as b2:
                for s in range(2):
                    pool.wait_ge(fin_var, 2 * b2 + s + 1)
                    g.tensor_tensor(rstd[:], var[:], neg_half[:], ALU.pow).then_inc(fin_rstd, 1)

        @block.vector
        def _(dve):
            v = nc.vector

            def cut(src, rest, parts, sem_):
                v.tensor_copy(parts[0], src).then_inc(sem_, 1)
                k = cut.n = cut.n + 1
                dve.wait_ge(sem_, k)
                init.link(v.tensor_tensor(rest, src, parts[0], ALU.subtract))
                v.tensor_copy(parts[1], rest).then_inc(sem_, 1)
                k = cut.n = cut.n + 1
                dve.wait_ge(sem_, k)
                init.link(v.tensor_tensor(rest, rest, parts[1], ALU.subtract))
                v.tensor_copy(parts[2], rest).then_inc(sem_, 1)
                cut.n += 1
            cut.n = 0

            init = Steps(dve, prep)
            init.link(v.memset(blank[:], 0.0))
            v.memset(blank[:, D:D + 1], FAR).then_inc(zero_rows, 1)
            dve.wait_ge(a_exp, NT)
            v.tensor_scalar(var_in[:], ss_in[:], 1.0 / D, RMS_EPS, ALU.mult, ALU.add).then_inc(first_var, 1)
            dve.wait_ge(pos_loaded, 4 * 16)
            cut(pos_q, rest_q, [k3[0:HD, s, :] for s in range(3)], parts_cut)
            init.link(v.tensor_scalar(pos_k, pos_tab[:, 0], rel_own[:], None, ALU.mult))
            init.link(v.scalar_tensor_tensor(pos_k, pos_tab[:, 1], rel_other[:], pos_k, ALU.mult, ALU.add))
            cut(pos_k, rest_k, [q3[:, s, :] for s in range(3)], parts_cut)
            dve.wait_ge(w_loaded, loaded_all)
            dve.wait_ge(a_exp, NT + 2)
            init.mark(v.memset(w_dt[:], 0.0))
            init.mark(v.memset(w_route0[:, E:P], 0.0))
            init.mark(v.memset(w_route1[:, E:P], 0.0))
            init.mark(v.memset(fill[:], 0.0))
            v.memset(turn_base[:], 0.0).then_inc(base_step, 1)
            init.mark(v.tensor_scalar(b_q[:], b_q[:], float(HD) ** -0.5, None, ALU.mult))
            for j in range(2):
                init.mark(v.scalar_tensor_tensor(w_out[:, j], w_out[:, j], norm_w[:, j:j + 1], mixer_row[:], ALU.mult, ALU.mult))
            init.mark(v.tensor_tensor(w_down[:], w_down[:], mlp_row[:].unsqueeze(1).to_broadcast([P, HID_TILES, D]), ALU.mult))
            init.link(v.tensor_scalar(a_neg[:], a_neg[:], -1.0, None, ALU.mult))
            init.link(v.tensor_copy(w_dt[:, 0:SSM_HEADS], w_in[:, 768:768 + SSM_HEADS]))
            dve.wait_ge(consts, N_CONSTS)
            init.wait(init.n)
            dve.wait_ge(base_step, 1)
            dve.sem_inc(prepared, 1)

            mine = Steps(dve, S.dve_step)

            def layer_norm(src, dst, nth):
                for i in range(NT):
                    last = mine.mark(v.bn_stats(st[:, i, :], src[:, i, :]))
                mine.wait(last)
                for i in range(NT):
                    last = mine.mark(v.bn_aggr(mv[:, i, :], st[:, i, :]))
                mine.wait(last)
                v.tensor_scalar(var[:], mv[:, :, 1], LN_EPS, None, ALU.add).then_inc(S.ln_var, 1)
                dve.wait_ge(S.ln_rstd, nth)
                for i in range(NT):
                    ins = v.tensor_scalar(dst[:, i, :], src[:, i, :], mv[:, i, 0:1], rstd[:, i:i + 1],
                                          ALU.subtract, ALU.mult)
                    if i % HT == HT - 1:
                        ins.then_inc(S.normed, 1)
                    else:
                        mine.mark(ins)

            def rms_apply(src, rstd_, done):
                for H in range(2):
                    tl = slice(H * HT, (H + 1) * HT)
                    v.tensor_tensor(xn[:, tl, :], src[:, tl, :], per_tile(rstd_[:, tl]), ALU.mult).then_inc(done, 1)

            def routing(psum_ready, shift, exp_ready, bias):
                dve.wait_ge(psum_ready, 1)
                for H in range(2):
                    tl = slice(H * HT, (H + 1) * HT)
                    src = tiles4(2 + H)[:, :, 0:E]
                    if bias is not None:
                        v.tensor_tensor(lg[:, tl, :], src, bias[:].unsqueeze(1).to_broadcast([P, HT, E]), ALU.add).then_inc(shift, 1)
                    else:
                        v.tensor_copy(lg[:, tl, :], src).then_inc(shift, 1)
                dve.wait_ge(shift, 2)
                mine.link(v.tensor_reduce(red[:], lg[:], AX.X, ALU.max))
                v.tensor_tensor(lg[:], lg[:], red[:].unsqueeze(2).to_broadcast([P, NT, E]), ALU.subtract).then_inc(shift, 1)
                dve.wait_ge(exp_ready, 1)
                mine.link(v.tensor_reduce(red[:], sc[:], AX.X, ALU.add))
                mine.link(v.reciprocal(red[:], red[:]))
                mine.link(v.tensor_tensor(lg[:], sc[:], red[:].unsqueeze(2).to_broadcast([P, NT, E]), ALU.mult))
                for i in range(NT):
                    last = mine.mark(v.max(top8[:, i, :], lg[:, i, :]))
                mine.wait(last)
                for i in range(NT):
                    last = mine.mark(v.max_index(idx8[:, i, :], top8[:, i, :], lg[:, i, :]))
                mine.wait(last)
                mine.link(v.tensor_copy(idxf[:], idx8[:]))
                for k in range(TOPK):
                    last = mine.mark(v.tensor_tensor(pick[:, k], iota_e[:].unsqueeze(1).to_broadcast([P, NT, E]),
                                                     idxf[:, :, k:k + 1].to_broadcast([P, NT, E]), ALU.is_equal))
                mine.wait(last)

            with dve.Fori(0, B) as b:
                mine.n = 0
                rms_apply(xin, rstd_in, S.xn1)
                mine.mark(v.memset(raw[:, :, 0:TAPS - 1], 0.0))
                for H in range(2):
                    dve.wait_ge(S.dt_psum, H + 1)
                    last = mine.mark(v.tensor_tensor(dtz[:, H * HT:(H + 1) * HT, :], tiles4(6 + H)[:, :, 0:SSM_HEADS],
                                                     dt_bias[:].unsqueeze(1).to_broadcast([P, HT, SSM_HEADS]), ALU.add))
                mine.wait(last)
                v.scalar_tensor_tensor(dts[:], dtz[:], -1.0, dtz[:], ALU.mult, ALU.max).then_inc(S.dt_abs, 1)
                dve.wait_ge(S.dt_u, 1)
                mine.link(v.tensor_scalar(dtp[:], dtu[:], 2.0, None, ALU.add))
                mine.link(v.reciprocal(dtp[:], dtp[:]))
                mine.link(v.tensor_tensor(dts[:], dtu[:], dtp[:], ALU.mult))
                mine.link(v.tensor_tensor(dts2[:], dts[:], dts[:], ALU.mult))
                mine.link(v.tensor_scalar(dtp[:], dts2[:], ATANH[-1], None, ALU.mult))
                for coef in reversed(ATANH[1:-1]):
                    mine.link(v.scalar_tensor_tensor(dtp[:], dtp[:], coef, dts2[:], ALU.add, ALU.mult))
                mine.link(v.scalar_tensor_tensor(dtp[:], dtp[:], ATANH[0], dts[:], ALU.add, ALU.mult))
                mine.link(v.tensor_scalar(dtp[:], dtp[:], 2.0, None, ALU.mult))
                mine.link(v.scalar_tensor_tensor(dt[:], dtz[:], 0.0, dtp[:], ALU.max, ALU.add))
                v.tensor_tensor(av[:], dt[:], a_neg[:].unsqueeze(1).to_broadcast([P, NT, SSM_HEADS]), ALU.mult)\
                    .then_inc(S.a_ready, 1)
                def convolve(H, f):
                    dve.wait_ge(S.tap0, CONV_TILES * H + f + 1)
                    lo = H * HALF
                    own = xbc[:, f, lo:lo + HALF]
                    for k in range(1, TAPS):
                        ins = v.scalar_tensor_tensor(own, raw[:, f, lo + k:lo + k + HALF], conv_w[:, f, k:k + 1], own,
                                                     ALU.mult, ALU.add)
                        if k < TAPS - 1:
                            mine.link(ins)
                        else:
                            ins.then_inc(S.conv_done, 1)

                for f in range(CONV_TILES):
                    convolve(0, f)

                def gate(H):
                    dve.wait_ge(S.y_psum, HT * (H + 1))
                    hs = slice(H * HALF, (H + 1) * HALF)
                    for j in range(2):
                        if H == 1 and j == 0:
                            dve.wait_ge(S.mix_psum, 1)
                            dve.wait_ge(S.z_ready, 2)
                        v.scalar_tensor_tensor(y1[:, j], xbc[:, j, hs], d_col[:, j:j + 1], bank(4 + j), ALU.mult, ALU.add)\
                            .then_inc(S.y_used, 1)
                    for j in range(2):
                        dve.wait_ge(S.y_used, 2 * H + j + 1)
                        v.tensor_tensor(zg[:, j, hs], zg[:, j, hs], y1[:, j], ALU.mult).then_inc(S.gated, 1)

                def mix_variance(H):
                    tl = slice(H * HT, (H + 1) * HT)
                    dve.wait_ge(S.mix_psum, H + 1)
                    v.tensor_scalar(var[:, tl], tiles4(7)[:, :, 0], 1.0 / D_INNER, 1e-5, ALU.mult, ALU.add).then_inc(S.mix_var, 1)

                def mix_norm(H):
                    dve.wait_ge(S.mix_rstd, H + 1)
                    for i in range(HT):
                        n = H * HT + i
                        ins = v.scalar_tensor_tensor(xb[:, n, :], tiles4(6)[:, i, :], rstd[:, n:n + 1], xin[:, n, :],
                                                     ALU.mult, ALU.add)
                        if i < HT - 1:
                            mine.mark(ins)
                        else:
                            ins.then_inc(S.x1_ready, 1)

                def chunk_inputs(c):
                    dve.wait_ge(S.tr_psum, c + 1)
                    if c >= 2:
                        dve.wait_ge(S.y_psum, c - 1)
                        dve.wait_ge(S.xw_ready, c - 1)
                    v.tensor_tensor(xdt[:, c % 2], bank(0)[:, 0:D_INNER].rearrange("p (h d) -> p h d", h=SSM_HEADS),
                                    dt[:, c].unsqueeze(2).to_broadcast([P, SSM_HEADS, SSM_DIM]), ALU.mult)\
                        .then_inc(S.xdt_ready, 1)
                    v.tensor_tensor(Gm[:, c % 2], bank(0)[:, 3 * P:4 * P], upto[:], ALU.mult).then_inc(S.gm_ready, 1)

                def chunk_weights(c):
                    dve.wait_ge(S.l_ready, c + 1)
                    dve.wait_ge(S.gm_ready, c + 1)
                    v.tensor_tensor(Wm[:, c % 2], EL[:, c % 2, 0], Gm[:, c % 2].unsqueeze(1).to_broadcast([P, SSM_HEADS, P]),
                                    ALU.mult).then_inc(S.w_ready, 1)
                    v.tensor_tensor(Cs[:, c % 2], xbc[:, 3, c * P:(c + 1) * P].unsqueeze(1).to_broadcast([P, SSM_HEADS, P]),
                                    EL[:, c % 2, 1], ALU.mult).then_inc(S.cs_ready, 1)

                dve.wait_ge(rows_out, b + 1)
                dve.sem_inc(fence, 1)
                dve.wait_ge(pos_dma, POS_STORED)
                chunk_inputs(0)
                chunk_weights(0)
                for c in range(NT - 1):
                    chunk_inputs(c + 1)
                    dve.wait_ge(S.hdec_ready, c + 1)
                    dve.wait_ge(S.stu_psum, c + 1)
                    v.tensor_tensor(hst[:, (c + 1) % 2].rearrange("p h d -> p (h d)"),
                                    hdec[:].rearrange("p h d -> p (h d)"), bank(1)[:, 0:D_INNER], ALU.add)\
                        .then_inc(S.h_ready, 1)
                    if c == HT:
                        gate(0)
                    for f in {0: (0, 1), 1: (2,), 2: (3,)}.get(c, ()):
                        convolve(1, f)
                    if c == HT + 2:
                        mix_variance(0)
                    chunk_weights(c + 1)
                mix_norm(0)
                gate(1)
                mix_variance(1)
                mix_norm(1)
                dve.wait_ge(S.ss3, NT)
                v.tensor_scalar(var[:], ss[:], 1.0 / D, RMS_EPS, ALU.mult, ALU.add).then_inc(S.rms3_var, 1)
                dve.wait_ge(S.rms3, 1)
                rms_apply(xb, rstd, S.xn3)
                for n in range(2 * HID_TILES):
                    H, f = n // HID_TILES, n % HID_TILES
                    dve.wait_ge(S.gate_silu, n + 1)
                    v.tensor_tensor(hidT[:, f, H * HALF:(H + 1) * HALF], silu_g[:, n % 2], bank(3 + 2 * (n % 2)), ALU.mult)\
                        .then_inc(S.hid_ready, 1)
                dve.wait_ge(S.res_sum, 1)
                for H in range(2):
                    dve.wait_ge(S.down_psum, H + 1)
                    tl = slice(H * HT, (H + 1) * HT)
                    v.tensor_tensor(xa[:, tl, :], xa[:, tl, :], tiles4(6 + H), ALU.add).then_inc(S.skip_sum, 1)
                dve.wait_ge(S.skip_sum, 2)
                layer_norm(xa, xb, 1)
                routing(S.route_psum, S.route_shift, S.route_exp, b_route0)
                for k in range(TOPK):
                    last = mine.mark(v.tensor_tensor(pw[:, k], pick[:, k], top8[:, :, k:k + 1].to_broadcast([P, NT, E]), ALU.mult))
                mine.wait(last)
                v.tensor_tensor(gsel[:], pw[:, 0], pw[:, 1], ALU.add).then_inc(S.gsel_ready, 1)
                dve.wait_ge(S.gsel_ready, 1)
                v.tensor_copy(g3[:, :, 0], gsel[:]).then_inc(S.g3_ready, 1)
                dve.wait_ge(S.g3_ready, 1)
                mine.link(v.tensor_tensor(grest[:], gsel[:], g3[:, :, 0], ALU.subtract))
                v.tensor_copy(g3[:, :, 1], grest[:]).then_inc(S.g3_ready, 1)
                dve.wait_ge(S.g3_ready, 2)
                v.tensor_tensor(g3[:, :, 2], grest[:], g3[:, :, 1], ALU.subtract).then_inc(S.g3_ready, 1)
                dve.wait_ge(S.g3T_psum, 1)
                v.tensor_copy(g3T, bank(4)[0:3 * E, :].bitcast(BF16)).then_inc(S.g3T_sb, 1)
                for k in range(2 * E):
                    H = k // E
                    dve.wait_ge(S.gate_rows, k + 1)
                    if k >= XS_SLOTS:
                        dve.wait_ge(S.xs_used, k + 1 - XS_SLOTS)
                    v.tensor_tensor(xs[:, k % XS_SLOTS], xnT[:, H * HALF:(H + 1) * HALF], bank(4 + k % 4), ALU.mult)\
                        .then_inc(S.xs_ready, 1)
                    if k in (E + 1, 2 * E - 1):
                        H = k // (2 * E - 1)
                        tl = slice(H * HT, (H + 1) * HT)
                        dve.wait_ge(S.moe_psum, H + 1)
                        last = mine.mark(v.tensor_tensor(eacc[:, tl, :], xb[:, tl, :], tiles4(H), ALU.add))
                mine.wait(last)
                layer_norm(eacc, xa, 2)
                dve.wait_ge(S.normed, 4)
                layer_norm(xa, xn, 3)
                for H in range(2):
                    dve.wait_ge(S.qk_psum, 2 + H + 1)
                    v.tensor_scalar(kf[:, H * HALF:(H + 1) * HALF], bank(4 + H), b_k[:], None, ALU.add).then_inc(S.k_ready, 1)
                for H in range(2):
                    dve.wait_ge(S.v_psum, H + 1)
                    own = vall[:, H * HT:(H + 1) * HT, 0:VSTEP * HEADS].rearrange("p t (h d) -> p t h d", h=HEADS)[:, :, :, 0:HD]
                    v.tensor_tensor(own, tiles4(6 + H).rearrange("p t (h d) -> p t h d", h=HEADS),
                                    b_v[:].rearrange("p (h d) -> p h d", h=HEADS).unsqueeze(1)
                                    .to_broadcast([P, HT, HEADS, HD]), ALU.add).then_inc(S.v_ready, 1)
                for s in range(2):
                    dve.wait_ge(S.q_part, s + 1)
                    if s == 1:
                        dve.wait_ge(S.q_rest, 1)
                    v.tensor_tensor(qrest, qf if s == 0 else qrest, q3[:, s, :], ALU.subtract).then_inc(S.q_rest, 1)
                    dve.wait_ge(S.k_part, s + 1)
                    if s == 1:
                        dve.wait_ge(S.k_rest, 1)
                    v.tensor_tensor(krest, kf if s == 0 else krest, k3[:, s, :], ALU.subtract).then_inc(S.k_rest, 1)

                def pair_max(pair):
                    n, p = pair // 16, pair % 16
                    dve.wait_ge(S.s_psum, 2 * pair + 2)
                    b0 = 2 * (p % 2)
                    v.tensor_reduce(smax[:, n % 2, p:p + 1], ps[:, b0:b0 + 2, :].rearrange("p k n -> p (k n)"),
                                    AX.X, ALU.max).then_inc(S.s_max, 1)

                def cut_shift(n):
                    dve.wait_ge(S.s_max, 16 * n + 16)
                    v.tensor_scalar(shift16[:, 0, :], smax[:, n % 2, :], -1.0, None, ALU.mult).then_inc(S.shift_hi, 1)
                    dve.wait_ge(S.shift_hi, n + 1)
                    v.scalar_tensor_tensor(shift16[:, 1, :], smax[:, n % 2, :], -1.0, shift16[:, 0, :],
                                           ALU.mult, ALU.subtract).then_inc(S.shift_cut, 1)

                def evac_shift(n):
                    dve.wait_ge(S.shiftT_psum, n + 1)
                    if n > 0:
                        dve.wait_ge(S.shift_stored, 16 * n)
                    v.tensor_copy(shiftT[:], bank(7)[0:SHIFT_PARTS * 16, 0:P // 2].bitcast(BF16)).then_inc(S.shiftT_sb, 1)
                    dve.wait_ge(S.shiftT_sb, n + 1)
                    dve.sem_inc(S.tbank_free, 1)

                def outputs(n):
                    dve.wait_ge(S.pvT_psum, n + 1)
                    o4 = bank(7).rearrange("p (t h d) -> p t h d", t=HT, h=QUAD)
                    v.reciprocal(o_rec[:], o4[:, :, :, HD]).then_inc(S.o_recip, 1)
                    dve.wait_ge(S.o_recip, n + 1)
                    q, qh = n // 2, n % 2
                    own = o_tok[:, qh * HT:(qh + 1) * HT, QUAD * HD * q:QUAD * HD * (q + 1)].rearrange("p t (h d) -> p t h d", h=QUAD)
                    v.tensor_tensor(own, o4[:, :, :, 0:HD], o_rec[:].unsqueeze(3).to_broadcast([P, HT, QUAD, HD]),
                                    ALU.mult).then_inc(S.o_ready, 1)
                    dve.wait_ge(S.o_ready, n + 1)
                    dve.sem_inc(S.tbank_free, 1)

                dve.wait_ge(S.v_ready, 2)
                dve.sem_inc(S.tbank_free, 1)
                for pair in range(16 + LEAD + 16 * HALVES):
                    if pair < 16 * HALVES:
                        pair_max(pair)
                        if pair % 16 == 15:
                            cut_shift(pair // 16)
                    if pair == 8:
                        dve.wait_ge(S.ss1, NT)
                        v.tensor_scalar(var_in[:], ss_in[:], 1.0 / D, RMS_EPS, ALU.mult, ALU.add).then_inc(S.rms1_var, 1)
                    if pair == 16 + LEAD // 2:
                        evac_shift(0)
                    if pair >= 16 + LEAD:
                        n, i = (pair - 16 - LEAD) // 16, (pair - 16 - LEAD) % 16
                        if i == OUTPUTS_AT and n > 0:
                            outputs(n - 1)
                        if i == EVAC_SHIFT_AT and n < HALVES - 1:
                            evac_shift(n + 1)
                outputs(HALVES - 1)
                dve.wait_ge(S.res_bias, 1)
                for H in range(2):
                    dve.wait_ge(S.proj_out, H + 1)
                    tl = slice(H * HT, (H + 1) * HT)
                    last = mine.mark(v.tensor_tensor(xa[:, tl, :], xa[:, tl, :], tiles4(2 + H), ALU.add))
                mine.wait(last)
                layer_norm(xa, xb, 4)
                routing(S.route1_psum, S.route1_shift, S.route1_exp, None)
                v.tensor_tensor(pick16[:], pick[:, 0], pick[:, 1], ALU.add).then_inc(S.pick16_ready, 1)
                dve.wait_ge(S.rank_psum, 1)
                counts = bank(5)[:, 0:NT * E].rearrange("p (t e) -> p t e", t=NT)
                ranks = bank(4)[:, 0:NT * E].rearrange("p (t e) -> p t e", t=NT)
                mine.link(v.tensor_copy(pos[:, 0, :], fill[:]))
                for i in range(1, NT):
                    mine.link(v.tensor_tensor(pos[:, i, :], pos[:, i - 1, :], counts[:, i - 1, :], ALU.add))
                mine.mark(v.tensor_tensor(fill[:], pos[:, NT - 1, :], counts[:, NT - 1, :], ALU.add))
                mine.wait(mine.n)
                mine.link(v.tensor_tensor(pos[:], pos[:], ranks, ALU.add))
                for k in range(TOPK):
                    last = mine.mark(v.tensor_tensor(pw[:, k], pick[:, k], pos[:], ALU.mult))
                mine.wait(last)
                mine.link(v.tensor_reduce(posk[:], pw[:], AX.X, ALU.add))
                mine.link(v.tensor_scalar(okk[:], posk[:], float(CAPACITY), None, ALU.is_lt))
                for k in range(TOPK):
                    last = mine.mark(v.scalar_tensor_tensor(slotf[:, k], idxf[:, :, k], float(CAPACITY), posk[:, k],
                                                            ALU.mult, ALU.add))
                last = mine.mark(v.tensor_scalar(fark[:], okk[:], -FAR, FAR, ALU.mult, ALU.add))
                mine.wait(last)
                v.tensor_tensor(slot[:], slotf[:], fark[:], ALU.add).then_inc(S.slot_ready, 1)
                for k in range(TOPK):
                    last = mine.mark(v.tensor_tensor(wgt_all[:, bass.ds(NT * b, NT), k], okk[:, k], top8[:, :, k], ALU.mult))
                mine.wait(last)
                dve.wait_ge(S.slot_ready, 1)
                dve.sem_inc(ended, 1)
                dve.wait_ge(go_on, b + 1)
            dve.sem_inc(ex_up_free, 2)
            dve.sem_inc(ex_ids_free, 2)
            dve.sem_inc(res_free, 2)
            with dve.Fori(0, E // 2) as e2:
                for s in range(2):
                    dve.wait_ge(ex_loaded[s], 48 * e2 + 48)
                    dve.wait_ge(ex_out_free, 2 * e2 + s + 1)
                    v.tensor_copy(ex_ids[:, s, :], ex_in[:, s, :, D]).then_inc(ex_ids_ready, 1)
                    dve.wait_ge(ex_ids_ready, 2 * e2 + s + 1)
                    dve.sem_inc(ex_ids_free, 1)
                    dve.wait_ge(ex_down_free, 2 * e2 + s + 1)
                    for j in range(2):
                        dve.wait_ge(ex_silu_ready, 4 * e2 + 2 * s + j + 1)
                        v.tensor_tensor(ex_hid[0:FFH, s, j], ex_silu[0:FFH, j], bank(2 + 2 * j)[0:FFH], ALU.mult)\
                            .then_inc(ex_hid_ready, 1)
                        dve.wait_ge(ex_hid_ready, 4 * e2 + 2 * s + j + 1)
                        dve.sem_inc(ex_up_free, 1)
            with dve.Fori(0, B // 2) as b2:
                for s in range(2):
                    dve.wait_ge(res_loaded[s], 16 * b2 + 16)
                    bb = 2 * b2 + s
                    v.tensor_copy(fin_w[:], wgt_all[:, bass.ds(NT * bb, NT), :]).then_inc(fin_step, 1)
                    dve.wait_ge(fin_step, FIN_STEPS * bb + 1)
                    for k in range(TOPK):
                        v.tensor_tensor(res[:, s, :, k * D:(k + 1) * D], res[:, s, :, k * D:(k + 1) * D],
                                        fin_w[:, :, k:k + 1].to_broadcast([P, NT, D]), ALU.mult).then_inc(fin_step, 1)
                    dve.wait_ge(fin_step, FIN_STEPS * bb + 3)
                    v.tensor_tensor(res[:, s, :, 0:D], res[:, s, :, 0:D], res[:, s, :, D:2 * D], ALU.add).then_inc(fin_step, 1)
                    dve.wait_ge(fin_step, FIN_STEPS * bb + 4)
                    v.tensor_tensor(fsum[:], res[:, s, :, 0:D], x3_all[:, bass.ds(NT * bb, NT), :], ALU.add).then_inc(fin_step, 1)
                    dve.wait_ge(fin_step, FIN_STEPS * bb + 5)
                    dve.sem_inc(res_free, 1)
                    for i in range(NT):
                        v.bn_stats(st[:, i, :], fsum[:, i, :]).then_inc(fin_step, 1)
                    dve.wait_ge(fin_step, FIN_STEPS * bb + 5 + NT)
                    dve.sem_inc(fence, 1)
                    for i in range(NT):
                        v.bn_aggr(mv[:, i, :], st[:, i, :]).then_inc(fin_step, 1)
                    dve.wait_ge(fin_step, FIN_STEPS * bb + 5 + 2 * NT)
                    v.tensor_scalar(var[:], mv[:, :, 1], LN_EPS, None, ALU.add).then_inc(fin_var, 1)
                    dve.wait_ge(fin_rstd, bb + 1)
                    dve.wait_ge(stored, 16 * bb + 16)
                    for i in range(NT):
                        v.tensor_scalar(fin[:, s, i, :], fsum[:, i, :], mv[:, i, 0:1], rstd[:, i:i + 1],
                                        ALU.subtract, ALU.mult).then_inc(fin_step, 1)
                    dve.wait_ge(fin_step, FIN_STEPS * bb + FIN_STEPS)
                    dve.sem_inc(fin_out, 1)


_OUT = "out"


def kernel(**inputs):
    import concourse.bacc as bacc
    from concourse.bass_utils import run_bass_kernel_spmd

    x = {k: np.asarray(v) for k, v in inputs.items()}
    query, key = position_tables()
    w_rel = x["L1_attn_w_rel"]
    swapped = np.arange(HD) ^ 1
    arrays = {
        "x": np.concatenate([x["L0_attn_x"], np.zeros_like(x["L0_attn_x"][:1])]),
        "in_proj_wT": x["L0_attn_in_proj_w"].T, "conv_w": x["L0_attn_conv_w"],
        "conv_b": x["L0_attn_conv_b"].reshape(CONV_TILES, P).T.reshape(-1),
        "dt_bias": x["L0_attn_dt_bias"], "A_log": x["L0_attn_A_log"], "D": x["L0_attn_D"],
        "norm_w": x["L0_attn_norm_w"].reshape(2, P).T.reshape(-1), "out_proj_wT": x["L0_attn_out_proj_w"].T,
        "gate_wT": x["L0_attn_gate_w"].T, "up_wT": x["L0_attn_up_w"].T, "down_wT": x["L0_attn_down_w"].T,
        "mixer_scale": x["L0_attn_mixer_scale"], "mlp_scale": x["L0_attn_mlp_scale"],
        "expert_wT": x["L0_ffn_W"].transpose(2, 0, 1), "expert_b": x["L0_ffn_b"],
        "route0_wT": x["L0_ffn_Wg"].T, "route0_b": x["L0_ffn_bg"],
        "ln_g": x["L1_attn_ln_g"], "ln_b": x["L1_attn_ln_b"],
        "w_qkv": x["L1_attn_w_qkv"], "b_qkv": x["L1_attn_b_qkv"],
        "rel_own": w_rel.T.reshape(-1), "rel_other": w_rel[swapped].T.reshape(-1),
        "w_attn_out": x["L1_attn_w_out"], "b_attn_out": x["L1_attn_b_out"],
        "route1_w": x["L1_ffn_w_gate"], "c_fc": x["L1_ffn_c_fc"], "c_proj": x["L1_ffn_c_proj"],
        "pick_rows": np.repeat(np.tile(np.eye(E, dtype=np.float32), (3, 1)), P, axis=1),
        "pos_query": query, "pos_key": key,
    }
    arrays = {k: np.ascontiguousarray(a) for k, a in arrays.items()}
    nc = bacc.Bacc("TRN2", target_bir_lowering=False, num_devices=1)
    nc.disable_value_cache = True
    tensors = {k: nc.dram_tensor("in_" + k, a.shape, mybir.dt.from_np(a.dtype), kind="ExternalInput").ap()
               for k, a in arrays.items()}
    tensors[_OUT] = nc.dram_tensor(_OUT, (B, L, D), F32, kind="ExternalOutput").ap()
    build(nc, tensors)
    return run_bass_kernel_spmd(nc, [{"in_" + k: a for k, a in arrays.items()}], core_ids=[0]).results[0][_OUT]
```

```python
from contextlib import ExitStack

import numpy as np

import concourse.bass as bass
from concourse import mybir

F32 = mybir.dt.float32
BF16 = mybir.dt.bfloat16
I32 = mybir.dt.int32
U32 = mybir.dt.uint32
ALU = mybir.AluOpType
ACT = mybir.ActivationFunctionType
AX = mybir.AxisListType

P = 128
D = 128
B = 4
L = 1024
NT = L // P
HALF = L // 2
HT = NT // 2
D_INNER = 256
NSTATE = 128
SSM_HEADS = 4
SSM_DIM = D_INNER // SSM_HEADS
TAPS = 4
CONV_TILES = (D_INNER + 2 * NSTATE) // P
HIDDEN = 512
HID_TILES = HIDDEN // P
E = 8
TOPK = 2
HEADS = 16
HD = D // HEADS
QUAD = 4
HALVES = 2 * HEADS // QUAD
CAPACITY = 512
CAP_TILES = CAPACITY // P
D_GATE = 192
FFH = D_GATE // 2
PARTS = ((0, 0), (0, 1), (1, 0), (1, 1), (0, 2), (2, 0))
SCORE_ROWS = len(PARTS) * 2 * HD
SHIFT_PARTS = 2
VSTEP = HD + 1
LEAD = 6
TURN_AT, SHIFT_AT = 7, 24
OUTPUTS_AT, EVAC_SHIFT_AT = 5, 12
VROW = VSTEP * (HEADS - 1) + 32
PROB_SETS = 4
BURST_COLS = 256
BURST_PARTS = HALF // BURST_COLS
BURSTS = NT * BURST_PARTS
PROJECTIONS = {0: (2, 3, 4), 1: (5,)}
ROWS_FROM = 1
ROWS_AT = (0, 3, 6, 9, 11, 13, 16)
BURST_AT = [8 + round(n * 28 / (BURSTS - 1)) for n in range(BURSTS)]
RMS_EPS = float(np.finfo(np.float32).eps)
LN_EPS = 1e-5
EX_SLOTS = 3
XS_SLOTS = 4
FAR = float(1 << 20)
ROW = D + 1
ATANH = [1.0 / (2 * i + 1) for i in range(9)]


def position_tables():
    div = np.exp(np.arange(0, HD, 2, dtype=np.float32) * np.float32(-np.log(10000.0) / HD)).astype(np.float64)
    angle = div[:, None] * np.arange(L)[None, :]
    query = np.zeros((HD, L))
    query[0::2], query[1::2] = np.sin(angle), np.cos(angle)
    key_direct, key_swapped = np.zeros((HD, L)), np.zeros((HD, L))
    key_direct[0::2] = key_direct[1::2] = np.cos(angle)
    key_swapped[0::2], key_swapped[1::2] = np.sin(angle), -np.sin(angle)
    rows = np.tile(np.stack([key_direct, key_swapped]), (1, HEADS, 1)).astype(np.float32)
    return query.astype(np.float32), rows


def build(nc, t):
    with ExitStack() as ctx:
        def sb(name, shape, dt=F32):
            return ctx.enter_context(nc.sbuf_tensor(name, shape, dt))

        def dram(name, shape, dt=F32):
            return nc.dram_tensor(name, shape, dt, kind="Internal").ap()

        q_parts = dram("q_parts", [3, P, L], BF16)
        k_parts = dram("k_parts", [3, P, L], BF16)
        shift_rows = dram("shift_rows", [SHIFT_PARTS * 16, P], BF16)
        expert_in = dram("expert_in", [E * CAPACITY, ROW])
        expert_out = dram("expert_out", [TOPK * B * L, D])

        ident = sb("ident", [P, P])
        ident16 = sb("ident16", [P, P], BF16)
        ones = sb("ones", [P, P])
        ones16 = sb("ones16", [P, P], BF16)
        upto = sb("upto", [P, P])
        after = sb("after", [P, P])
        before16 = sb("before16", [P, P], BF16)
        iota_e = sb("iota_e", [P, E])
        neg_half = sb("neg_half", [P, NT])
        eps_sum = sb("eps_sum", [P, NT])
        w_in = sb("w_in", [P, 2 * D_INNER + 2 * NSTATE + SSM_HEADS])
        w_dt = sb("w_dt", [P, P])
        conv_w = sb("conv_w", [P, CONV_TILES, TAPS])
        conv_b = sb("conv_b", [P, CONV_TILES])
        dt_bias = sb("dt_bias", [P, SSM_HEADS])
        a_neg = sb("a_neg", [P, SSM_HEADS])
        d_col = sb("d_col", [P, 2])
        norm_w = sb("norm_w", [P, 2])
        w_out = sb("w_out", [P, 2, D])
        mixer_row = sb("mixer_row", [P, D])
        w_gate = sb("w_gate", [P, HIDDEN])
        w_up = sb("w_up", [P, HIDDEN])
        w_down = sb("w_down", [P, HID_TILES, D])
        mlp_row = sb("mlp_row", [P, D])
        w_exp = sb("w_exp", [P, E, D])
        b_exp = sb("b_exp", [E, D])
        pick_rows = sb("pick_rows", [3 * E, E, P], BF16)
        w_route0 = sb("w_route0", [P, P])
        b_route0 = sb("b_route0", [P, E])
        w_route1 = sb("w_route1", [P, P])
        ln_g = sb("ln_g", [P, 1])
        ln_b = sb("ln_b", [P, 1])
        w_qkv = sb("w_qkv", [P, 3 * D])
        b_q = sb("b_q", [P, 1])
        b_k = sb("b_k", [P, 1])
        b_v = sb("b_v", [P, D])
        w_proj = sb("w_proj", [P, D])
        b_proj = sb("b_proj", [P, D])
        rel_own = sb("rel_own", [P, 1])
        rel_other = sb("rel_other", [P, 1])

        AQ = sb("AQ", [SCORE_ROWS + SHIFT_PARTS, HEADS, L], BF16)
        BK = sb("BK", [SCORE_ROWS + SHIFT_PARTS, HEADS, L], BF16)
        x3_all = sb("x3_all", [P, B * NT, D])
        wgt_all = sb("wgt_all", [P, (B + 1) * NT, TOPK])
        fill = sb("fill", [P, E])

        xin = sb("xin", [P, NT, D])
        work = sb("work", [P, NT * TOPK * ROW])
        xa = work[:, 0:NT * D].rearrange("p (t d) -> p t d", t=NT)
        xb = sb("xb", [P, NT, D])
        xn = work[:, NT * D:2 * NT * D].rearrange("p (t d) -> p t d", t=NT)
        xrow = work[:].rearrange("p (t k d) -> p t k d", t=NT, k=TOPK)
        xnT = sb("xnT", [P, L])
        xinT = sb("xinT", [P, L])
        st = sb("st", [P, NT, 6])
        mv = sb("mv", [P, NT, 2])
        ss = sb("ss", [P, NT])
        ss_in = sb("ss_in", [P, NT])
        rstd_in = sb("rstd_in", [P, NT])
        var = sb("var", [P, NT])
        rstd = sb("rstd", [P, NT])
        rstd3 = sb("rstd3", [P, NT])
        arena = sb("arena", [P, 15372])
        raw = arena[:, 0:CONV_TILES * (L + TAPS - 1)].rearrange("p (f n) -> p f n", f=CONV_TILES)
        xbc = arena[:, 4108:8204].rearrange("p (f n) -> p f n", f=CONV_TILES)
        zg = arena[:, 8204:10252].rearrange("p (j n) -> p j n", j=2)
        EL = arena[:, 10252:12300].rearrange("p (s k h n) -> p s k h n", s=2, k=2, h=SSM_HEADS)
        Wm = arena[:, 12300:13324].rearrange("p (s h n) -> p s h n", s=2, h=SSM_HEADS)
        Cs = arena[:, 13324:14348].rearrange("p (s h n) -> p s h n", s=2, h=SSM_HEADS)
        xdt = arena[:, 14348:14860].rearrange("p (s h n) -> p s h n", s=2, h=SSM_HEADS)
        xw = arena[:, 14860:15372].rearrange("p (s h n) -> p s h n", s=2, h=SSM_HEADS)
        y1 = arena[:, 0:1024].rearrange("p (j n) -> p j n", j=2)
        xin_n = arena[:, 2400:3424].rearrange("p (t d) -> p t d", t=NT)
        gT = arena[0:E, 1024:2048]
        g3T = arena[0:3 * E, 2048:2560].bitcast(BF16)
        xs = arena[:, 4096:4096 + XS_SLOTS * HALF].rearrange("p (s n) -> p s n", s=XS_SLOTS)
        o_tok = xn
        hidT = arena[:, 0:4096].rearrange("p (f n) -> p f n", f=HID_TILES)
        silu_g = arena[:, 4108:5132].rearrange("p (s n) -> p s n", s=2)
        eacc = arena[:, 0:1024].rearrange("p (t d) -> p t d", t=NT)
        prob = arena[:, 4096:12288].rearrange("p (s n) -> p s n", s=PROB_SETS * QUAD)
        qf = arena[:, 8192:9216]
        kf = arena[:, 9216:10240]
        qrest = arena[:, 10240:11264]
        krest = arena[:, 11264:12288]
        q3 = arena[:, 12288:13824].bitcast(BF16).rearrange("p (s n) -> p s n", s=3)
        k3 = arena[:, 13824:15360].bitcast(BF16).rearrange("p (s n) -> p s n", s=3)
        vall = arena[:, 1024:1024 + NT * VROW].rearrange("p (t n) -> p t n", t=NT)
        pv_sb = arena[:, 0:HALF]
        o_rec = sb("o_rec", [P, HT, QUAD])
        smax = sb("smax", [P, 2, 16])
        shift16 = sb("shift16", [P, SHIFT_PARTS, 16], BF16)
        shiftT = sb("shiftT", [SHIFT_PARTS * 16, P], BF16)
        dtz = sb("dtz", [P, NT, SSM_HEADS])
        dtu = sb("dtu", [P, NT, SSM_HEADS])
        dts = sb("dts", [P, NT, SSM_HEADS])
        dts2 = sb("dts2", [P, NT, SSM_HEADS])
        dtp = sb("dtp", [P, NT, SSM_HEADS])
        dt = sb("dt", [P, NT, SSM_HEADS])
        av = sb("av", [P, NT, SSM_HEADS])
        decay = sb("decay", [P, 2, NT, SSM_HEADS])
        aU = sb("aU", [P, 2, SSM_HEADS, P])
        Gm = sb("Gm", [P, 2, P])
        btok = sb("btok", [P, 2, NSTATE])
        hst = sb("hst", [P, 2, SSM_HEADS, SSM_DIM])
        hdec = sb("hdec", [P, SSM_HEADS, SSM_DIM])
        lg = sb("lg", [P, NT, E])
        sc = sb("sc", [P, NT, E])
        red = sb("red", [P, NT])
        top8 = sb("top8", [P, NT, 8])
        idx8 = sb("idx8", [P, NT, 8], U32)
        idxf = sb("idxf", [P, NT, 8])
        pick = sb("pick", [P, TOPK, NT, E])
        pw = sb("pw", [P, TOPK, NT, E])
        gsel = sb("gsel", [P, NT, E])
        grest = sb("grest", [P, NT, E])
        g3 = sb("g3", [P, NT, 3, E], BF16)
        pick16 = sb("pick16", [P, NT, E], BF16)
        pos = sb("pos", [P, NT, E])
        ranks = sb("ranks", [P, NT, E])
        counts = sb("counts", [P, NT, E])
        posk = sb("posk", [P, TOPK, NT])
        okk = sb("okk", [P, TOPK, NT])
        fark = sb("fark", [P, TOPK, NT])
        slotf = sb("slotf", [P, TOPK, NT])
        slot = sb("slot", [P, TOPK, NT], U32)
        iota_i = sb("iota_i", [P, E], I32)
        ids = sb("ids", [P, NT, TOPK], I32)
        idsf = sb("idsf", [P, NT, TOPK])
        turn_base = sb("turn_base", [P, 1])
        blank = sb("blank", [P, ROW])
        place = [0]

        def carve(cols):
            place[0] += cols
            assert place[0] <= 15372
            return arena[:, place[0] - cols:place[0]]

        ex_in = carve(EX_SLOTS * CAP_TILES * ROW).rearrange("p (s c d) -> p s c d", s=EX_SLOTS, c=CAP_TILES)
        cfc = carve(EX_SLOTS * 2 * D_GATE).rearrange("p (s n) -> p s n", s=EX_SLOTS)
        cproj = carve(EX_SLOTS * 2 * D)[0:FFH].rearrange("p (s j n) -> p s j n", s=EX_SLOTS, j=2)
        ex_xT = carve(2 * CAPACITY).rearrange("p (s n) -> p s n", s=2)
        ex_silu = carve(2 * CAPACITY).rearrange("p (s n) -> p s n", s=2)
        ex_hid = carve(4 * CAPACITY).rearrange("p (s j n) -> p s j n", s=2, j=2)
        ex_out = carve(2 * CAPACITY).rearrange("p (s c d) -> p s c d", s=2, c=CAP_TILES)
        place[0] = 0
        res = carve(B * NT * TOPK * D).rearrange("p (b t d) -> p b t d", b=B, t=NT)
        fin = carve(B * NT * D).rearrange("p (b t d) -> p b t d", b=B, t=NT)
        fin_mv = carve(4 * NT).rearrange("p (s t k) -> p s t k", s=2, t=NT)
        fin_var = carve(2 * NT).rearrange("p (s t) -> p s t", s=2)
        fin_rstd = carve(2 * NT).rearrange("p (s t) -> p s t", s=2)
        fin_shift = carve(2 * NT).rearrange("p (s t) -> p s t", s=2)
        ex_ids = sb("ex_ids", [P, 2, CAP_TILES], U32)

        ps = ctx.enter_context(nc.psum_tensor("ps", [P, 8, HALF], F32))

        def sem(name):
            return ctx.enter_context(nc.semaphore(name))

        turn = {n: sem(n) for n in """
            ss1 in_norm in_T_psum in_T dt_psum dt_abs dt_u a_ready cum_psum decay_exp first_psum first_used first_tap first_conv first_silu first_aU ranked
            headers proj_psum proj_used tap0 conv_done xbc_ready z_ready
            aU_ready tr_psum xdt_ready btok_ready gm_ready seg_psum l_ready cs_ready w_ready
            y_psum stu_psum h_ready hdec_ready xw_ready y_used gated sq_ready mix_psum x1_ready
            ss3 xn3 var_ready rstd_ready eps_added mlp_psum gate_silu hid_ready down_psum res_sum skip_sum
            normed route_psum route_shift route_exp
            gsel_ready g3_ready gT_psum gT_sb g3T_psum g3T_sb gate_rows xs_ready xs_used moe_psum
            xT_psum xnT_ready qk_psum v_psum q_ready k_ready q_part k_part q_rest k_rest v_ones stored0 stored1 stored2 qk_back v_ready
            s_psum s_max shift_hi shift_cut shiftT_psum shiftT_sb shift_stored shift_back
            st_psum p_ready pv_done pv_evac pvT_psum o_recip o_ready tbank_free
            oT_psum oT_sb proj_out res_bias x3_kept route1_psum route1_shift route1_exp
            pick16_ready rank_psum slot_ready row_ids dve_step
            """.split()}
        S = type("Turn", (), turn)
        numbers = sorted(s.num for s in turn.values())
        assert numbers == list(range(numbers[0], numbers[-1] + 1))
        turn_range = range(numbers[0], numbers[-1] + 1)
        pos_loaded, pos_dma, w_loaded, consts, zero_rows, zero_filled, parts_cut, prep, a_exp, prepared, base_step = (
            sem(n) for n in ("pos_loaded pos_dma w_loaded consts zero_rows zero_filled parts_cut prep a_exp prepared "
                             "base_step").split())
        ended, clearing, go_on = (sem(n) for n in "ended clearing go_on".split())
        fence = sem("fence")
        scattered, rows_out, x_loaded = sem("scattered"), sem("rows_out"), sem("x_loaded")
        ex_loaded = [sem(f"ex_loaded{s}") for s in range(EX_SLOTS)]
        ex_tr, ex_xT_ready, ex_up, ex_silu_ready, ex_hid_ready, ex_down, ex_out_ready, ex_ids_ready, all_scattered = (
            sem(n) for n in "ex_tr ex_xT_ready ex_up ex_silu_ready ex_hid_ready ex_down ex_out_ready ex_ids_ready "
                            "all_scattered".split())
        ex_scattered = sem("ex_scattered0"), sem("ex_scattered1")
        res_loaded = [sem(f"res_loaded{b}") for b in range(B)]
        stored = sem("stored")
        fin_step, fin_weighed, fin_summed, fin_var_ready, fin_rstd_ready, fin_shift_ready, fin_out = (
            sem(n) for n in "fin_step fin_weighed fin_summed fin_var_ready fin_rstd_ready fin_shift_ready fin_out".split())
        N_CONSTS = 21

        class Steps:

            def __init__(self, eng, semaphore):
                self.eng, self.sem, self.n = eng, semaphore, 0

            def mark(self, ins):
                self.n += 1
                ins.then_inc(self.sem, 1)
                return self.n

            def wait(self, n):
                self.eng.wait_ge(self.sem, n)

            def link(self, ins):
                self.wait(self.mark(ins))

        def bank(i):
            return ps[:, i, :]

        def tiles4(i):
            return ps[:, i, :].rearrange("p (t d) -> p t d", t=HT)

        def per_tile(ap):
            return ap.unsqueeze(2).to_broadcast([P, ap.shape[1], D])

        block = ctx.enter_context(nc.Block())

        def row(ap, n=P):
            return ap.rearrange("(a n) -> a n", a=1).partition_broadcast(n)

        def col(ap):
            return ap.rearrange("(p a) -> p a", a=1)

        pick_in = arena[0:3 * E, 6 * L:7 * L]
        weights = [
            (w_in[:], t["in_proj_wT"]), (w_gate[:], t["gate_wT"]), (w_up[:], t["up_wT"]),
            (w_down[:], t["down_wT"].rearrange("(f p) d -> p f d", p=P)),
            (w_out[:], t["out_proj_wT"].rearrange("(j p) d -> p j d", p=P)),
            (conv_w[:], t["conv_w"].rearrange("(f p) k -> p f k", p=P)),
            (conv_b[:], t["conv_b"].rearrange("(p f) -> p f", f=CONV_TILES)),
            (norm_w[:], t["norm_w"].rearrange("(p f) -> p f", f=2)),
            (dt_bias[:], row(t["dt_bias"])), (a_neg[:], row(t["A_log"])),
            (mixer_row[:], row(t["mixer_scale"])), (mlp_row[:], row(t["mlp_scale"])),
            (w_exp[:], t["expert_wT"]), (b_exp[:], t["expert_b"]), (pick_in, t["pick_rows"]),
            (w_route0[:, 0:E], t["route0_wT"]), (w_route1[:, 0:E], t["route1_w"]), (b_route0[:], row(t["route0_b"])),
            (ln_g[:], col(t["ln_g"])), (ln_b[:], col(t["ln_b"])),
            (w_qkv[:], t["w_qkv"]), (w_proj[:], t["w_attn_out"]),
            (b_q[:], col(t["b_qkv"][0:D])), (b_k[:], col(t["b_qkv"][D:2 * D])),
            (b_v[:], row(t["b_qkv"][2 * D:3 * D])), (b_proj[:], row(t["b_attn_out"])),
        ] + [(d_col[SSM_DIM * (h % 2):SSM_DIM * (h % 2 + 1), h // 2:h // 2 + 1], row(t["D"][h:h + 1], SSM_DIM))
             for h in range(SSM_HEADS)]
        loaded_all = 16 * len(weights)
        POS_STORED, POS_BACK = 2 * 16, (2 + 2 * len(PARTS)) * 16
        pos_tab = arena[:, 0:2 * L].rearrange("p (s n) -> p s n", s=2)
        pos_q = arena[0:HD, 2 * L:3 * L]
        pos_k = arena[:, 3 * L:4 * L]
        rest_q = arena[0:HD, 4 * L:5 * L]
        rest_k = arena[:, 5 * L:6 * L]

        @block.sync
        def _(sp):
            x_tiles = t["x"].rearrange("b (t p) d -> b p t d", p=P)
            sp.dma_start(xin[:], x_tiles[0]).then_inc(x_loaded, 16)
            for dst, src in [(pos_q, t["pos_query"]), (pos_tab, t["pos_key"].rearrange("s p n -> p s n")),
                             (rel_own[:], col(t["rel_own"])), (rel_other[:], col(t["rel_other"]))]:
                sp.dma_start(dst, src).then_inc(pos_loaded, 16)
            for dst, src in weights:
                sp.dma_start(dst, src).then_inc(w_loaded, 16)
            sp.wait_ge(parts_cut, 3)
            sp.dma_start(q_parts[:, 0:HD, :].rearrange("s p n -> p s n"), k3[0:HD]).then_inc(pos_dma, 16)
            sp.wait_ge(parts_cut, 6)
            sp.dma_start(k_parts.rearrange("s p n -> p s n"), q3).then_inc(pos_dma, 16)
            sp.wait_ge(pos_dma, POS_STORED)
            for n, (qp, kp) in enumerate(PARTS):
                lo = 2 * HD * n + HD
                sp.dma_start(AQ[lo:lo + HD, :, :], q_parts[qp, 0:HD, :].unsqueeze(1)
                             .to_broadcast([HD, HEADS, L])).then_inc(pos_dma, 16)
                sp.dma_start(BK[lo:lo + HD, :, :],
                             k_parts[kp].rearrange("(h d) n -> d h n", d=HD)).then_inc(pos_dma, 16)
            sp.wait_ge(zero_rows, 2)
            sp.dma_start(expert_in.rearrange("(p c) d -> p c d", p=P),
                         blank[:].unsqueeze(1).to_broadcast([P, E * CAPACITY // P, ROW])).then_inc(zero_filled, 16)
            for n in range(TOPK):
                sp.dma_start(expert_out[n * B * L:(n + 1) * B * L, :].rearrange("(p c) d -> p c d", p=P),
                             x3_all[:]).then_inc(zero_filled, 16)
            sp.wait_ge(pos_dma, POS_BACK)

            def clear_turn(before):
                sp.wait_ge(ended, before + 4)
                sp.sem_inc(clearing, 1)
                sp.sem_clear(turn_range)
                sp.sem_inc(go_on, 1)

            clear_turn(0)
            with sp.Fori(0, B) as b:
                sp.wait_ge(S.res_sum, 1)
                sp.dma_start(xin[:], x_tiles[b + 1]).then_inc(x_loaded, 16)
                def store_parts(s):
                    sp.wait_ge(S.q_part, s + 1)
                    sp.dma_start(q_parts[s], q3[:, s, :]).then_inc(stored_parts[s], 16)
                    sp.wait_ge(S.k_part, s + 1)
                    sp.dma_start(k_parts[s], k3[:, s, :]).then_inc(stored_parts[s], 16)

                def rows_of_parts(s):
                    sp.wait_ge(stored_parts[s], 2 * 16)
                    for n, (qp, kp) in enumerate(PARTS):
                        lo = 2 * HD * n
                        if qp == s:
                            sp.dma_start(AQ[lo:lo + HD, :, :],
                                         q_parts[qp].rearrange("(h d) n -> d h n", d=HD)).then_inc(S.qk_back, 16)
                        if kp == s:
                            sp.dma_start(BK[lo:lo + HD, :, :],
                                         k_parts[kp].rearrange("(h d) n -> d h n", d=HD)).then_inc(S.qk_back, 16)

                stored_parts = S.stored0, S.stored1, S.stored2
                store_parts(0)
                store_parts(1)
                rows_of_parts(0)
                store_parts(2)
                rows_of_parts(1)
                rows_of_parts(2)
                def shift_rows_back(n):
                    sp.wait_ge(S.shiftT_sb, n + 1)
                    sp.dma_start(shift_rows, shiftT[:]).then_inc(S.shift_stored, 16)
                    sp.wait_ge(S.shift_stored, 16 * n + 16)
                    q, qh = n // 2, n % 2
                    sp.dma_start(AQ[SCORE_ROWS:SCORE_ROWS + SHIFT_PARTS, QUAD * q:QUAD * q + QUAD, qh * HALF:(qh + 1) * HALF],
                                 shift_rows.rearrange("(s h q) n -> s h (q n)", s=SHIFT_PARTS, h=QUAD))\
                        .then_inc(S.shift_back, 16)

                for n in range(HALVES):
                    shift_rows_back(n)
                clear_turn(4 * b + 4)
            for e in range(E):
                s = e % EX_SLOTS
                if e >= EX_SLOTS:
                    sp.wait_ge(ex_down, e - EX_SLOTS + 1)
                    sp.wait_ge(ex_ids_ready, e - EX_SLOTS + 1)
                sp.dma_start(cfc[:, s], t["c_fc"][e]).then_inc(ex_loaded[s], 16)
                sp.dma_start(cproj[:, s], t["c_proj"][e].rearrange("(j p) n -> p j n", p=FFH)).then_inc(ex_loaded[s], 16)
                if e == 0:
                    sp.wait_ge(rows_out, B + 1)
                sp.dma_start(ex_in[:, s], expert_in[CAPACITY * e:CAPACITY * (e + 1), :]
                             .rearrange("(c p) d -> p c d", p=P)).then_inc(ex_loaded[s], 16)
            sp.wait_ge(all_scattered, 1)
            rows_v = expert_out.rearrange("(b t p k) d -> b p t (k d)", b=B, t=NT, k=TOPK)
            out_v = t["out"].rearrange("b (t p) d -> b p t d", p=P)
            for b in range(B):
                sp.dma_start(res[:, b], rows_v[b]).then_inc(res_loaded[b], 16)
            for b in range(B):
                sp.wait_ge(fin_out, NT * (b + 1))
                sp.dma_start(out_v[b], fin[:, b]).then_inc(stored, 16)
            sp.wait_ge(stored, 16 * B)

        @block.tensor
        def _(pe):
            def transposes(src, dst_bank, done, n=HT):
                for i in range(n):
                    last = nc.tensor.transpose(bank(dst_bank)[:, i * P:(i + 1) * P], src(i), ident[:])
                last.then_inc(done, 1)

            def half_transposes(src, ready, before=0):
                for H in range(2):
                    pe.wait_ge(ready, before + H + 1)
                    transposes(lambda i: src[:, H * HT + i, :], H, S.xT_psum)

            def tile(a, n):
                return a[:, n * P:(n + 1) * P]

            def mm(out, lhsT, rhs, first=True, last=True):
                return nc.tensor.matmul(out, lhsT, rhs, start=first, stop=last)

            def half(H):
                return slice(H * HALF, (H + 1) * HALF)

            def input_turned():
                pe.wait_ge(S.in_norm, 2)
                for H in range(2):
                    transposes(lambda i: xin_n[:, H * HT + i, :], H, S.in_T_psum)

            def step_sizes():
                pe.wait_ge(S.in_T, 2)
                for H in range(2):
                    for i in range(HT):
                        last = mm(tile(bank(2 + H), i), tile(xinT, H * HT + i), w_dt[:])
                    last.then_inc(S.dt_psum, 1)

            def decay_sums():
                pe.wait_ge(S.a_ready, 1)
                a32 = av[:].rearrange("p c h -> p (c h)")
                for i, m in enumerate((after, ones)):
                    last = mm(bank(5)[:, 32 * i:32 * i + 32], m[:], a32)
                last.then_inc(S.cum_psum, 1)

            def project_first(n):
                if n >= CONV_TILES:
                    pe.wait_ge(S.first_used, n - 1)
                mm(bank(4 + n if n < CONV_TILES else 2 + n), tile(w_in, (n + 2) % 6), xinT[:, half(0)]).then_inc(S.first_psum, 1)

            def project(n):
                if n < 2:
                    pe.wait_ge(S.first_used, CONV_TILES + n + 1)
                else:
                    pe.wait_ge(S.proj_used, n - 1)
                mm(bank(6 + n % 2), tile(w_in, (n + 2) % 6), xinT[:, half(1)])\
                    .then_inc(S.first_psum if n < 2 else S.proj_psum, 1)

            TRB, STUB, SEGB, YB, OUTB, SSB = 0, 1, 2, 4, 6, 7

            def chunk_front(c):
                if c == HT:
                    pe.wait_ge(S.xbc_ready, CONV_TILES)
                if c >= 1:
                    pe.wait_ge(S.xdt_ready, c)
                    pe.wait_ge(S.gm_ready, c)
                    pe.wait_ge(S.btok_ready, c)
                for i, f in enumerate((0, 1, 2)):
                    nc.tensor.transpose(tile(bank(TRB), i), tile(xbc[:, f], c), ident[:])
                mm(tile(bank(TRB), 3), tile(xbc[:, 2], c), tile(xbc[:, 3], c)).then_inc(S.tr_psum, 1)
                if c >= 2:
                    pe.wait_ge(S.aU_ready, c - 1)
                if c >= 1:
                    pe.wait_ge(S.l_ready, c)
                sums = aU[:, c % 2].rearrange("p h n -> p (h n)")
                mm(bank(SEGB), after[:], sums)
                mm(bank(SEGB + 1), ones[:], sums).then_inc(S.seg_psum, 1)

            def chunk_state(c):
                pe.wait_ge(S.xw_ready, c + 1)
                pe.wait_ge(S.btok_ready, c + 1)
                if c >= 1:
                    pe.wait_ge(S.h_ready, c + 1)
                mm(bank(STUB)[:, 0:D_INNER], btok[:, c % 2], xw[:, c % 2].rearrange("p h d -> p (h d)"))\
                    .then_inc(S.stu_psum, 1)

            def chunk_out(c):
                if c == HT:
                    pe.wait_ge(S.y_used, 2)
                pe.wait_ge(S.xdt_ready, c + 1)
                pe.wait_ge(S.w_ready, c + 1)
                pe.wait_ge(S.cs_ready, c + 1)
                pe.wait_ge(S.h_ready, c + 1)
                for h in range(SSM_HEADS):
                    lo = SSM_DIM * (h % 2)
                    out = bank(YB + h // 2)[lo:lo + SSM_DIM, (c % HT) * P:(c % HT + 1) * P]
                    mm(out, xdt[:, c % 2, h], Wm[:, c % 2, h], True, False)
                    last = mm(out, hst[:, c % 2, h], Cs[:, c % 2, h], False, True)
                last.then_inc(S.y_psum, 1)

            def mix_out(H):
                if H == 0:
                    pe.wait_ge(S.proj_used, 6)
                if H == 1:
                    pe.wait_ge(S.x1_ready, 1)
                pe.wait_ge(S.gated, 2 * H + 2)
                pe.wait_ge(S.sq_ready, 2 * H + 2)
                for i in range(HT):
                    n = H * HT + i
                    for j in range(2):
                        mm(tile(bank(OUTB), i), tile(zg[:, j], n), w_out[:, j], j == 0, j == 1)
                    for j in range(2):
                        last = mm(tile(bank(SSB), i), tile(y1[:, j], i), ones[:], j == 0, j == 1)
                last.then_inc(S.mix_psum, 1)

            def mlp():
                pe.wait_ge(S.h_ready, NT)
                pe.wait_ge(S.l_ready, NT)
                pe.wait_ge(S.gm_ready, NT)
                pe.wait_ge(S.btok_ready, NT)
                pe.wait_ge(S.y_used, 4)
                n = 0
                for H in range(2):
                    pe.wait_ge(S.xn3, H + 1)
                    transposes(lambda i: xn[:, H * HT + i, :], H, S.xT_psum)
                    pe.wait_ge(S.xnT_ready, H + 1)
                    for f in range(HID_TILES):
                        if n >= 2:
                            pe.wait_ge(S.hid_ready, n - 1)
                        g = 2 + 2 * (n % 2)
                        mm(bank(g), tile(w_gate, f), xnT[:, half(H)])
                        mm(bank(g + 1), tile(w_up, f), xnT[:, half(H)]).then_inc(S.mlp_psum, 1)
                        n += 1
                pe.wait_ge(S.x1_ready, 2)
                for H in range(2):
                    pe.wait_ge(S.hid_ready, HID_TILES * (H + 1))
                    for i in range(HT):
                        for f in range(HID_TILES):
                            last = mm(tile(bank(6 + H), i), tile(hidT[:, f], H * HT + i), w_down[:, f],
                                      f == 0, f == HID_TILES - 1)
                    last.then_inc(S.down_psum, 1)

            def route(w, done):
                for i in range(NT):
                    last = mm(tile(bank(2 + i // HT), i % HT), tile(xnT, i), w[:])
                last.then_inc(done, 1)

            def moe0():
                pe.wait_ge(S.xnT_ready, 2)
                half_transposes(xb, S.normed, 0)
                pe.wait_ge(S.xnT_ready, 2 + 2)
                pe.wait_ge(S.hid_ready, 2 * HID_TILES)
                route(w_route0, S.route_psum)
                pe.wait_ge(S.gsel_ready, 1)
                for n in range(NT):
                    last = nc.tensor.transpose(bank(n // HT)[0:E, (n % HT) * P:(n % HT + 1) * P], gsel[:, n, :], ident[:])
                last.then_inc(S.gT_psum, 1)
                pe.wait_ge(S.g3_ready, 3)
                for n in range(NT):
                    last = nc.tensor.transpose(bank(4)[0:3 * E, :].bitcast(BF16)[:, n * P:(n + 1) * P],
                                               g3[:, n].rearrange("p s e -> p (s e)"), ident16[:])
                last.then_inc(S.g3T_psum, 1)
                pe.wait_ge(S.skip_sum, 2)
                pe.wait_ge(S.g3T_sb, 1)

                def gate_rows(k):
                    H, e = k // E, k % E
                    if k >= 4:
                        pe.wait_ge(S.xs_ready, k - 3)
                    mm(bank(4 + k % 4), pick_rows[:, e, :], g3T[:, half(H)]).then_inc(S.gate_rows, 1)

                gate_rows(0)
                gate_rows(1)
                for k in range(2 * E):
                    H, e = k // E, k % E
                    if k == 0:
                        pe.wait_ge(S.gT_sb, 1)
                    if e == 0:
                        for i in range(HT):
                            mm(tile(bank(H), i), gT[:, (H * HT + i) * P:(H * HT + i + 1) * P], b_exp[:], i == 0, False)
                    if k + 2 < 2 * E:
                        gate_rows(k + 2)
                    pe.wait_ge(S.xs_ready, k + 1)
                    for i in range(HT):
                        last = mm(tile(bank(H), i), tile(xs[:, k % XS_SLOTS], i), w_exp[:, e, :], False,
                                  e == E - 1 and i == HT - 1)
                    last.then_inc(S.xs_used, 1)
                    if e == E - 1:
                        pe.wait_ge(S.xs_used, k + 1)
                        pe.sem_inc(S.moe_psum, 1)

            def qkv():
                half_transposes(xn, S.normed, 4)
                pe.wait_ge(S.xs_ready, 2 * E)
                for i in range(2):
                    for H in range(2):
                        if i == 0:
                            pe.wait_ge(S.xnT_ready, 4 + H + 1)
                        mm(bank(2 + 2 * i + H), tile(w_qkv, i), xnT[:, half(H)]).then_inc(S.qk_psum, 1)
                for H in range(2):
                    for i in range(HT):
                        last = mm(tile(bank(6 + H), i), tile(xnT, H * HT + i), w_qkv[:, 2 * D:3 * D])
                    last.then_inc(S.v_psum, 1)
                input_turned()
                pe.wait_ge(S.q_ready, 2)
                step_sizes()

            SB, STB, PVB, TB = 0, 4, 6, 7

            def score_matmul(pair, kh):
                n, p = pair // 16, pair % 16
                head, b0 = QUAD * (n // 2) + p // HT, SB + 2 * (p % 2)
                if kh == 0 and pair >= 2:
                    pe.wait_ge(S.s_max, pair - 1)
                q0 = (n % 2) * HALF + (p % HT) * P
                mm(bank(b0 + kh), AQ[0:SCORE_ROWS, head, q0:q0 + P], BK[0:SCORE_ROWS, head, half(kh)]).then_inc(S.s_psum, 1)

            def shift_transpose(n):
                pe.wait_ge(S.shift_cut, n + 1)
                pe.wait_ge(S.tbank_free, 1 if n == 0 else 2 * n)
                nc.tensor.transpose(bank(TB)[0:SHIFT_PARTS * 16, 0:P // 2].bitcast(BF16),
                                    shift16[:].rearrange("p s n -> p (s n)"), ident16[:])\
                    .then_inc(S.shiftT_psum, 1)

            def pv_burst(n, m):
                kt, c = m // BURST_PARTS, m % BURST_PARTS
                if m == 0 and n > 0:
                    pe.wait_ge(S.pv_evac, n)
                pe.wait_ge(S.p_ready, 32 * n + QUAD * kt + QUAD)
                for g in range(QUAD):
                    lo = VSTEP * (QUAD * (n // 2) + g)
                    cols = slice(c * BURST_COLS, (c + 1) * BURST_COLS)
                    last = mm(bank(PVB)[32 * g:32 * g + 32, cols], vall[:, kt, lo:lo + 32],
                              prob[:, QUAD * (kt % PROB_SETS) + g, cols], m == 0, m == BURSTS - 1)
                last.then_inc(S.pv_done, 1)

            def pv_transpose(n):
                pe.wait_ge(S.pv_evac, n + 1)
                pe.wait_ge(S.tbank_free, 2 * n + 3 if n < HALVES - 1 else 2 * n + 2)
                transposes(lambda i: tile(pv_sb, i), TB, S.pvT_psum)

            def attention():
                pe.wait_ge(pos_dma, POS_BACK)
                pe.wait_ge(S.qk_back, 2 * len(PARTS) * 16)
                pe.wait_ge(S.k_ready, 2)
                pe.wait_ge(S.v_ready, 2)
                pe.wait_ge(S.v_ones, 1)
                pe.wait_ge(S.dt_abs, 1)
                for pair in range(16 + LEAD):
                    for kh in range(2):
                        score_matmul(pair, kh)
                    if pair == 4:
                        decay_sums()
                    if pair == 16 + LEAD // 2:
                        shift_transpose(0)
                for unit in range(32 * HALVES):
                    n, u = unit // 32, unit % 32
                    kt, head = u // QUAD, QUAD * (n // 2) + u % QUAD
                    pair = 16 + LEAD + unit // 2
                    if pair < 16 * HALVES:
                        score_matmul(pair, unit % 2)
                    if u == 0:
                        pe.wait_ge(S.shift_back, 16 * n + 16)
                    if unit >= 2:
                        pe.wait_ge(S.p_ready, unit - 1)
                    if unit == 1:
                        pe.wait_ge(S.decay_exp, 1)
                    mm(bank(STB + unit % 2), BK[:, head, kt * P:(kt + 1) * P], AQ[:, head, half(n % 2)]).then_inc(S.st_psum, 1)
                    for m in range(BURSTS):
                        if BURST_AT[m] == u:
                            pv_burst(n, m)
                        if BURST_AT[m] == u + 32 and n > 0:
                            pv_burst(n - 1, m)
                    if u == TURN_AT and n > 0:
                        pv_transpose(n - 1)
                    if unit == 32 * (HALVES - 1) + 8:
                        pe.wait_ge(S.s_max, 16 * HALVES)
                        input_turned()
                    if unit == 32 * (HALVES - 1) + 16:
                        step_sizes()
                    if u == SHIFT_AT and n < HALVES - 1:
                        shift_transpose(n + 1)
                for m in range(BURSTS):
                    if BURST_AT[m] >= 32:
                        pv_burst(HALVES - 1, m)
                pv_transpose(HALVES - 1)

            def attention_out():
                pe.wait_ge(S.o_ready, HALVES)
                for H in range(2):
                    transposes(lambda i: o_tok[:, H * HT + i, :], H, S.oT_psum)
                for H in range(2):
                    pe.wait_ge(S.oT_sb, H + 1)
                    for i in range(HT):
                        last = mm(tile(bank(2 + H), i), tile(xnT, H * HT + i), w_proj[:])
                    last.then_inc(S.proj_out, 1)
                for n in range(CONV_TILES):
                    project_first(n)

            def moe1_route():
                half_transposes(xb, S.normed, 6)
                pe.wait_ge(S.xnT_ready, 6 + 2)
                route(w_route1, S.route1_psum)
                for n in range(CONV_TILES, CONV_TILES + 2):
                    project_first(n)
                pe.wait_ge(S.pick16_ready, 1)
                pe.wait_ge(S.first_used, 2)
                m = pick16[:].rearrange("p t e -> p (t e)")
                mm(bank(4)[:, 0:NT * E], before16[:], m)
                mm(bank(5)[:, 0:NT * E], ones16[:], m).then_inc(S.rank_psum, 1)
                project(0)
                project(1)
                pe.wait_ge(S.first_psum, CONV_TILES + 4)

            pe.wait_ge(prepared, 1)
            pe.wait_ge(consts, N_CONSTS)
            input_turned()
            step_sizes()
            for n in range(CONV_TILES):
                project_first(n)
            pe.wait_ge(S.first_used, 2)
            decay_sums()
            for n in range(CONV_TILES, CONV_TILES + 2):
                project_first(n)
            project(0)
            project(1)
            pe.wait_ge(S.first_psum, CONV_TILES + 4)
            pe.sem_inc(ended, 1)
            pe.wait_ge(go_on, 1)
            with pe.Fori(0, B) as b:
                chunk_front(0)
                for c in range(NT):
                    if c < NT - 1:
                        chunk_state(c)
                        chunk_front(c + 1)
                    for n in PROJECTIONS.get(c, ()):
                        project(n)
                    chunk_out(c)
                    if c == HT + 1:
                        mix_out(0)
                mix_out(1)
                mlp()
                moe0()
                qkv()
                attention()
                attention_out()
                moe1_route()
                pe.sem_inc(ended, 1)
                pe.wait_ge(go_on, b + 2)

            def rows_turned(e):
                pe.wait_ge(ex_loaded[e % EX_SLOTS], 48 * (e // EX_SLOTS) + 48)
                if e >= 2:
                    pe.wait_ge(ex_xT_ready, e - 1)
                for i in range(CAP_TILES):
                    last = nc.tensor.transpose(tile(bank(7 * (e % 2)), i), ex_in[:, e % EX_SLOTS, i, 0:D], ident[:])
                last.then_inc(ex_tr, 1)

            def up(e, j):
                if j == 0:
                    pe.wait_ge(ex_xT_ready, e + 1)
                if e >= 1:
                    pe.wait_ge(ex_hid_ready, 2 * e - 1 + j)
                for k in range(2):
                    last = mm(bank(1 + 2 * j + k)[0:FFH], cfc[:, e % EX_SLOTS, k * D_GATE + j * FFH:k * D_GATE + (j + 1) * FFH],
                              ex_xT[:, e % 2])
                last.then_inc(ex_up, 1)

            def down(e):
                s = e % 2
                pe.wait_ge(ex_hid_ready, 2 * e + 2)
                if e >= 2:
                    pe.wait_ge(ex_out_ready, e - 1)
                for i in range(CAP_TILES):
                    for j in range(2):
                        last = mm(tile(bank(5 + s), i), ex_hid[0:FFH, s, j, i * P:(i + 1) * P], cproj[:, e % EX_SLOTS, j],
                                  j == 0, j == 1)
                last.then_inc(ex_down, 1)

            rows_turned(0)
            up(0, 0)
            up(0, 1)
            for e in range(E):
                if e + 1 < E:
                    rows_turned(e + 1)
                    up(e + 1, 0)
                down(e)
                if e + 1 < E:
                    up(e + 1, 1)

        @block.scalar
        def _(act):
            def squares(src, sums, done, junk):
                for i in range(src.shape[1]):
                    nc.scalar.activation(junk[:, i, :], src[:, i, :], ACT.Square, scale=float(D) ** -0.5, accum_out=sums[:, i:i + 1]).then_inc(done, 1)

            def evac_T(nth, halves=(0, 1), **affine):
                for H in halves:
                    act.wait_ge(S.xT_psum, 2 * nth + H + 1)
                    func = ACT.Identity if affine else ACT.Copy
                    nc.scalar.activation(xnT[:, H * HALF:(H + 1) * HALF], bank(H), func, **affine).then_inc(S.xnT_ready, 1)

            act.wait_ge(x_loaded, 16)
            squares(xin, ss_in, a_exp, xn)
            act.wait_ge(w_loaded, loaded_all)
            nc.scalar.activation(a_neg[:], a_neg[:], ACT.Exp).then_inc(a_exp, 1)
            nc.scalar.activation(pick_rows[:].rearrange("k e n -> k (e n)"), pick_in, ACT.Copy).then_inc(a_exp, 1)
            act.wait_ge(a_exp, NT + 2)
            act.wait_ge(prepared, 1)
            act.wait_ge(consts, N_CONSTS)

            def evac_input():
                for H in range(2):
                    act.wait_ge(S.in_T_psum, H + 1)
                    nc.scalar.activation(xinT[:, H * HALF:(H + 1) * HALF], bank(H), ACT.Copy).then_inc(S.in_T, 1)

            def step_exp():
                act.wait_ge(S.dt_abs, 1)
                nc.scalar.activation(dtu[:], dts[:], ACT.Exp, scale=-1.0).then_inc(S.dt_u, 1)

            def decays():
                act.wait_ge(S.cum_psum, 1)
                nc.scalar.activation(decay[:].rearrange("p s c h -> p (s c h)"), bank(5)[:, 0:64], ACT.Exp)\
                    .then_inc(S.decay_exp, 1)

            def projected(H, n):
                lo = H * HALF
                return raw[:, n, TAPS - 1 + lo:TAPS - 1 + lo + HALF] if n < CONV_TILES else zg[:, n - CONV_TILES, lo:lo + HALF]

            def evac_first(n):
                act.wait_ge(S.first_psum, n + 1)
                nc.scalar.activation(projected(0, n), bank(4 + n if n < CONV_TILES else 2 + n),
                                     ACT.Copy if n < CONV_TILES else ACT.Silu).then_inc(S.first_used, 1)

            def evac_projection(n):
                if n >= 2:
                    act.wait_ge(S.proj_psum, n - 1)
                nc.scalar.activation(projected(1, n), bank(6 + n % 2), ACT.Copy).then_inc(S.proj_used, 1)

            def tap(H, f, done):
                nc.scalar.activation(xbc[:, f, H * HALF:(H + 1) * HALF], raw[:, f, H * HALF:(H + 1) * HALF], ACT.Identity,
                                     scale=conv_w[:, f, 0:1], bias=conv_b[:, f:f + 1]).then_inc(done, 1)

            def first_taps():
                act.wait_ge(S.headers, 1)
                for f in range(CONV_TILES):
                    act.wait_ge(S.first_used, f + 1)
                    tap(0, f, S.first_tap)

            def first_silus():
                for n in range(CONV_TILES, CONV_TILES + 2):
                    evac_first(n)
                for f in range(CONV_TILES):
                    act.wait_ge(S.first_conv, f + 1)
                    own = xbc[:, f, 0:HALF]
                    nc.scalar.activation(own, own, ACT.Silu).then_inc(S.first_silu, 1)
                act.wait_ge(S.first_used, CONV_TILES + 2)
                act.wait_ge(S.first_silu, CONV_TILES)

            def silu_xbc():
                for f in range(CONV_TILES):
                    act.wait_ge(S.conv_done, f + 1)
                    own = xbc[:, f, HALF:L]
                    nc.scalar.activation(own, own, ACT.Silu).then_inc(S.xbc_ready, 1)

            evac_input()
            step_exp()
            for n in range(CONV_TILES):
                evac_first(n)
            first_taps()
            decays()
            first_silus()
            act.sem_inc(ended, 1)
            act.wait_ge(go_on, 1)
            with act.Fori(0, B) as b:
                def input_squares(H):
                    act.wait_ge(S.x1_ready, H + 1)
                    tl = slice(H * HT, (H + 1) * HT)
                    squares(xb[:, tl], ss[:, tl], S.ss3, xn[:, tl])

                for n in range(2):
                    evac_projection(n)
                for f in range(2):
                    act.wait_ge(S.proj_used, f + 1)
                    tap(1, f, S.tap0)
                for c in range(NT):
                    act.wait_ge(S.tr_psum, c + 1)
                    act.wait_ge(S.gm_ready, c + 1)
                    if c >= 2:
                        act.wait_ge(S.stu_psum, c - 1)
                    nc.scalar.activation(btok[:, c % 2], bank(0)[:, 2 * P:3 * P], ACT.Copy).then_inc(S.btok_ready, 1)
                    act.wait_ge(S.seg_psum, c + 1)
                    if c >= 2:
                        act.wait_ge(S.w_ready, c - 1)
                        act.wait_ge(S.cs_ready, c - 1)
                    nc.scalar.activation(EL[:, c % 2].rearrange("p k h n -> p (k h n)"),
                                         ps[:, 2:4, :].rearrange("p k n -> p (k n)"), ACT.Exp).then_inc(S.l_ready, 1)
                    for n in PROJECTIONS.get(c, ()):
                        evac_projection(n)
                    for f in range(2, CONV_TILES) if c == 0 else ():
                        act.wait_ge(S.proj_used, f + 1)
                        tap(1, f, S.tap0)
                    if c == 2:
                        act.wait_ge(S.proj_used, 6)
                        silu_xbc()
                        for j in range(2):
                            nc.scalar.activation(zg[:, j, HALF:L], zg[:, j, HALF:L], ACT.Silu).then_inc(S.z_ready, 1)
                    if c == NT - 1:
                        act.wait_ge(rows_out, b + 1)
                        act.sem_inc(fence, 1)
                        input_squares(0)
                    if c in (HT + 1, NT - 1):
                        H = 0 if c == HT + 1 else 1
                        for j in range(2):
                            act.wait_ge(S.gated, 2 * H + j + 1)
                            nc.scalar.activation(y1[:, j], zg[:, j, H * HALF:(H + 1) * HALF], ACT.Square,
                                                 scale=float(D_INNER) ** -0.5).then_inc(S.sq_ready, 1)
                evac_T(0, (0,))
                for n in range(2 * HID_TILES):
                    if n == 2:
                        input_squares(1)
                    if n == HID_TILES:
                        evac_T(0, (1,))
                    act.wait_ge(S.mlp_psum, n + 1)
                    if n >= 2:
                        act.wait_ge(S.hid_ready, n - 1)
                    nc.scalar.activation(silu_g[:, n % 2], bank(2 + 2 * (n % 2)), ACT.Silu).then_inc(S.gate_silu, 1)
                evac_T(1)
                act.wait_ge(S.route_shift, 3)
                nc.scalar.activation(sc[:], lg[:], ACT.Exp).then_inc(S.route_exp, 1)
                act.wait_ge(S.gT_psum, 1)
                for H in range(2):
                    last = nc.scalar.activation(gT[:, H * HALF:(H + 1) * HALF], bank(H)[0:E], ACT.Copy)
                last.then_inc(S.gT_sb, 1)
                act.wait_ge(x_loaded, 16 * b + 32)
                act.sem_inc(fence, 1)
                squares(xin, ss_in, S.ss1, kf.rearrange("p (i n) -> p i n", n=P))
                act.wait_ge(S.ss1, NT)
                evac_T(2, scale=ln_g[:], bias=ln_b[:])
                for H in range(2):
                    act.wait_ge(S.qk_psum, H + 1)
                    nc.scalar.activation(qf[:, H * HALF:(H + 1) * HALF], bank(2 + H), ACT.Identity,
                                         scale=float(HD) ** -0.5, bias=b_q[:]).then_inc(S.q_ready, 1)
                for s in range(3):
                    act.wait_ge(*((S.q_ready, 2) if s == 0 else (S.q_rest, s)))
                    nc.scalar.activation(q3[:, s, :], qf if s == 0 else qrest, ACT.Copy).then_inc(S.q_part, 1)
                    act.wait_ge(*((S.k_ready, 2) if s == 0 else (S.k_rest, s)))
                    nc.scalar.activation(k3[:, s, :], kf if s == 0 else krest, ACT.Copy).then_inc(S.k_part, 1)

                def evac_pv(n):
                    act.wait_ge(S.pv_done, BURSTS * (n + 1))
                    if n > 0:
                        act.wait_ge(S.pvT_psum, n)
                    nc.scalar.activation(pv_sb[:], bank(6), ACT.Copy).then_inc(S.pv_evac, 1)

                evac_input()
                step_exp()
                act.wait_ge(S.k_part, 3)
                decays()
                for unit in range(32 * HALVES):
                    act.wait_ge(S.st_psum, unit + 1)
                    step = unit // QUAD
                    if unit % QUAD == 0 and step >= PROB_SETS:
                        act.wait_ge(S.pv_done, BURST_PARTS * (step + 1 - PROB_SETS))
                    nc.scalar.activation(prob[:, QUAD * (step % PROB_SETS) + unit % QUAD, :], bank(4 + unit % 2), ACT.Exp)\
                        .then_inc(S.p_ready, 1)
                    if unit % 32 == 4 and unit > 32:
                        evac_pv(unit // 32 - 1)
                evac_pv(HALVES - 1)
                for H in range(2):
                    act.wait_ge(S.oT_psum, H + 1)
                    nc.scalar.activation(xnT[:, H * HALF:(H + 1) * HALF], bank(H), ACT.Copy).then_inc(S.oT_sb, 1)
                for n in range(CONV_TILES):
                    evac_first(n)
                first_taps()
                for H in range(2):
                    act.wait_ge(S.xT_psum, 6 + H + 1)
                    act.wait_ge(S.proj_out, 2)
                    nc.scalar.activation(xnT[:, H * HALF:(H + 1) * HALF], bank(H), ACT.Copy).then_inc(S.xnT_ready, 1)
                act.wait_ge(zero_filled, 3 * 16)
                nc.scalar.activation(x3_all[:, bass.ds(NT * b, NT), :], xb[:], ACT.Copy).then_inc(S.x3_kept, 1)
                for k in range(TOPK):
                    nc.scalar.activation(xrow[:, :, k, 0:D], xb[:], ACT.Copy).then_inc(S.x3_kept, 1)
                act.wait_ge(S.route1_shift, 3)
                nc.scalar.activation(sc[:], lg[:], ACT.Exp).then_inc(S.route1_exp, 1)
                act.wait_ge(S.route1_exp, 1)
                first_silus()
                act.wait_ge(S.x3_kept, 3)
                act.wait_ge(S.xnT_ready, 6 + 2)
                act.sem_inc(ended, 1)
                act.wait_ge(go_on, b + 2)
            def evac_rows(e):
                act.wait_ge(ex_tr, e + 1)
                if e >= 2:
                    act.wait_ge(ex_up, 2 * e - 2)
                nc.scalar.activation(ex_xT[:, e % 2], bank(7 * (e % 2)), ACT.Copy).then_inc(ex_xT_ready, 1)

            evac_rows(0)
            for e in range(E):
                for j in range(2):
                    act.wait_ge(ex_up, 2 * e + j + 1)
                    if e >= 1:
                        act.wait_ge(ex_hid_ready, 2 * e - 1 + j)
                    nc.scalar.activation(ex_silu[0:FFH, j], bank(1 + 2 * j)[0:FFH], ACT.Silu).then_inc(ex_silu_ready, 1)
                    if j == 0 and e + 1 < E:
                        evac_rows(e + 1)
                act.wait_ge(ex_down, e + 1)
                if e >= 2:
                    act.wait_ge(ex_scattered[e % 2], 16 * CAP_TILES * (e // 2))
                nc.scalar.activation(ex_out[:, e % 2].rearrange("p c d -> p (c d)"), bank(5 + e % 2), ACT.Copy)\
                    .then_inc(ex_out_ready, 1)
            for b in range(B + 1):
                if b < B:
                    act.wait_ge(res_loaded[b], 16)
                    for i in range(NT):
                        second = res[:, b, i, D:2 * D]
                        nc.scalar.activation(second, second, ACT.Copy, scale=wgt_all[:, NT * (b + 1) + i, 1:2])\
                            .then_inc(fin_weighed, 1)
                if b >= 1:
                    act.wait_ge(fin_shift_ready, b)
                    for i in range(NT):
                        nc.scalar.activation(fin[:, b - 1, i, :], fin[:, b - 1, i, :], ACT.Identity,
                                             scale=fin_rstd[:, (b - 1) % 2, i:i + 1],
                                             bias=fin_shift[:, (b - 1) % 2, i:i + 1]).then_inc(fin_out, 1)

        @block.gpsimd
        def _(pool):
            g = nc.gpsimd
            pool_c = [0]

            def const(ins):
                pool_c[0] += 1
                ins.then_inc(consts, 1)

            g.memset(x3_all[:], 0.0).then_inc(zero_rows, 1)
            const(g.memset(ident[:], 0.0))
            const(g.memset(upto[:], 1.0))
            const(g.memset(after[:], 1.0))
            const(g.memset(before16[:], 1.0))
            const(g.memset(ident16[:], 0.0))
            const(g.memset(ones[:], 1.0))
            const(g.memset(ones16[:], 1.0))
            const(g.memset(neg_half[:], -0.5))
            const(g.iota(iota_i[:], pattern=[[1, E]], base=0, channel_multiplier=0))
            const(g.iota(ids[:], pattern=[[P * TOPK, NT], [1, TOPK]], base=0, channel_multiplier=TOPK))
            pool.wait_ge(consts, pool_c[0])
            sel = dict(channel_multiplier=1, pattern=[[-1, P]], base=0)
            const(g.affine_select(out=ident[:], in_=ident[:], compare_op=ALU.not_equal, fill=1.0, **sel))
            const(g.affine_select(out=ident16[:], in_=ident16[:], compare_op=ALU.not_equal, fill=1.0, **sel))
            const(g.affine_select(out=after[:], in_=after[:], compare_op=ALU.is_gt, fill=0.0, **sel))
            flip = dict(channel_multiplier=-1, pattern=[[1, P]], base=0)
            const(g.affine_select(out=upto[:], in_=upto[:], compare_op=ALU.is_ge, fill=0.0, **flip))
            const(g.affine_select(out=before16[:], in_=before16[:], compare_op=ALU.is_gt, fill=0.0, **flip))
            const(g.tensor_copy(iota_e[:], iota_i[:]))
            const(g.tensor_copy(idsf[:], ids[:]))
            pool.wait_ge(a_exp, NT)
            const(g.memset(work[:], 0.0))
            const(g.tensor_scalar(eps_sum[:], ss_in[:], RMS_EPS, None, ALU.add))
            pool.wait_ge(consts, pool_c[0])
            const(g.tensor_tensor(rstd_in[:], eps_sum[:], neg_half[:], ALU.pow))
            pool.wait_ge(consts, pool_c[0])
            const(g.memset(BK[SCORE_ROWS:SCORE_ROWS + SHIFT_PARTS, :, :], 1.0))
            assert pool_c[0] == N_CONSTS
            pool.wait_ge(prepared, 1)
            pool.wait_ge(consts, N_CONSTS)

            def inverse_root(src, eps, out, ready, need):
                pool.wait_ge(ready, need)
                inverse_root.n += 1
                n = src.shape[1]
                if inverse_root.n > 1:
                    pool.wait_ge(S.rstd_ready, inverse_root.n - 1)
                g.tensor_scalar(eps_sum[:, 0:n], src, eps, None, ALU.add).then_inc(S.eps_added, 1)
                pool.wait_ge(S.eps_added, inverse_root.n)
                g.tensor_tensor(out, eps_sum[:, 0:n], neg_half[:, 0:n], ALU.pow).then_inc(S.rstd_ready, 1)
            inverse_root.n = 0

            def own(H):
                return slice(H * HT, (H + 1) * HT)

            def rows_leave(lo, hi):
                for r in range(lo, hi):
                    i, k = r // TOPK, r % TOPK
                    g.indirect_dma_start(expert_in, bass.IndirectOffsetOnAxis(ap=slot[:, k, i:i + 1], axis=0),
                                         xrow[:, i, k, :], None, bounds_check=E * CAPACITY - 1, oob_is_err=False)\
                        .then_inc(scattered, 16)

            def decays_so_far(c, done):
                if c >= 2:
                    pool.wait_ge(S.seg_psum, c - 1)
                g.tensor_tensor(aU[:, c % 2], upto[:].unsqueeze(1).to_broadcast([P, SSM_HEADS, P]),
                                av[:, c].unsqueeze(2).to_broadcast([P, SSM_HEADS, P]), ALU.mult).then_inc(done, 1)

            def first_decays():
                pool.wait_ge(S.a_ready, 1)
                for c in range(2):
                    decays_so_far(c, S.first_aU)
                pool.wait_ge(S.first_aU, 2)

            first_decays()
            pool.sem_inc(ended, 1)
            pool.wait_ge(go_on, 1)
            with pool.Fori(0, B) as b:
                g.memset(hst[:, 0], 0.0).then_inc(S.h_ready, 1)

                for c in range(NT - 1):
                    pool.wait_ge(S.xdt_ready, c + 1)
                    if c >= 2:
                        pool.wait_ge(S.stu_psum, c - 1)
                    g.tensor_tensor(xw[:, c % 2], xdt[:, c % 2],
                                    decay[:, 0, c].unsqueeze(2).to_broadcast([P, SSM_HEADS, SSM_DIM]),
                                    ALU.mult).then_inc(S.xw_ready, 1)
                    pool.wait_ge(S.h_ready, c + 1)
                    g.tensor_tensor(hdec[:], hst[:, c % 2],
                                    decay[:, 1, c].unsqueeze(2).to_broadcast([P, SSM_HEADS, SSM_DIM]),
                                    ALU.mult).then_inc(S.hdec_ready, 1)
                    if c + 2 < NT:
                        decays_so_far(c + 2, S.aU_ready)
                    if c == ROWS_FROM:
                        pool.wait_ge(S.slot_ready, 1)
                        pool.wait_ge(zero_filled, 3 * 16)
                    if c >= ROWS_FROM:
                        rows_leave(ROWS_AT[c - ROWS_FROM], ROWS_AT[c - ROWS_FROM + 1])
                pool.wait_ge(scattered, (16 * NT * TOPK) * b + 16 * NT * TOPK)
                pool.sem_inc(rows_out, 1)
                for H in range(2):
                    inverse_root(var[:, own(H)], 1e-5, rstd[:, own(H)], S.var_ready, H + 1)
                    inverse_root(ss[:, own(H)], RMS_EPS, rstd3[:, own(H)], S.ss3, HT * (H + 1))
                g.tensor_tensor(xa[:], xin[:], xb[:], ALU.add).then_inc(S.res_sum, 1)
                for n in range(6):
                    inverse_root(mv[:, own(n % 2), 1], LN_EPS, rstd[:, own(n % 2)], S.var_ready, 3 + n)
                    if n == 1:
                        inverse_root(ss_in[:], RMS_EPS, rstd_in[:], S.ss1, NT)
                pool.wait_ge(S.normed, 6)
                g.memset(vall[:, :, 0:VSTEP * HEADS].rearrange("p t (h d) -> p t h d", h=HEADS)[:, :, :, HD:VSTEP], 1.0)\
                    .then_inc(S.v_ones, 1)
                g.tensor_tensor(xa[:], xa[:], b_proj[:].unsqueeze(1).to_broadcast([P, NT, D]), ALU.add).then_inc(S.res_bias, 1)

                first_decays()
                for H in range(2):
                    inverse_root(mv[:, own(H), 1], LN_EPS, rstd[:, own(H)], S.var_ready, 9 + H)
                pool.wait_ge(S.x3_kept, 3)
                for k in range(TOPK):
                    g.tensor_scalar(xrow[:, :, k, D:D + 1], idsf[:, :, k:k + 1], turn_base[:, 0:1], None, ALU.add)\
                        .then_inc(S.row_ids, 1)
                pool.wait_ge(S.row_ids, TOPK)
                g.tensor_scalar(turn_base[:], turn_base[:], float(L * TOPK), None, ALU.add).then_inc(base_step, 1)
                pool.wait_ge(base_step, b + 2)
                pool.wait_ge(S.rstd_ready, 13)
                pool.sem_inc(ended, 1)
                pool.wait_ge(go_on, b + 2)
            pool.wait_ge(S.slot_ready, 1)
            rows_leave(0, NT * TOPK)
            pool.wait_ge(scattered, 16 * NT * TOPK * (B + 1))
            pool.sem_inc(rows_out, 1)
            for e in range(E):
                pool.wait_ge(ex_ids_ready, e + 1)
                pool.wait_ge(ex_out_ready, e + 1)
                for i in range(CAP_TILES):
                    g.indirect_dma_start(expert_out, bass.IndirectOffsetOnAxis(ap=ex_ids[:, e % 2, i:i + 1], axis=0),
                                         ex_out[:, e % 2, i, :], None, bounds_check=TOPK * B * L - 1, oob_is_err=False)\
                        .then_inc(ex_scattered[e % 2], 16)
            for s in range(2):
                pool.wait_ge(ex_scattered[s], 16 * CAP_TILES * E // 2)
            pool.sem_inc(all_scattered, 1)
            for b in range(B):
                pool.wait_ge(fin_var_ready, b + 1)
                if b >= 2:
                    pool.wait_ge(fin_out, NT * (b - 1))
                g.tensor_tensor(fin_rstd[:, b % 2], fin_var[:, b % 2], neg_half[:], ALU.pow).then_inc(fin_rstd_ready, 1)

        @block.vector
        def _(dve):
            v = nc.vector

            def cut(src, rest, parts, sem_):
                v.tensor_copy(parts[0], src).then_inc(sem_, 1)
                k = cut.n = cut.n + 1
                dve.wait_ge(sem_, k)
                init.link(v.tensor_tensor(rest, src, parts[0], ALU.subtract))
                v.tensor_copy(parts[1], rest).then_inc(sem_, 1)
                k = cut.n = cut.n + 1
                dve.wait_ge(sem_, k)
                init.link(v.tensor_tensor(rest, rest, parts[1], ALU.subtract))
                v.tensor_copy(parts[2], rest).then_inc(sem_, 1)
                cut.n += 1
            cut.n = 0

            init = Steps(dve, prep)
            init.link(v.memset(blank[:], 0.0))
            v.memset(blank[:, D:D + 1], FAR).then_inc(zero_rows, 1)
            dve.wait_ge(pos_loaded, 4 * 16)
            cut(pos_q, rest_q, [k3[0:HD, s, :] for s in range(3)], parts_cut)
            init.link(v.tensor_scalar(pos_k, pos_tab[:, 0], rel_own[:], None, ALU.mult))
            init.link(v.scalar_tensor_tensor(pos_k, pos_tab[:, 1], rel_other[:], pos_k, ALU.mult, ALU.add))
            cut(pos_k, rest_k, [q3[:, s, :] for s in range(3)], parts_cut)
            dve.wait_ge(w_loaded, loaded_all)
            dve.wait_ge(a_exp, NT + 2)
            init.mark(v.memset(w_dt[:], 0.0))
            init.mark(v.memset(w_route0[:, E:P], 0.0))
            init.mark(v.memset(w_route1[:, E:P], 0.0))
            for of_none, value in ((fill, 0.0), (counts, 0.0), (ranks, FAR), (pick, 1.0), (idxf, 0.0), (top8, 0.0)):
                init.mark(v.memset(of_none[:], value))
            v.memset(turn_base[:], 0.0).then_inc(base_step, 1)
            init.mark(v.tensor_scalar(b_q[:], b_q[:], float(HD) ** -0.5, None, ALU.mult))
            for j in range(2):
                init.mark(v.scalar_tensor_tensor(w_out[:, j], w_out[:, j], norm_w[:, j:j + 1], mixer_row[:], ALU.mult, ALU.mult))
            init.mark(v.tensor_tensor(w_down[:], w_down[:], mlp_row[:].unsqueeze(1).to_broadcast([P, HID_TILES, D]), ALU.mult))
            init.link(v.tensor_scalar(a_neg[:], a_neg[:], -1.0, None, ALU.mult))
            init.link(v.tensor_copy(w_dt[:, 0:SSM_HEADS], w_in[:, 768:768 + SSM_HEADS]))
            dve.wait_ge(consts, N_CONSTS)
            init.wait(init.n)
            dve.wait_ge(base_step, 1)
            dve.sem_inc(prepared, 1)

            mine = Steps(dve, S.dve_step)

            def statistics(src, H):
                for i in range(H * HT, (H + 1) * HT):
                    last = mine.mark(v.bn_stats(st[:, i, :], src[:, i, :]))
                mine.wait(last)
                for i in range(H * HT, (H + 1) * HT):
                    last = mine.mark(v.bn_aggr(mv[:, i, :], st[:, i, :]))
                mine.wait(last)
                dve.sem_inc(S.var_ready, 1)

            def normalise(src, dst, H, nth):
                dve.wait_ge(S.rstd_ready, nth)
                for i in range(H * HT, (H + 1) * HT):
                    ins = v.tensor_scalar(dst[:, i, :], src[:, i, :], mv[:, i, 0:1], rstd[:, i:i + 1],
                                          ALU.subtract, ALU.mult)
                    if i % HT == HT - 1:
                        ins.then_inc(S.normed, 1)
                    else:
                        mine.mark(ins)

            def rms_apply(src, rstd_, done, H):
                tl = slice(H * HT, (H + 1) * HT)
                v.tensor_tensor(xn[:, tl, :], src[:, tl, :], per_tile(rstd_[:, tl]), ALU.mult).then_inc(done, 1)

            def routing(psum_ready, shift, exp_ready, bias):
                dve.wait_ge(psum_ready, 1)
                for H in range(2):
                    tl = slice(H * HT, (H + 1) * HT)
                    src = tiles4(2 + H)[:, :, 0:E]
                    if bias is not None:
                        v.tensor_tensor(lg[:, tl, :], src, bias[:].unsqueeze(1).to_broadcast([P, HT, E]), ALU.add).then_inc(shift, 1)
                    else:
                        v.tensor_copy(lg[:, tl, :], src).then_inc(shift, 1)
                dve.wait_ge(shift, 2)
                mine.link(v.tensor_reduce(red[:], lg[:], AX.X, ALU.max))
                v.tensor_tensor(lg[:], lg[:], red[:].unsqueeze(2).to_broadcast([P, NT, E]), ALU.subtract).then_inc(shift, 1)
                dve.wait_ge(exp_ready, 1)
                mine.link(v.tensor_reduce(red[:], sc[:], AX.X, ALU.add))
                mine.link(v.reciprocal(red[:], red[:]))
                mine.link(v.tensor_tensor(lg[:], sc[:], red[:].unsqueeze(2).to_broadcast([P, NT, E]), ALU.mult))
                for i in range(NT):
                    last = mine.mark(v.max(top8[:, i, :], lg[:, i, :]))
                mine.wait(last)
                for i in range(NT):
                    last = mine.mark(v.max_index(idx8[:, i, :], top8[:, i, :], lg[:, i, :]))
                mine.wait(last)
                mine.link(v.tensor_copy(idxf[:], idx8[:]))
                for k in range(TOPK):
                    last = mine.mark(v.tensor_tensor(pick[:, k], iota_e[:].unsqueeze(1).to_broadcast([P, NT, E]),
                                                     idxf[:, :, k:k + 1].to_broadcast([P, NT, E]), ALU.is_equal))
                mine.wait(last)

            def input_norm():
                for H in range(2):
                    tl = slice(H * HT, (H + 1) * HT)
                    v.tensor_tensor(xin_n[:, tl, :], xin[:, tl, :], per_tile(rstd_in[:, tl]), ALU.mult).then_inc(S.in_norm, 1)

            def step_sizes():
                for H in range(2):
                    dve.wait_ge(S.dt_psum, H + 1)
                    last = mine.mark(v.tensor_tensor(dtz[:, H * HT:(H + 1) * HT, :], tiles4(2 + H)[:, :, 0:SSM_HEADS],
                                                     dt_bias[:].unsqueeze(1).to_broadcast([P, HT, SSM_HEADS]), ALU.add))
                mine.wait(last)
                v.scalar_tensor_tensor(dts[:], dtz[:], -1.0, dtz[:], ALU.mult, ALU.max).then_inc(S.dt_abs, 1)
                dve.wait_ge(S.dt_u, 1)
                mine.link(v.tensor_scalar(dtp[:], dtu[:], 2.0, None, ALU.add))
                mine.link(v.reciprocal(dtp[:], dtp[:]))
                mine.link(v.tensor_tensor(dts[:], dtu[:], dtp[:], ALU.mult))
                mine.link(v.tensor_tensor(dts2[:], dts[:], dts[:], ALU.mult))
                mine.link(v.tensor_scalar(dtp[:], dts2[:], ATANH[-1], None, ALU.mult))
                for coef in reversed(ATANH[1:-1]):
                    mine.link(v.scalar_tensor_tensor(dtp[:], dtp[:], coef, dts2[:], ALU.add, ALU.mult))
                mine.link(v.scalar_tensor_tensor(dtp[:], dtp[:], ATANH[0], dts[:], ALU.add, ALU.mult))
                mine.link(v.tensor_scalar(dtp[:], dtp[:], 2.0, None, ALU.mult))
                mine.link(v.scalar_tensor_tensor(dt[:], dtz[:], 0.0, dtp[:], ALU.max, ALU.add))
                v.tensor_tensor(av[:], dt[:], a_neg[:].unsqueeze(1).to_broadcast([P, NT, SSM_HEADS]), ALU.mult)\
                    .then_inc(S.a_ready, 1)

            def headers():
                v.memset(raw[:, :, 0:TAPS - 1], 0.0).then_inc(S.headers, 1)

            def convolve(H, f):
                tapped, done = ((S.first_tap, S.first_conv), (S.tap0, S.conv_done))[H]
                dve.wait_ge(tapped, f + 1)
                lo = H * HALF
                own = xbc[:, f, lo:lo + HALF]
                for k in range(1, TAPS):
                    ins = v.scalar_tensor_tensor(own, raw[:, f, lo + k:lo + k + HALF], conv_w[:, f, k:k + 1], own,
                                                 ALU.mult, ALU.add)
                    if k < TAPS - 1:
                        mine.link(ins)
                    else:
                        ins.then_inc(done, 1)

            def places(tiles):
                mine.link(v.tensor_copy(pos[:, 0, :], fill[:]))
                for i in range(1, NT):
                    mine.link(v.tensor_tensor(pos[:, i, :], pos[:, i - 1, :], counts[:, i - 1, :], ALU.add))
                mine.mark(v.tensor_tensor(fill[:], pos[:, NT - 1, :], counts[:, NT - 1, :], ALU.add))
                mine.wait(mine.n)
                mine.link(v.tensor_tensor(pos[:], pos[:], ranks[:], ALU.add))
                for k in range(TOPK):
                    last = mine.mark(v.tensor_tensor(pw[:, k], pick[:, k], pos[:], ALU.mult))
                mine.wait(last)
                mine.link(v.tensor_reduce(posk[:], pw[:], AX.X, ALU.add))
                mine.link(v.tensor_scalar(okk[:], posk[:], float(CAPACITY), None, ALU.is_lt))
                for k in range(TOPK):
                    last = mine.mark(v.scalar_tensor_tensor(slotf[:, k], idxf[:, :, k], float(CAPACITY), posk[:, k],
                                                            ALU.mult, ALU.add))
                last = mine.mark(v.tensor_scalar(fark[:], okk[:], -FAR, FAR, ALU.mult, ALU.add))
                mine.wait(last)
                v.tensor_tensor(slot[:], slotf[:], fark[:], ALU.add).then_inc(S.slot_ready, 1)
                for k in range(TOPK):
                    last = mine.mark(v.tensor_tensor(wgt_all[:, tiles, k], okk[:, k], top8[:, :, k], ALU.mult))
                mine.wait(last)

            EARLY = 3
            mine.n = 0
            input_norm()
            step_sizes()
            headers()
            for f in range(CONV_TILES):
                convolve(0, f)
            dve.wait_ge(S.a_ready, 1)
            dve.wait_ge(S.headers, 1)
            dve.sem_inc(ended, 1)
            dve.wait_ge(go_on, 1)
            with dve.Fori(0, B) as b:
                mine.n = 0
                def gate(H):
                    dve.wait_ge(S.y_psum, HT * (H + 1))
                    hs = slice(H * HALF, (H + 1) * HALF)
                    for j in range(2):
                        if H == 1 and j == 0:
                            dve.wait_ge(S.mix_psum, 1)
                            dve.wait_ge(S.z_ready, 2)
                        v.scalar_tensor_tensor(y1[:, j], xbc[:, j, hs], d_col[:, j:j + 1], bank(4 + j), ALU.mult, ALU.add)\
                            .then_inc(S.y_used, 1)
                    for j in range(2):
                        dve.wait_ge(S.y_used, 2 * H + j + 1)
                        v.tensor_tensor(zg[:, j, hs], zg[:, j, hs], y1[:, j], ALU.mult).then_inc(S.gated, 1)

                def mix_variance(H):
                    tl = slice(H * HT, (H + 1) * HT)
                    dve.wait_ge(S.mix_psum, H + 1)
                    v.tensor_copy(var[:, tl], tiles4(7)[:, :, 0]).then_inc(S.var_ready, 1)

                def mix_norm(H):
                    dve.wait_ge(S.rstd_ready, 2 * H + 1)
                    for i in range(HT):
                        n = H * HT + i
                        ins = v.scalar_tensor_tensor(xb[:, n, :], tiles4(6)[:, i, :], rstd[:, n:n + 1], xin[:, n, :],
                                                     ALU.mult, ALU.add)
                        if i < HT - 1:
                            mine.mark(ins)
                        else:
                            ins.then_inc(S.x1_ready, 1)

                def chunk_inputs(c):
                    dve.wait_ge(S.tr_psum, c + 1)
                    if c >= 2:
                        dve.wait_ge(S.y_psum, c - 1)
                        dve.wait_ge(S.xw_ready, c - 1)
                    v.tensor_tensor(xdt[:, c % 2], bank(0)[:, 0:D_INNER].rearrange("p (h d) -> p h d", h=SSM_HEADS),
                                    dt[:, c].unsqueeze(2).to_broadcast([P, SSM_HEADS, SSM_DIM]), ALU.mult)\
                        .then_inc(S.xdt_ready, 1)
                    v.tensor_tensor(Gm[:, c % 2], bank(0)[:, 3 * P:4 * P], upto[:], ALU.mult).then_inc(S.gm_ready, 1)

                def chunk_weights(c):
                    dve.wait_ge(S.l_ready, c + 1)
                    dve.wait_ge(S.gm_ready, c + 1)
                    v.tensor_tensor(Wm[:, c % 2], EL[:, c % 2, 0], Gm[:, c % 2].unsqueeze(1).to_broadcast([P, SSM_HEADS, P]),
                                    ALU.mult).then_inc(S.w_ready, 1)
                    v.tensor_tensor(Cs[:, c % 2], xbc[:, 3, c * P:(c + 1) * P].unsqueeze(1).to_broadcast([P, SSM_HEADS, P]),
                                    EL[:, c % 2, 1], ALU.mult).then_inc(S.cs_ready, 1)

                dve.wait_ge(pos_dma, POS_STORED)
                chunk_inputs(0)
                places(bass.ds(NT * b, NT))
                chunk_weights(0)
                for c in range(NT - 1):
                    chunk_inputs(c + 1)
                    dve.wait_ge(S.hdec_ready, c + 1)
                    dve.wait_ge(S.stu_psum, c + 1)
                    v.tensor_tensor(hst[:, (c + 1) % 2].rearrange("p h d -> p (h d)"),
                                    hdec[:].rearrange("p h d -> p (h d)"), bank(1)[:, 0:D_INNER], ALU.add)\
                        .then_inc(S.h_ready, 1)
                    if c == HT:
                        gate(0)
                    for f in {0: (0, 1), 1: (2, 3)}.get(c, ()):
                        convolve(1, f)
                    if c == HT + 2:
                        mix_variance(0)
                    chunk_weights(c + 1)
                mix_norm(0)
                gate(1)
                dve.wait_ge(S.rstd_ready, 2)
                dve.wait_ge(rows_out, b + 1)
                dve.sem_inc(fence, 1)
                rms_apply(xb, rstd3, S.xn3, 0)
                mix_variance(1)
                mix_norm(1)
                for n in range(2 * HID_TILES):
                    if n == 2:
                        dve.wait_ge(S.rstd_ready, 4)
                        rms_apply(xb, rstd3, S.xn3, 1)
                    H, f = n // HID_TILES, n % HID_TILES
                    dve.wait_ge(S.gate_silu, n + 1)
                    v.tensor_tensor(hidT[:, f, H * HALF:(H + 1) * HALF], silu_g[:, n % 2], bank(3 + 2 * (n % 2)), ALU.mult)\
                        .then_inc(S.hid_ready, 1)
                dve.wait_ge(S.res_sum, 1)
                for H in range(2):
                    dve.wait_ge(S.down_psum, H + 1)
                    tl = slice(H * HT, (H + 1) * HT)
                    v.tensor_tensor(xa[:, tl, :], xa[:, tl, :], tiles4(6 + H), ALU.add).then_inc(S.skip_sum, 1)
                    dve.wait_ge(S.skip_sum, H + 1)
                    statistics(xa, H)
                for H in range(2):
                    normalise(xa, xb, H, 5 + H)
                routing(S.route_psum, S.route_shift, S.route_exp, b_route0)
                for k in range(TOPK):
                    last = mine.mark(v.tensor_tensor(pw[:, k], pick[:, k], top8[:, :, k:k + 1].to_broadcast([P, NT, E]), ALU.mult))
                mine.wait(last)
                v.tensor_tensor(gsel[:], pw[:, 0], pw[:, 1], ALU.add).then_inc(S.gsel_ready, 1)
                dve.wait_ge(S.gsel_ready, 1)
                v.tensor_copy(g3[:, :, 0], gsel[:]).then_inc(S.g3_ready, 1)
                dve.wait_ge(S.g3_ready, 1)
                mine.link(v.tensor_tensor(grest[:], gsel[:], g3[:, :, 0], ALU.subtract))
                v.tensor_copy(g3[:, :, 1], grest[:]).then_inc(S.g3_ready, 1)
                dve.wait_ge(S.g3_ready, 2)
                v.tensor_tensor(g3[:, :, 2], grest[:], g3[:, :, 1], ALU.subtract).then_inc(S.g3_ready, 1)
                dve.wait_ge(S.g3T_psum, 1)
                v.tensor_copy(g3T, bank(4)[0:3 * E, :].bitcast(BF16)).then_inc(S.g3T_sb, 1)
                for k in range(2 * E):
                    H = k // E
                    dve.wait_ge(S.gate_rows, k + 1)
                    if k >= XS_SLOTS:
                        dve.wait_ge(S.xs_used, k + 1 - XS_SLOTS)
                    v.tensor_tensor(xs[:, k % XS_SLOTS], xnT[:, H * HALF:(H + 1) * HALF], bank(4 + k % 4), ALU.mult)\
                        .then_inc(S.xs_ready, 1)
                    if k in (E + 1, 2 * E - 1):
                        H = k // (2 * E - 1)
                        tl = slice(H * HT, (H + 1) * HT)
                        dve.wait_ge(S.moe_psum, H + 1)
                        last = mine.mark(v.tensor_tensor(eacc[:, tl, :], xb[:, tl, :], tiles4(H), ALU.add))
                mine.wait(last)
                statistics(eacc, 0)
                statistics(eacc, 1)
                for H in range(2):
                    normalise(eacc, xa, H, 8 + H)
                    dve.wait_ge(S.normed, 3 + H)
                    mine.wait(mine.n)
                    statistics(xa, H)
                for H in range(2):
                    normalise(xa, xn, H, 10 + H)
                input_norm()
                for H in range(2):
                    dve.wait_ge(S.qk_psum, 2 + H + 1)
                    v.tensor_scalar(kf[:, H * HALF:(H + 1) * HALF], bank(4 + H), b_k[:], None, ALU.add).then_inc(S.k_ready, 1)
                for s in range(2):
                    dve.wait_ge(S.q_part, s + 1)
                    if s == 1:
                        dve.wait_ge(S.q_rest, 1)
                    v.tensor_tensor(qrest, qf if s == 0 else qrest, q3[:, s, :], ALU.subtract).then_inc(S.q_rest, 1)
                    dve.wait_ge(S.k_part, s + 1)
                    if s == 1:
                        dve.wait_ge(S.k_rest, 1)
                    v.tensor_tensor(krest, kf if s == 0 else krest, k3[:, s, :], ALU.subtract).then_inc(S.k_rest, 1)
                for H in range(2):
                    dve.wait_ge(S.v_psum, H + 1)
                    own = vall[:, H * HT:(H + 1) * HT, 0:VSTEP * HEADS].rearrange("p t (h d) -> p t h d", h=HEADS)[:, :, :, 0:HD]
                    v.tensor_tensor(own, tiles4(6 + H).rearrange("p t (h d) -> p t h d", h=HEADS),
                                    b_v[:].rearrange("p (h d) -> p h d", h=HEADS).unsqueeze(1)
                                    .to_broadcast([P, HT, HEADS, HD]), ALU.add).then_inc(S.v_ready, 1)
                step_sizes()

                def pair_max(pair):
                    n, p = pair // 16, pair % 16
                    dve.wait_ge(S.s_psum, 2 * pair + 2)
                    b0 = 2 * (p % 2)
                    v.tensor_reduce(smax[:, n % 2, p:p + 1], ps[:, b0:b0 + 2, :].rearrange("p k n -> p (k n)"),
                                    AX.X, ALU.max).then_inc(S.s_max, 1)

                def cut_shift(n):
                    dve.wait_ge(S.s_max, 16 * n + 16)
                    v.tensor_scalar(shift16[:, 0, :], smax[:, n % 2, :], -1.0, None, ALU.mult).then_inc(S.shift_hi, 1)
                    dve.wait_ge(S.shift_hi, n + 1)
                    v.scalar_tensor_tensor(shift16[:, 1, :], smax[:, n % 2, :], -1.0, shift16[:, 0, :],
                                           ALU.mult, ALU.subtract).then_inc(S.shift_cut, 1)

                def evac_shift(n):
                    dve.wait_ge(S.shiftT_psum, n + 1)
                    if n > 0:
                        dve.wait_ge(S.shift_stored, 16 * n)
                    v.tensor_copy(shiftT[:], bank(7)[0:SHIFT_PARTS * 16, 0:P // 2].bitcast(BF16)).then_inc(S.shiftT_sb, 1)
                    dve.wait_ge(S.shiftT_sb, n + 1)
                    dve.sem_inc(S.tbank_free, 1)

                def outputs(n):
                    dve.wait_ge(S.pvT_psum, n + 1)
                    o4 = bank(7).rearrange("p (t h d) -> p t h d", t=HT, h=QUAD)
                    v.reciprocal(o_rec[:], o4[:, :, :, HD]).then_inc(S.o_recip, 1)
                    dve.wait_ge(S.o_recip, n + 1)
                    q, qh = n // 2, n % 2
                    own = o_tok[:, qh * HT:(qh + 1) * HT, QUAD * HD * q:QUAD * HD * (q + 1)].rearrange("p t (h d) -> p t h d", h=QUAD)
                    v.tensor_tensor(own, o4[:, :, :, 0:HD], o_rec[:].unsqueeze(3).to_broadcast([P, HT, QUAD, HD]),
                                    ALU.mult).then_inc(S.o_ready, 1)
                    dve.wait_ge(S.o_ready, n + 1)
                    dve.sem_inc(S.tbank_free, 1)

                dve.wait_ge(S.v_ready, 2)
                dve.sem_inc(S.tbank_free, 1)
                for pair in range(16 + LEAD + 16 * HALVES):
                    if pair < 16 * HALVES:
                        pair_max(pair)
                        if pair % 16 == 15:
                            cut_shift(pair // 16)
                    if pair == 16 + LEAD // 2:
                        evac_shift(0)
                    if pair >= 16 + LEAD:
                        n, i = (pair - 16 - LEAD) // 16, (pair - 16 - LEAD) % 16
                        if i == OUTPUTS_AT and n > 0:
                            outputs(n - 1)
                        if i == EVAC_SHIFT_AT and n < HALVES - 1:
                            evac_shift(n + 1)
                outputs(HALVES - 1)
                headers()
                dve.wait_ge(S.res_bias, 1)
                for H in range(2):
                    dve.wait_ge(S.proj_out, H + 1)
                    tl = slice(H * HT, (H + 1) * HT)
                    mine.link(v.tensor_tensor(xa[:, tl, :], xa[:, tl, :], tiles4(2 + H), ALU.add))
                    statistics(xa, H)
                for H in range(2):
                    normalise(xa, xb, H, 12 + H)
                for f in range(EARLY):
                    convolve(0, f)
                routing(S.route1_psum, S.route1_shift, S.route1_exp, None)
                v.tensor_tensor(pick16[:], pick[:, 0], pick[:, 1], ALU.add).then_inc(S.pick16_ready, 1)
                for f in range(EARLY, CONV_TILES):
                    convolve(0, f)
                dve.wait_ge(S.rank_psum, 1)
                v.tensor_copy(ranks[:].rearrange("p t e -> p (t e)"), bank(4)[:, 0:NT * E]).then_inc(S.ranked, 1)
                v.tensor_copy(counts[:].rearrange("p t e -> p (t e)"), bank(5)[:, 0:NT * E]).then_inc(S.ranked, 1)
                dve.wait_ge(S.ranked, 2)
                dve.wait_ge(S.headers, 1)
                dve.sem_inc(ended, 1)
                dve.wait_ge(go_on, b + 2)
            mine.n = 0
            places(slice(NT * B, NT * B + NT))
            for e in range(E):
                s = e % 2
                for j in range(2):
                    dve.wait_ge(ex_silu_ready, 2 * e + j + 1)
                    if e >= 2:
                        dve.wait_ge(ex_down, e - 1)
                    v.tensor_tensor(ex_hid[0:FFH, s, j], ex_silu[0:FFH, j], bank(2 + 2 * j)[0:FFH], ALU.mult)\
                        .then_inc(ex_hid_ready, 1)
                if e >= 2:
                    dve.wait_ge(ex_scattered[s], 16 * CAP_TILES * (e // 2))
                v.tensor_copy(ex_ids[:, s, :], ex_in[:, e % EX_SLOTS, :, D]).then_inc(ex_ids_ready, 1)
            end = Steps(dve, fin_step)

            def shift(b):
                if b >= 2:
                    dve.wait_ge(fin_out, NT * (b - 1))
                dve.wait_ge(fin_rstd_ready, b + 1)
                v.scalar_tensor_tensor(fin_shift[:, b % 2], fin_mv[:, b % 2, :, 0], -1.0, fin_rstd[:, b % 2],
                                       ALU.mult, ALU.mult).then_inc(fin_shift_ready, 1)

            for b in range(B):
                s = b % 2
                dve.wait_ge(res_loaded[b], 16)
                for i in range(NT):
                    last = end.mark(v.scalar_tensor_tensor(fin[:, b, i, :], res[:, b, i, 0:D], wgt_all[:, NT * (b + 1) + i, 0:1],
                                                           x3_all[:, NT * b + i, :], ALU.mult, ALU.add))
                end.wait(last)
                dve.wait_ge(fin_weighed, NT * (b + 1))
                v.tensor_tensor(fin[:, b], fin[:, b], res[:, b, :, D:2 * D], ALU.add).then_inc(fin_summed, 1)
                if b >= 1:
                    shift(b - 1)
                dve.wait_ge(fin_summed, b + 1)
                for i in range(NT):
                    last = end.mark(v.bn_stats(st[:, i, :], fin[:, b, i, :]))
                end.wait(last)
                for i in range(NT):
                    last = end.mark(v.bn_aggr(fin_mv[:, s, i, :], st[:, i, :]))
                end.wait(last)
                v.tensor_scalar(fin_var[:, s], fin_mv[:, s, :, 1], LN_EPS, None, ALU.add).then_inc(fin_var_ready, 1)
            shift(B - 1)


_OUT = "out"


def kernel(**inputs):
    import concourse.bacc as bacc
    from concourse.bass_utils import run_bass_kernel_spmd

    x = {k: np.asarray(v) for k, v in inputs.items()}
    query, key = position_tables()
    w_rel = x["L1_attn_w_rel"]
    swapped = np.arange(HD) ^ 1
    arrays = {
        "x": np.concatenate([x["L0_attn_x"], np.zeros_like(x["L0_attn_x"][:1])]),
        "in_proj_wT": x["L0_attn_in_proj_w"].T, "conv_w": x["L0_attn_conv_w"],
        "conv_b": x["L0_attn_conv_b"].reshape(CONV_TILES, P).T.reshape(-1),
        "dt_bias": x["L0_attn_dt_bias"], "A_log": x["L0_attn_A_log"], "D": x["L0_attn_D"],
        "norm_w": x["L0_attn_norm_w"].reshape(2, P).T.reshape(-1), "out_proj_wT": x["L0_attn_out_proj_w"].T,
        "gate_wT": x["L0_attn_gate_w"].T, "up_wT": x["L0_attn_up_w"].T, "down_wT": x["L0_attn_down_w"].T,
        "mixer_scale": x["L0_attn_mixer_scale"], "mlp_scale": x["L0_attn_mlp_scale"],
        "expert_wT": x["L0_ffn_W"].transpose(2, 0, 1), "expert_b": x["L0_ffn_b"],
        "route0_wT": x["L0_ffn_Wg"].T, "route0_b": x["L0_ffn_bg"],
        "ln_g": x["L1_attn_ln_g"], "ln_b": x["L1_attn_ln_b"],
        "w_qkv": x["L1_attn_w_qkv"], "b_qkv": x["L1_attn_b_qkv"],
        "rel_own": w_rel.T.reshape(-1), "rel_other": w_rel[swapped].T.reshape(-1),
        "w_attn_out": x["L1_attn_w_out"], "b_attn_out": x["L1_attn_b_out"],
        "route1_w": x["L1_ffn_w_gate"], "c_fc": x["L1_ffn_c_fc"], "c_proj": x["L1_ffn_c_proj"],
        "pick_rows": np.repeat(np.tile(np.eye(E, dtype=np.float32), (3, 1)), P, axis=1),
        "pos_query": query, "pos_key": key,
    }
    arrays = {k: np.ascontiguousarray(a) for k, a in arrays.items()}
    nc = bacc.Bacc("TRN2", target_bir_lowering=False, num_devices=1)
    nc.disable_value_cache = True
    tensors = {k: nc.dram_tensor("in_" + k, a.shape, mybir.dt.from_np(a.dtype), kind="ExternalInput").ap()
               for k, a in arrays.items()}
    tensors[_OUT] = nc.dram_tensor(_OUT, (B, L, D), F32, kind="ExternalOutput").ap()
    build(nc, tensors)
    return run_bass_kernel_spmd(nc, [{"in_" + k: a for k, a in arrays.items()}], core_ids=[0]).results[0][_OUT]
```
